# Optimizing a Trainium2 kernel written in Bass

```python
import numpy as np
import jax
import jax.numpy as jnp

def _softmax(x, axis=-1):
    return jax.nn.softmax(x, axis=axis)

def _gelu(x):
    return jax.nn.gelu(x, approximate=True)

def _silu(x):
    return jax.nn.silu(x)

def _sigmoid(x):
    return jax.nn.sigmoid(x)

def _layernorm(x, axis=-1, eps=1e-05):
    m = jnp.mean(x, axis=axis, keepdims=True)
    v = jnp.var(x, axis=axis, keepdims=True)
    return (x - m) / jnp.sqrt(v + eps)

def _scatter_add(tgt, idx, src, axis=0):
    return tgt.at[idx].add(src)

def _segment_sum(src, seg, n):
    return jax.ops.segment_sum(src, seg, n)
kernel_name = 'mk_gps_d1_gnn_r8_4f17bc'

def setup_inputs(seed: int=0):
    np.random.seed(seed)
    _w = jnp.asarray

    def _rec_inputs():
        import jax
        import jax.numpy as jnp
        _gk = jax.random.key(seed)
        x = -0.0003019 + 1 * jax.random.normal(jax.random.fold_in(_gk, 1), (1250, 1024), jnp.float32)
        _s = jax.random.randint(jax.random.fold_in(_gk, 2), (10000,), 0, 1250, jnp.int32)
        _d = jax.random.randint(jax.random.fold_in(_gk, 3), (10000,), 0, 1250, jnp.int32)
        _loop = jnp.arange(1250, dtype=jnp.int32)
        src = jnp.concatenate([_s, _d, _loop])
        dst = jnp.concatenate([_d, _s, _loop])
        _o = jnp.argsort(dst, stable=True)
        src = src[_o]
        dst = dst[_o]
        return (x, src, dst)
    x, src, dst = _rec_inputs()

    def _L0_gnn_setup():
        import jax, jax.numpy as jnp
        import numpy as np
        N = 2500
        E = 40000
        D_IN = 1024
        D_OUT = 1024
        key = jax.random.key(seed)
        k1, k2, k3, k4 = jax.random.split(key, 4)
        x = jax.random.normal(k1, (N, D_IN), dtype=jnp.float32)
        edge_index = jax.random.randint(k2, (2, E), 0, N, dtype=jnp.int64)
        W = jax.random.normal(k3, (D_OUT, D_IN), dtype=jnp.float32) * (1.0 / np.sqrt(D_IN))
        b = jax.random.normal(k4, (D_OUT,), dtype=jnp.float32) * 0.01
        return {'x': x, 'edge_index': edge_index, 'W': W, 'b': b}
    _L0_gnn_all = _L0_gnn_setup()
    _L0_gnn_in = {k: v for k, v in _L0_gnn_all.items() if k in ('W', 'b')}
    del _L0_gnn_all

    def _L0_mix_setup():
        import jax, jax.numpy as jnp
        import numpy as np
        D = 1024
        key = jax.random.key(seed)
        ks = jax.random.split(key, 9)
        s = 1.0 / np.sqrt(D)
        x = jax.random.normal(ks[0], (8, 512, D), dtype=jnp.float32)
        Wq = jax.random.uniform(ks[1], (D, D), jnp.float32, -s, s)
        bq = jax.random.uniform(ks[2], (D,), jnp.float32, -s, s)
        Wk = jax.random.uniform(ks[3], (D, D), jnp.float32, -s, s)
        bk = jax.random.uniform(ks[4], (D,), jnp.float32, -s, s)
        Wv = jax.random.uniform(ks[5], (D, D), jnp.float32, -s, s)
        bv = jax.random.uniform(ks[6], (D,), jnp.float32, -s, s)
        Wo = jax.random.uniform(ks[7], (D, D), jnp.float32, -s, s)
        bo = jax.random.uniform(ks[8], (D,), jnp.float32, -s, s)
        return {'x': x, 'Wq': Wq, 'bq': bq, 'Wk': Wk, 'bk': bk, 'Wv': Wv, 'bv': bv, 'Wo': Wo, 'bo': bo}
    _L0_mix_all = _L0_mix_setup()
    _L0_mix_in = {k: v for k, v in _L0_mix_all.items() if k in ('Wq', 'bq', 'Wk', 'bk', 'Wv', 'bv', 'Wo', 'bo')}
    del _L0_mix_all

    def _L0_ffn_setup():
        import jax, jax.numpy as jnp
        import numpy as np
        NUM_HEADS = 16
        HEAD_DIM = 64
        ROT_DIM = 64
        NUM_EXPERTS = 8
        TOP_K = 2
        EPS = 1e-06

        def _rms_norm(x, w):
            var = jnp.mean(x * x, axis=-1, keepdims=True)
            return w * x * jax.lax.rsqrt(var + EPS)

        def _rotate_half(x):
            h = x.shape[-1] // 2
            return jnp.concatenate((-x[..., h:], x[..., :h]), axis=-1)

        def _rotary_cos_sin(seq_len, rot_dim, dtype):
            inv_freq = 1.0 / 10000.0 ** (jnp.arange(0, rot_dim, 2, dtype=jnp.float32) / rot_dim)
            t = jnp.arange(seq_len, dtype=jnp.float32)
            freqs = t[:, None] * inv_freq[None, :]
            emb = jnp.concatenate((freqs, freqs), axis=-1)
            return (jnp.cos(emb).astype(dtype), jnp.sin(emb).astype(dtype))

        def _attention(x, qkv_w, qkv_b, out_w, out_b):
            B, S, D = x.shape
            qkv = x @ qkv_w.T + qkv_b
            qkv = qkv.reshape(B, S, 3, NUM_HEADS, HEAD_DIM)
            qkv = jnp.transpose(qkv, (2, 0, 3, 1, 4))
            q, k, v = (qkv[0], qkv[1], qkv[2])
            cos, sin = _rotary_cos_sin(S, ROT_DIM, x.dtype)
            cos = cos[None, None]
            sin = sin[None, None]

            def rope(t):
                tr = t[..., :ROT_DIM]
                return jnp.concatenate((tr * cos + _rotate_half(tr) * sin, t[..., ROT_DIM:]), axis=-1)
            q, k = (rope(q), rope(k))
            scale = HEAD_DIM ** (-0.5)
            scores = jnp.einsum('bhqd,bhkd->bhqk', q, k) * scale
            attn = jax.nn.softmax(scores, axis=-1)
            out = jnp.einsum('bhqk,bhkd->bhqd', attn, v)
            out = jnp.transpose(out, (0, 2, 1, 3)).reshape(B, S, D)
            return out @ out_w.T + out_b

        def _sparse_moe(x, gate_w, w1, b1, w2, b2, w3, b3):
            logits = x @ gate_w.T
            top_vals, top_idx = jax.lax.top_k(logits, TOP_K)
            gate_scores = jax.nn.softmax(top_vals, axis=-1)
            comb = jnp.sum(jax.nn.one_hot(top_idx, NUM_EXPERTS, dtype=x.dtype) * gate_scores[..., None], axis=-2)
            out = jnp.zeros_like(x)
            for e in range(NUM_EXPERTS):
                h = jax.nn.silu(x @ w1[e].T + b1[e]) * (x @ w2[e].T + b2[e])
                y = h @ w3[e].T + b3[e]
                out = out + y * comb[..., e:e + 1]
            return out
        key = jax.random.key(seed)
        ks = jax.random.split(key, 10)
        B, S, D, H, E = (2, 256, 1024, 256, NUM_EXPERTS)
        s = lambda fan: 1.0 / np.sqrt(fan)
        return {'x': jax.random.normal(ks[0], (B, S, D), jnp.float32), 'norm1_w': jnp.ones((D,), jnp.float32), 'norm2_w': jnp.ones((D,), jnp.float32), 'qkv_w': jax.random.normal(ks[1], (3 * D, D), jnp.float32) * s(D), 'qkv_b': jnp.zeros((3 * D,), jnp.float32), 'out_w': jax.random.normal(ks[2], (D, D), jnp.float32) * s(D), 'out_b': jnp.zeros((D,), jnp.float32), 'gate_w': jax.random.normal(ks[3], (E, D), jnp.float32) * s(D), 'w1': jax.random.normal(ks[4], (E, H, D), jnp.float32) * s(D), 'b1': jnp.zeros((E, H), jnp.float32), 'w2': jax.random.normal(ks[5], (E, H, D), jnp.float32) * s(D), 'b2': jnp.zeros((E, H), jnp.float32), 'w3': jax.random.normal(ks[6], (E, D, H), jnp.float32) * s(H), 'b3': jnp.zeros((E, D), jnp.float32)}
    _L0_ffn_all = _L0_ffn_setup()
    _L0_ffn_in = {k: v for k, v in _L0_ffn_all.items() if k in ('norm1_w', 'norm2_w', 'qkv_w', 'qkv_b', 'out_w', 'out_b', 'gate_w', 'w1', 'b1', 'w2', 'b2', 'w3', 'b3')}
    del _L0_ffn_all
    return {'x': x, 'src': src, 'dst': dst, 'L0_gnn_W': _L0_gnn_in['W'], 'L0_gnn_b': _L0_gnn_in['b'], 'L0_mix_Wq': _L0_mix_in['Wq'], 'L0_mix_bq': _L0_mix_in['bq'], 'L0_mix_Wk': _L0_mix_in['Wk'], 'L0_mix_bk': _L0_mix_in['bk'], 'L0_mix_Wv': _L0_mix_in['Wv'], 'L0_mix_bv': _L0_mix_in['bv'], 'L0_mix_Wo': _L0_mix_in['Wo'], 'L0_mix_bo': _L0_mix_in['bo'], 'L0_ffn_norm1_w': _L0_ffn_in['norm1_w'], 'L0_ffn_norm2_w': _L0_ffn_in['norm2_w'], 'L0_ffn_qkv_w': _L0_ffn_in['qkv_w'], 'L0_ffn_qkv_b': _L0_ffn_in['qkv_b'], 'L0_ffn_out_w': _L0_ffn_in['out_w'], 'L0_ffn_out_b': _L0_ffn_in['out_b'], 'L0_ffn_gate_w': _L0_ffn_in['gate_w'], 'L0_ffn_w1': _L0_ffn_in['w1'], 'L0_ffn_b1': _L0_ffn_in['b1'], 'L0_ffn_w2': _L0_ffn_in['w2'], 'L0_ffn_b2': _L0_ffn_in['b2'], 'L0_ffn_w3': _L0_ffn_in['w3'], 'L0_ffn_b3': _L0_ffn_in['b3']}

def reference(x, src, dst, L0_gnn_W, L0_gnn_b, L0_mix_Wq, L0_mix_bq, L0_mix_Wk, L0_mix_bk, L0_mix_Wv, L0_mix_bv, L0_mix_Wo, L0_mix_bo, L0_ffn_norm1_w, L0_ffn_norm2_w, L0_ffn_qkv_w, L0_ffn_qkv_b, L0_ffn_out_w, L0_ffn_out_b, L0_ffn_gate_w, L0_ffn_w1, L0_ffn_b1, L0_ffn_w2, L0_ffn_b2, L0_ffn_w3, L0_ffn_b3):
    import jax
    import jax.numpy as jnp

    def _L0_gnn_ref(x, edge_index, W, b):
        import jax, jax.numpy as jnp
        import numpy as np
        N = 2500
        E = 40000
        D_IN = 1024
        D_OUT = 1024
        num_nodes = x.shape[0]
        self_idx = jnp.arange(num_nodes, dtype=edge_index.dtype)
        ei = jnp.concatenate([edge_index, jnp.stack([self_idx, self_idx], axis=0)], axis=1)
        row, col = (ei[0], ei[1])
        h = jnp.einsum('nd,od->no', x, W) + b
        deg = jnp.zeros((num_nodes,), dtype=h.dtype).at[row].add(1.0)
        deg_inv_sqrt = deg ** (-0.5)
        norm = deg_inv_sqrt[row] * deg_inv_sqrt[col]
        msg = norm[:, None] * h[col]
        out = jax.ops.segment_sum(msg, row, num_segments=num_nodes)
        return out

    def _L0_mix_ref(x, Wq, bq, Wk, bk, Wv, bv, Wo, bo):
        import jax, jax.numpy as jnp
        import numpy as np
        D = 1024
        Q = x @ Wq.T + bq
        K = x @ Wk.T + bk
        V = x @ Wv.T + bv
        Q = jax.nn.elu(Q) + 1.0
        K = jax.nn.elu(K) + 1.0
        KV = jnp.einsum('bnd,bne->bde', K, V)
        Z = jnp.einsum('bnd,bd->bn', Q, K.sum(axis=1) + 1e-06)
        context = jnp.einsum('bnd,bde->bne', Q, KV) / Z[..., None]
        return context @ Wo.T + bo

    def _L0_ffn_ref(x, norm1_w, norm2_w, qkv_w, qkv_b, out_w, out_b, gate_w, w1, b1, w2, b2, w3, b3):
        import jax, jax.numpy as jnp
        import numpy as np
        NUM_HEADS = 16
        HEAD_DIM = 64
        ROT_DIM = 64
        NUM_EXPERTS = 8
        TOP_K = 2
        EPS = 1e-06

        def _rms_norm(x, w):
            var = jnp.mean(x * x, axis=-1, keepdims=True)
            return w * x * jax.lax.rsqrt(var + EPS)

        def _rotate_half(x):
            h = x.shape[-1] // 2
            return jnp.concatenate((-x[..., h:], x[..., :h]), axis=-1)

        def _rotary_cos_sin(seq_len, rot_dim, dtype):
            inv_freq = 1.0 / 10000.0 ** (jnp.arange(0, rot_dim, 2, dtype=jnp.float32) / rot_dim)
            t = jnp.arange(seq_len, dtype=jnp.float32)
            freqs = t[:, None] * inv_freq[None, :]
            emb = jnp.concatenate((freqs, freqs), axis=-1)
            return (jnp.cos(emb).astype(dtype), jnp.sin(emb).astype(dtype))

        def _attention(x, qkv_w, qkv_b, out_w, out_b):
            B, S, D = x.shape
            qkv = x @ qkv_w.T + qkv_b
            qkv = qkv.reshape(B, S, 3, NUM_HEADS, HEAD_DIM)
            qkv = jnp.transpose(qkv, (2, 0, 3, 1, 4))
            q, k, v = (qkv[0], qkv[1], qkv[2])
            cos, sin = _rotary_cos_sin(S, ROT_DIM, x.dtype)
            cos = cos[None, None]
            sin = sin[None, None]

            def rope(t):
                tr = t[..., :ROT_DIM]
                return jnp.concatenate((tr * cos + _rotate_half(tr) * sin, t[..., ROT_DIM:]), axis=-1)
            q, k = (rope(q), rope(k))
            scale = HEAD_DIM ** (-0.5)
            scores = jnp.einsum('bhqd,bhkd->bhqk', q, k) * scale
            attn = jax.nn.softmax(scores, axis=-1)
            out = jnp.einsum('bhqk,bhkd->bhqd', attn, v)
            out = jnp.transpose(out, (0, 2, 1, 3)).reshape(B, S, D)
            return out @ out_w.T + out_b

        def _sparse_moe(x, gate_w, w1, b1, w2, b2, w3, b3):
            logits = x @ gate_w.T
            top_vals, top_idx = jax.lax.top_k(logits, TOP_K)
            gate_scores = jax.nn.softmax(top_vals, axis=-1)
            comb = jnp.sum(jax.nn.one_hot(top_idx, NUM_EXPERTS, dtype=x.dtype) * gate_scores[..., None], axis=-2)
            out = jnp.zeros_like(x)
            for e in range(NUM_EXPERTS):
                h = jax.nn.silu(x @ w1[e].T + b1[e]) * (x @ w2[e].T + b2[e])
                y = h @ w3[e].T + b3[e]
                out = out + y * comb[..., e:e + 1]
            return out
        x = x + _attention(_rms_norm(x, norm1_w), qkv_w, qkv_b, out_w, out_b)
        x = x + _sparse_moe(_rms_norm(x, norm2_w), gate_w, w1, b1, w2, b2, w3, b3)
        return x
    edge_index = jnp.stack([src, dst])
    xn = _layernorm(x, axis=-1)
    x = x + _L0_gnn_ref(xn, edge_index, L0_gnn_W, L0_gnn_b) + _L0_mix_ref(xn[None], L0_mix_Wq, L0_mix_bq, L0_mix_Wk, L0_mix_bk, L0_mix_Wv, L0_mix_bv, L0_mix_Wo, L0_mix_bo)[0]
    x = x + _L0_ffn_ref(_layernorm(x, axis=-1)[None], L0_ffn_norm1_w, L0_ffn_norm2_w, L0_ffn_qkv_w, L0_ffn_qkv_b, L0_ffn_out_w, L0_ffn_out_b, L0_ffn_gate_w, L0_ffn_w1, L0_ffn_b1, L0_ffn_w2, L0_ffn_b2, L0_ffn_w3, L0_ffn_b3)[0]
    return x

_drawn_inputs = setup_inputs


def setup_inputs(seed=0):
    import zlib

    import numpy as np

    out = dict(_drawn_inputs(seed))
    spreads = {'L0_ffn_norm1_w': (1.0, 0.2),
     'L0_ffn_norm2_w': (1.0, 0.2),
     'L0_ffn_qkv_b': (0.0, 0.1),
     'L0_ffn_out_b': (0.0, 0.1),
     'L0_ffn_b1': (0.0, 0.343),
     'L0_ffn_b2': (0.0, 0.353),
     'L0_ffn_b3': (0.0, 0.1)}
    factors = {'L0_mix_Wq': 8.0, 'L0_mix_bq': 8.0, 'L0_mix_Wk': 8.0, 'L0_mix_bk': 8.0}
    for name, (base, spread) in spreads.items():
        noise = np.random.default_rng([zlib.crc32(name.encode()), seed]).standard_normal(out[name].shape)
        drawn = base * np.exp(spread * noise) if base else spread * noise
        out[name] = jnp.asarray(drawn.astype(out[name].dtype))
    for name, factor in factors.items():
        out[name] = (out[name] * factor).astype(out[name].dtype)
    return out
```

```python
import numpy as np
import concourse.bass as bass
from concourse import mybir
from contextlib import ExitStack

F32 = mybir.dt.float32
F32R = mybir.dt.float32r
F16 = mybir.dt.float16
I32 = mybir.dt.int32
ALU = mybir.AluOpType
ACT = mybir.ActivationFunctionType
AX = mybir.AxisListType

N = 1250
D = 1024
TT, TP = 10, 125
KT = D // 128
EDGES = 21250
EC = EDGES // TP
HEADS, HD = 16, 64
EXPERTS, HID = 8, 256
CH_N = [(0, 512), (512, 512), (1024, 226)]
CH_D = [(0, 512), (512, 512)]
PAIRS = 5
LN_EPS, RMS_EPS = 1e-5, 1e-6


def build(nc, io):
    ctx = ExitStack()
    with ctx:
        sems = {}

        per_phase = {
            "mm": (("q", 8), ("k", 10), ("h", 10), ("m1", 8), ("m2", 8), ("m3", 8), ("mix", 10), ("gnn", 10), ("qk", 16),
                   ("v", 10), ("op", 10), ("gate", 1), ("ex", 32), ("w3", 10)),
            "lo": (("ln", 10), ("q", 24), ("k", 20), ("h", 20), ("m1", 16), ("m2", 16), ("m3", 16), ("qk", 48), ("v", 20),
                   ("ex", 48)),
            "val": (("q", 24), ("k", 20), ("h", 20), ("m2", 16), ("qk", 48), ("v", 20), ("ex", 48)),
            "psf": (("q", 24), ("k", 20), ("qk", 48)),
            "m": (("q", 24), ("k", 20)),
            "st0": (("q", 384), ("k", 320), ("h", 320), ("m2", 256), ("mix", 160), ("qk", 768), ("v", 320), ("att", 1280),
                    ("ex", 768), ("w3", 160)),
            "slab0": (("k", 160), ("h", 160), ("m1", 128), ("m3", 128), ("mix", 160), ("v", 160), ("op", 160), ("w3", 240)),
            "raw0": (("q", 64), ("m2", 64), ("qk", 128), ("gate", 16), ("ex", 256)),
            "raw1": (("q", 64), ("m2", 64), ("qk", 128), ("ex", 256)),
            "split": (("q", 8), ("m2", 8), ("qk", 16), ("gate", 1), ("ex", 32)),
            "rr0": (("k", 128), ("h", 128), ("m3", 128), ("v", 128), ("op", 128), ("w3", 256)),
            "res": (("k", 16), ("h", 16), ("m3", 16), ("v", 16), ("op", 16), ("w3", 32)),
            "v": (("mix", 20), ("w3", 20)),
            "in0": (("mix", 160), ("w3", 160)),
            "tr": (("ln", 10), ("gnn", 10), ("op", 10)),
            "sq": (("gnn", 10), ("op", 10)),
            "bn": (("ln", 20), ("gnn", 20)),
            "var": (("ln", 10), ("gnn", 10)),
        }
        for signal, like in (("hi", "lo"), ("e", "m"), ("st1", "st0"), ("slab1", "slab0"), ("sh", "split"), ("rr1", "rr0"),
                             ("rh", "res"), ("in1", "in0"), ("tv", "tr"), ("nb", "tr"), ("rt", "tr"), ("nh", "tr"), ("ms", "sq"),
                             ("rsd", "sq"), ("rmsr", "sq"), ("ag", "var"), ("sd", "var"), ("rc", "var")):
            per_phase[signal] = per_phase[like]

        def before(name):
            ph, _, signal = name.partition("_")
            count = 0
            for p, n in per_phase.get(signal, ()):
                if p == ph:
                    return signal, count
                count += n
            return name, 0

        def sem(name):
            name = before(name)[0]
            if name not in sems:
                sems[name] = ctx.enter_context(nc.semaphore(name))
            return sems[name]

        base = nc.sbuf_base + (-nc.sbuf_base) % 32
        A0 = base
        B0 = A0 + 80000
        L0 = B0 + 81920
        RAW0 = L0 + 20480
        W0 = RAW0 + 8192
        S0 = W0 + 16384
        C0 = S0 + 4096
        cpos = [C0]

        def at(name, shape, dt, off):
            return nc.alloc_sbuf_tensor_at(name, shape, dt, offset=off, align_bytes=16)

        def const(name, cols, dt=F32):
            t = at(name, [128, cols], dt, cpos[0])
            cpos[0] += (cols * 4 + 31) // 32 * 32
            return t

        def pair(name, cols, off):
            return at(name + "_hi", [128, cols], F32R, off), at(name + "_lo", [128, cols], F32R, off + 4 * cols)

        def scratch(name, rows, cols, dt=F32):
            return nc.dram_tensor(name, [rows, cols], dt, kind="Internal").ap()

        def scratch_pair(name, rows, cols):
            return scratch(name + "_hi", rows, cols), scratch(name + "_lo", rows, cols)

        PS = ctx.enter_context(nc.psum_tensor("products", [128, 2, 1536], F32))
        PX = ctx.enter_context(nc.psum_tensor("small_products", [128, 2, 512], F32))

        T1 = at("work1", [128, 1024], F32, W0)
        T2 = at("work2", [128, 1024], F32, W0 + 4096)
        HI = at("stage_hi", [128, 1024], F32R, W0 + 8192)
        LO = at("stage_lo", [128, 1024], F32R, W0 + 12288)
        RAW = at("raw_slab", [128, 2, 1024], F32, RAW0)
        RAWR = at("raw_resident", [128, 2, 512], F32, S0)
        L = [pair(f"slab{b}", 1280, L0 + 10240 * b) for b in range(2)]
        ident = const("ident", 128)
        bq = const("bq_col", KT)
        bv = const("bv_col", KT)
        bqk = const("bqk_col", 16)
        b1 = const("b1_col", 16)
        b2 = const("b2_col", 16)
        n1w = const("norm1_col", KT)
        n2w = const("norm2_col", KT)
        stat6 = const("stat6", 12)
        mv = const("mean_var", 2)
        rstd = const("rstd", 1)
        mean_all = const("x1_mean", TT)
        rstd_all = const("x1_rstd", TT)
        dis = const("deg_inv_sqrt", TT)
        zr = const("z_recip", 2)
        small = const("small", 8)
        ksT_hi = const("ksum_col_hi", 2 * KT, F32R)
        ksT_lo = const("ksum_col_lo", 2 * KT, F32R)
        ones2 = const("ones2", 2)
        assert cpos[0] <= 229344, cpos[0]

        xnT = pair("xnT", KT * N, A0)
        wk = pair("wk", KT * D, B0)
        wg = pair("wg", KT * D, A0)
        kres = pair("k_resident", TT * D, B0)
        m1T = pair("m1T", KT * D, A0)
        wo = pair("wo", KT * D, B0)
        m3 = pair("m3", KT * D, A0 + 0)
        ksb = at("ksum_bcast", [128, D], F32, A0 + 65536)
        counts = at("counts", [128, TT, N], F32, A0)
        hres = pair("h_resident", TT * D, B0)
        rT = pair("rT", KT * N, A0)
        wv2 = pair("wv2", KT * D, B0)
        wo2 = pair("wo2", KT * D, A0)
        zT = pair("zT", KT * N, B0)
        w3 = pair("w3", 2 * KT * D, A0)
        cosT = at("cos", [128, N], F32, B0 + 65536)
        sinT = at("sin", [128, N], F32, B0 + 65536 + 5024)
        bias_a = at("bias_rows_a", [128, D], F32, A0 + 65536 + 4096)
        bias_b = at("bias_rows_b", [128, D], F32, B0 + 65536 + 12288)

        T3 = at("work3", [128, 1024], F32, B0 + 65536 + 10048)
        ones_r = at("ones_r", [128, 128], F32R, A0 + 65536 + 8192)

        XN = scratch_pair("xn_rows", N, D)
        XNT = scratch_pair("xn_cols", D, N)
        QT = scratch_pair("q_cols", D, N)
        KR = scratch_pair("k_rows", N, D)
        HR = scratch_pair("h_rows", N, D)
        M2T = scratch_pair("m2_cols", D, D)
        ACC = scratch("acc_rows", N, D, F32)
        X1 = scratch("x1_rows", N, D, F32)
        RT = scratch_pair("r_cols", D, N)
        QK = scratch_pair("qk_cols", 2 * D, N)
        VR = scratch("v_rows", N, HEADS * 128)
        AT = scratch_pair("att_cols", D, N)
        XY = scratch("xy_rows", N, D, F32)
        CTS = scratch("comb_cols", EXPERTS, N, F32)
        G = scratch_pair("g_cols", 2 * D, N)

        V, S, P, SP, TE = nc.vector, nc.scalar, nc.gpsimd, nc.sync, nc.tensor

        def nth(name, count):
            return before(name)[1] + count

        def begun(count):
            return not isinstance(count, int) or count > 0

        def apart(eng):
            eng.sem_inc(sem("apart"), 1)

        def rounds(eng, n):
            yield 0
            with eng.Fori(1, n) as i:
                yield i

        def product(out, lhs, rhs, kts, kp, m, chunks, rw, lw=None, last=True):
            lw = lw or m
            first, ins = True, None
            for kt in range(kts):
                for l, rs in ((lhs[0], (rhs[0], rhs[1])), (lhs[1], (rhs[0],))):
                    for r in rs:
                        for off, n in chunks:
                            end = kt == kts - 1 and l is lhs[1] and last
                            ins = TE.matmul(out[0:m, off:off + n], l[0:kp, kt * lw:kt * lw + m],
                                            r[0:kp, kt * rw + off:kt * rw + off + n], start=first, stop=end)
                        first = False
            return ins

        ends = {}

        def enter(eng, ph):
            for name, value in ends[ph]:
                eng.wait_ge(sem(name), nth(name, value))

        def stage_ends(ph, n, per):
            return [(ph + "_mm", n), (ph + "_lo", n * per), (ph + "_st0", 32 * ((n * per + 1) // 2)),
                    (ph + "_st1", 32 * (n * per // 2))]

        ends["ln"] = [("ln_rt", TT), ("ln_st", 64 * TT)]
        ends["q"] = stage_ends("q", 8, 3)
        ends["k"] = stage_ends("k", 10, 2)
        ends["h"] = stage_ends("h", 10, 2)
        ends["m1"] = [("m1_mm", 8), ("m1_lo", 16)]
        ends["m2"] = stage_ends("m2", 8, 2)
        ends["m3"] = [("m3_mm", 8), ("m3_lo", 16), ("ks_col", 1)]
        ends["mix"] = [("mix_mm", 10), ("mix_v", 20), ("mix_st0", 160), ("mix_st1", 160)]
        ends["adj"] = [("adj_ev", PAIRS)]
        ends["deg"] = [("deg_scaled", 1)]
        ends["gnn"] = [("gnn_mm", 10), ("gnn_rt", 10), ("gnn_st", 16 * 30)]
        ends["qk"] = stage_ends("qk", 16, 3)
        ends["v"] = stage_ends("v", 10, 2)
        ends["att"] = [("att_pv", 80), ("att_olo", 80), ("att_st0", 32 * 40), ("att_st1", 32 * 40)]
        ends["op"] = [("op_mm", 10), ("op_rt", 10), ("op_st", 160)]
        ends["gate"] = [("gate_cb", 24), ("gate_st", 16)]
        ends["ex"] = [("ex_mm", 32), ("ex_lo", 48), ("ex_st0", 32 * 24), ("ex_st1", 32 * 24)]

        def copy_words(eng, out, in_):
            ap = [v.bitcast(F32) if v.dtype == F32R else v for v in (out, in_)]
            return eng.dma_start(ap[0], ap[1])

        def ln_store(sp, t):
            sp.wait_ge(sem("ln_lo"), nth("ln_lo", t + 1))
            for part, buf in ((0, HI), (1, LO)):
                copy_words(sp, XN[part][t * TP:(t + 1) * TP, :], buf[0:TP, :]).then_inc(sem("ln_st"), 16)
            sp.wait_ge(sem("ln_rt"), nth("ln_rt", t + 1))
            for part in (0, 1):
                copy_words(sp, XNT[part].rearrange("(k p) c -> p k c", p=128)[:, :, t * TP:(t + 1) * TP],
                             xnT[part][:, :].rearrange("p (k c) -> p k c", k=KT)[:, :, t * TP:(t + 1) * TP])\
                    .then_inc(sem("ln_st"), 16)

        def store_tile_pair(sp, dst, t, name):
            for part, buf in ((0, HI), (1, LO)):
                copy_words(sp, dst[part].rearrange("(k p) c -> p k c", p=128)[:, :, t * TP:(t + 1) * TP],
                             buf[:, 0:KT * TP].rearrange("p (k c) -> p k c", k=KT)).then_inc(sem(name), 16)

        def row_stream(sp, ph, load, rows_in, rows_out):
            def rows(s, b, c):
                if begun(2 * s + c - 1):
                    sp.wait_ge(sem(ph + "_v"), nth(ph + "_v", 2 * s + c - 1))
                copy_words(sp, T2[0:TP, 512 * c:512 * c + 512],
                             rows_in[bass.ds(s * TP, TP), 512 * c:512 * c + 512]).then_inc(sem(f"{ph}_in{c}"), 16)
                sp.wait_ge(sem(ph + "_v"), nth(ph + "_v", 2 * s + c + 1))
                copy_words(sp, rows_out[bass.ds(s * TP, TP), 512 * c:512 * c + 512],
                             T1[0:TP, 512 * c:512 * c + 512]).then_inc(sem(f"{ph}_st{c}"), 16)
            load(0, 0)
            load(1, 1)
            rows(0, 0, 0)
            rows(0, 0, 1)
            rows(1, 1, 0)
            rows(1, 1, 1)
            with sp.Fori(1, TT // 2) as i:
                for b in (0, 1):
                    if begun(2 * i + b - 1):
                        sp.wait_ge(sem(ph + "_mm"), nth(ph + "_mm", 2 * i + b - 1))
                    load(2 * i + b, b)
                for b in (0, 1):
                    for c in (0, 1):
                        rows(2 * i + b, b, c)

        EX1 = B0 + 65536
        nb = [at(f"norm{b}", [128, D], F32, EX1 + 4096 * b) for b in range(2)]
        tv = at("transposed", [128, KT * TP], F32, EX1 + 8192)
        EX2 = A0 + 50016 + (-(A0 + 50016)) % 32
        nb9 = [at(f"rnorm{b}", [128, D], F32, EX2 + 4096 * b) for b in range(2)]
        tv9 = at("rtransposed", [128, KT * TP], F32, EX2 + 8192)
        u9 = at("u_rows", [128, D], F32, EX2 + 12288)
        EX3 = A0 + 65536
        nb13 = [at("znorm", [128, D], F32, EX3)] * 2
        tv13 = at("ztransposed", [128, KT * TP], F32, EX3 + 4096)
        bias_a2 = at("bias_rows_a2", [128, D], F32, EX3 + 8192)
        AD = A0 + 50016 + (-(A0 + 50016)) % 32
        edge_src_i = at("edge_src_i", [128, EC], I32, AD)
        edge_dst_i = at("edge_dst_i", [128, EC], I32, AD + 704)
        edge_src = at("edge_src", [128, EC], F32, AD + 1408)
        edge_dst = at("edge_dst", [128, EC], F32, AD + 2112)
        iota = at("iota", [128, N], F16, AD + 2816)
        oh_src = at("onehot_src", [128, 2, N], F16, AD + 2816 + 2528)
        oh_dst = at("onehot_dst", [128, 2, 2 * 128], F16, AD + 2816 + 2528 + 5024)
        q_st = [at(f"q_stack{b}", [128, N], F32R, A0 + 5024 * b) for b in range(2)]
        k_st = [[at(f"k_stack{b}{p}", [128, N], F32R, A0 + 5024 * (2 + 2 * b + p)) for p in range(2)] for b in range(2)]
        v_st = [at(f"v_stack{b}", [128, TT * 128], F32R, A0 + 5024 * 6 + 5120 * b) for b in range(2)]
        A1 = A0 + 5024 * 6 + 10240
        prob = [at(f"prob{b}", [128, N], F32, A1 + 5024 * b) for b in range(2)]
        B1 = B0
        pT = [pair(f"pT{b}", TT * 250, B1 + 20000 * b) for b in range(2)]
        AC = B1 + 40000
        o_tmp = at("o_tmp", [128, 512], F32, AC)
        o_sum = at("o_sum", [128, 512], F32, AC + 2048)
        o_hi = at("o_hi", [128, 512], F32R, AC + 4096)
        o_lo = at("o_lo", [128, 512], F32R, AC + 6144)
        mx = at("att_max", [128, 2], F32, AC + 8192)
        nmx = at("att_negmax", [128, 2], F32, AC + 8224)
        rs = at("att_sum", [128, 2], F32, AC + 8256)
        rr = at("att_rsum", [128, 2], F32, AC + 8288)
        combB = at("comb_bcast", [128, EXPERTS, N], F32, A0)
        combT = at("combT", [128, N], F32, A0 + 40032)
        logT = at("logitsT", [128, N], F32, A0 + 45056)
        lg = at("logits", [128, 8], F32, A0 + 50112)
        m8 = at("top8", [128, 8], F32, A0 + 50144)
        top_i = at("top_index", [128, 8], mybir.dt.uint32, A0 + 50176)
        top_f = at("top_index_f", [128, 8], F32, A0 + 50208)
        eight = at("expert_number", [128, 8], F32, A0 + 54608)
        mask = at("mask", [128, 8], F32, A0 + 50240)
        ex8 = at("exp8", [128, 8], F32, A0 + 50272)
        nm1 = at("neg_top", [128, 8], F32, A0 + 50304)
        sel = at("select", [128, EXPERTS * 128], F32, A0 + 50336)
        comb = at("comb", [128, 8], F32, A0 + 50336 + 4096)
        LG = [pair(f"gslab{b}", 16 * TP, A0 + 131072 + 16000 * b) for b in range(2)]
        ct_tile = [at(f"ct_tile{b}", [128, 128], F32, A0 + 131072 + 32000 + 512 * b) for b in range(2)]
        b3r = at("b3_rows", [128, D], F32, A0 + 131072 + 33024)
        assert A0 + 131072 + 33024 + 4096 <= RAW0

        block = ctx.enter_context(nc.Block())

        @block.sync
        def _(sp):
            def load_slab_raw(ph, src, s, b, idx):
                copy_words(sp, RAW[:, b, :], src[s].rearrange("p k m -> p (k m)")).then_inc(sem(f"{ph}_raw{b}"), 16)

            def load_slab(ph, src, s, b, kts, kp, m, rows_are_k):
                for part in (0, 1):
                    v = src[part].rearrange("(k p) c -> p k c", p=kp)[:, :, bass.ds(s * m, m)]
                    copy_words(sp, L[b][part][0:kp, 0:kts * m].rearrange("p (k c) -> p k c", k=kts), v)\
                        .then_inc(sem(f"{ph}_slab{b}"), 16)

            def stream(ph, n, load, store, chunks, used="_mm"):
                load(0, 0)
                load(1, 1)
                per = len(chunks)

                def store_slab(s, b):
                    for c in range(per):
                        q = per * b + c
                        sp.wait_ge(sem(ph + "_lo"), nth(ph + "_lo", s * per + c + 1))
                        store(s, c, q % 2)

                with sp.Fori(0, n // 2 - 1) as i:
                    for b in (0, 1):
                        sp.wait_ge(sem(ph + used), nth(ph + used, 2 * i + b + 1))
                        load(2 * i + b + 2, b)
                        if store:
                            store_slab(2 * i + b, b)
                if store:
                    for b in (0, 1):
                        store_slab(n - 2 + b, b)

            def store_pair(ph, dst, rows, chunks, p):
                def go(s, c, h):
                    off, n = chunks[c]
                    for part, buf in ((0, HI), (1, LO)):
                        copy_words(sp, dst[part][bass.ds(s * rows, rows), off:off + n],
                                     buf[0:rows, 512 * h:512 * h + n]).then_inc(sem(f"{ph}_st{h}"), 16)
                return go

            for t, k in ((bq, "bq"), (bv, "bv"), (bqk, "bqk"), (b1, "b1"), (b2, "b2"), (n1w, "n1"), (n2w, "n2"),
                         (ident, "ident")):
                copy_words(sp, t[:, :], io[k]).then_inc(sem("consts"), 16)
            for t in range(TT):
                b = t % 2
                if t >= 2:
                    if begun(t - 1):
                        sp.wait_ge(sem("ln_nb"), nth("ln_nb", t - 1))
                copy_words(sp, [T1, T2][b][0:TP, :], io["x"][t * TP:(t + 1) * TP, :]).then_inc(sem(f"ln_x{b}"), 16)
                if t >= 1:
                    ln_store(sp, t - 1)
            ln_store(sp, TT - 1)
            enter(sp, "ln")
            copy_words(sp, bias_b[0:TP, :], io["bk"].partition_broadcast(TP)).then_inc(sem("k_bias"), 16)
            stream("q", 8, lambda s, b: load_slab_raw("q", io["Wq"], s, b, 0),
                   store_pair("q", QT, 128, CH_N, 128), CH_N, "_split")
            enter(sp, "q")
            copy_words(sp, bias_a[0:TP, :], io["bg"].partition_broadcast(TP)).then_inc(sem("g_bias"), 16)
            stream("k", 10, lambda s, b: load_slab("k", XNT, s, b, KT, 128, TP, 0),
                   store_pair("k", KR, TP, CH_D, TP), CH_D)
            enter(sp, "k")
            for part in (0, 1):
                copy_words(sp, kres[part][0:TP, :].rearrange("p (k c) -> p k c", k=TT),
                             KR[part].rearrange("(k p) c -> p k c", p=TP)).then_inc(sem("m1_full"), 16)
            stream("h", 10, lambda s, b: load_slab("h", XNT, s, b, KT, 128, TP, 0),
                   store_pair("h", HR, TP, CH_D, TP), CH_D)
            enter(sp, "h")
            stream("m1", 8, lambda s, b: load_slab("m1", XN, s, b, TT, TP, 128, 0), None, CH_D)
            enter(sp, "m1")
            stream("m2", 8, lambda s, b: load_slab_raw("m2", io["Wv"], s, b, 0),
                   store_pair("m2", M2T, 128, CH_D, 128), CH_D, "_split")
            enter(sp, "m2")
            stream("m3", 8, lambda s, b: load_slab("m3", M2T, s, b, KT, 128, 128, 0), None, CH_D)
            enter(sp, "m3")
            copy_words(sp, bias_a[0:TP, :], io["bo"].partition_broadcast(TP)).then_inc(sem("o_bias"), 16)
            for part in (0, 1):
                copy_words(sp, hres[part][0:TP, :].rearrange("p (k c) -> p k c", k=TT),
                             HR[part].rearrange("(k p) c -> p k c", p=TP)).then_inc(sem("gnn_full"), 16)
            row_stream(sp, "mix", lambda s, b: load_slab("mix", QT, s, b, KT, 128, TP, 0), io["x"], ACC)
            enter(sp, "mix")
            for k, t in (("src", edge_src_i), ("dst", edge_dst_i)):
                copy_words(sp, t[0:TP, :], io[k].rearrange("(p c) -> p c", p=TP)).then_inc(sem("edges"), 16)
            enter(sp, "deg")
            for t in range(TT):
                b = t % 2
                if t >= 1:
                    if begun(t):
                        sp.wait_ge(sem("gnn_x1"), nth("gnn_x1", t))
                copy_words(sp, T2[0:TP, :], ACC[t * TP:(t + 1) * TP, :]).then_inc(sem("gnn_acc"), 16)
                sp.wait_ge(sem("gnn_x1"), nth("gnn_x1", t + 1))
                copy_words(sp, X1[t * TP:(t + 1) * TP, :], T1[0:TP, :]).then_inc(sem("gnn_st"), 16)
                sp.wait_ge(sem("gnn_rt"), nth("gnn_rt", t + 1))
                store_tile_pair(sp, RT, t, "gnn_st")
            enter(sp, "gnn")
            for t, k in ((cosT, "cos"), (sinT, "sin")):
                copy_words(sp, t[:, :], io[k]).then_inc(sem("rope_tables"), 16)
            for part in (0, 1):
                copy_words(sp, rT[part][:, :].rearrange("p (k c) -> p k c", k=KT),
                             RT[part].rearrange("(k p) c -> p k c", p=128)).then_inc(sem("qk_full"), 16)
            stream("qk", 16, lambda s, b: load_slab_raw("qk", io["Wqk"], s, b, 0),
                   store_pair("qk", QK, 128, CH_N, 128), CH_N, "_split")
            enter(sp, "qk")
            copy_words(sp, bias_a[0:TP, :], io["bv2"].partition_broadcast(TP)).then_inc(sem("v2_bias"), 16)

            def store_v(s, c, h):
                for part, buf in ((0, HI), (1, LO)):
                    dst = VR.rearrange("t (h e d) -> t h e d", h=HEADS, e=2)[bass.ds(s * TP, TP), 8 * c:8 * c + 8, part, :]
                    copy_words(sp, dst, buf[0:TP, 512 * h:512 * h + 512].rearrange("t (h d) -> t h d", h=8))\
                        .then_inc(sem(f"v_st{h}"), 16)
            stream("v", 10, lambda s, b: load_slab("v", RT, s, b, KT, 128, TP, 0), store_v, CH_D)
            enter(sp, "v")

            def load_head(h, b):
                for part in (0, 1):
                    half = slice(64 * part, 64 * part + 64)
                    copy_words(sp, q_st[b][half, :], QK[part][bass.ds(h * HD, HD), :]).then_inc(sem(f"head{b}"), 16)
                    for dup in (0, 1):
                        copy_words(sp, k_st[b][part][64 * dup:64 * dup + 64, :],
                                     QK[part][bass.ds(h * HD + D, HD), :]).then_inc(sem(f"head{b}"), 16)
                copy_words(sp, v_st[b][0:TP, :].rearrange("p (k c) -> p k c", k=TT),
                             VR.rearrange("(k p) c -> p k c", p=TP)[:, :, bass.ds(h * 128, 128)])\
                    .then_inc(sem(f"head{b}"), 16)

            def store_out(h, hb, g):
                pb = (hb * 5 + g) % 2
                sp.wait_ge(sem("att_olo"), nth("att_olo", h * 5 + g + 1))
                for part, buf in ((0, o_hi), (1, o_lo)):
                    copy_words(sp, AT[part][bass.ds(h * HD, HD), 250 * g:250 * g + 250],
                                 buf[0:64, 250 * pb:250 * pb + 250]).then_inc(sem(f"att_st{pb}"), 16)
            load_head(0, 0)
            load_head(1, 1)
            with sp.Fori(0, HEADS // 2 - 1) as i:
                for b in (0, 1):
                    for g in range(5):
                        store_out(2 * i + b, b, g)
                    sp.wait_ge(sem("att_pv"), nth("att_pv", (2 * i + b + 1) * 5))
                    load_head(2 * i + b + 2, b)
            for b in (0, 1):
                for g in range(5):
                    store_out(HEADS - 2 + b, b, g)
            enter(sp, "att")
            copy_words(sp, bias_a2[0:TP, :], io["ob"].partition_broadcast(TP)).then_inc(sem("ob_bias"), 16)
            load_slab("op", AT, 0, 0, KT, 128, TP, 0)
            for t in range(TT):
                if t + 1 < TT:
                    if t >= 1:
                        if begun(t):
                            sp.wait_ge(sem("op_mm"), nth("op_mm", t))
                    load_slab("op", AT, t + 1, (t + 1) % 2, KT, 128, TP, 0)
                if t >= 1:
                    if begun(t):
                        sp.wait_ge(sem("op_xy"), nth("op_xy", t))
                copy_words(sp, T2[0:TP, :], X1[t * TP:(t + 1) * TP, :]).then_inc(sem("op_x1"), 16)
                sp.wait_ge(sem("op_xy"), nth("op_xy", t + 1))
                copy_words(sp, XY[t * TP:(t + 1) * TP, :], T2[0:TP, :]).then_inc(sem("op_st"), 16)
                sp.wait_ge(sem("op_st"), nth("op_st", 16 * (t + 1)))
            enter(sp, "op")
            copy_words(sp, RAW[:, 0, :], io["gate"].rearrange("p k m -> p (k m)")).then_inc(sem("gate_raw0"), 16)
            copy_words(sp, sel[0:EXPERTS, :], io["sel"]).then_inc(sem("gate_sel"), 16)
            sp.wait_ge(sem("gate_ct"), nth("gate_ct", TT))
            copy_words(sp, CTS, combT[0:EXPERTS, :]).then_inc(sem("gate_st"), 16)
            enter(sp, "gate")

            def store_g(r, c, h):
                off, n = CH_N[c]
                for part, buf in ((0, HI), (1, LO)):
                    copy_words(sp, G[part][bass.ds(r * 128, 128), off:off + n],
                                 buf[:, 512 * h:512 * h + n]).then_inc(sem(f"ex_st{h}"), 16)

            def store_expert(e):
                for j in range(2):
                    for c in range(3):
                        sp.wait_ge(sem("ex_lo"), nth("ex_lo", e * 6 + 3 * j + c + 1))
                        store_g(2 * e + j, c, (3 * j + c) % 2)
            load_slab_raw("ex", io["W12"], 0, 0, 0)
            load_slab_raw("ex", io["W12"], 1, 1, 0)
            with sp.Fori(0, EXPERTS - 1) as e:
                for j in range(2):
                    for b in (0, 1):
                        sp.wait_ge(sem("ex_split"), nth("ex_split", e * 4 + 2 * j + b + 1))
                        load_slab_raw("ex", io["W12"], e * 4 + 2 * j + b + 2, b, 0)
                    for c in range(3):
                        sp.wait_ge(sem("ex_lo"), nth("ex_lo", e * 6 + 3 * j + c + 1))
                        store_g(2 * e + j, c, (3 * j + c) % 2)
            for b in (0, 1):
                sp.wait_ge(sem("ex_split"), nth("ex_split", 4 * EXPERTS - 4 + b + 1))
                load_slab_raw("ex", io["W12"], 4 * EXPERTS - 4 + b + 2, b, 0)
            store_expert(EXPERTS - 1)
            enter(sp, "ex")

            def load_g(s, b):
                for part in (0, 1):
                    copy_words(sp, LG[b][part][:, :].rearrange("p (k c) -> p k c", k=16),
                                 G[part].rearrange("(k p) c -> p k c", p=128)[:, :, bass.ds(s * TP, TP)])\
                        .then_inc(sem(f"w3_slab{b}"), 16)
                copy_words(sp, ct_tile[b][0:EXPERTS, 0:TP], CTS[:, bass.ds(s * TP, TP)]).then_inc(sem(f"w3_slab{b}"), 16)
            row_stream(sp, "w3", load_g, XY, io["out"])
            sp.wait_ge(sem("w3_st0"), nth("w3_st0", 160))
            sp.wait_ge(sem("w3_st1"), nth("w3_st1", 160))

        @block.gpsimd
        def _(pool):
            def split_resident(ph, src, dst, pieces, first=0):
                def fetch(j, b):
                    pool.dma_start(RAWR[:, b, :], src[j // 2 * 128:(j // 2 + 1) * 128, 512 * (j % 2):512 * (j % 2) + 512])\
                        .then_inc(sem(f"{ph}_rr{b}"), 16)
                n = 2 * pieces
                fetch(0, 0)
                fetch(1, 1)
                for j in range(n):
                    b = j % 2
                    pool.wait_ge(sem(f"{ph}_rr{b}"), nth(f"{ph}_rr{b}", 16 * (j // 2 + 1)))
                    P.tensor_copy(dst[0][:, 512 * j:512 * j + 512], RAWR[:, b, :]).then_inc(sem(ph + "_rh"), 1)
                    pool.wait_ge(sem(ph + "_rh"), nth(ph + "_rh", j + 1))
                    P.tensor_tensor(dst[1][:, 512 * j:512 * j + 512], RAWR[:, b, :],
                                    dst[0][:, 512 * j:512 * j + 512].bitcast(F32), ALU.subtract)\
                        .then_inc(sem(ph + "_res"), 1)
                    if j + 2 < n:
                        pool.wait_ge(sem(ph + "_res"), nth(ph + "_res", j + 1))
                        fetch(j + 2, b)

            def split_slabs(ph, n):
                for r in rounds(pool, n // 2):
                    for b in (0, 1):
                        pool.wait_ge(sem(f"{ph}_raw{b}"), nth(f"{ph}_raw{b}", 16 * r + 16))
                        if begun(2 * r + b - 1):
                            pool.wait_ge(sem(ph + "_mm"), nth(ph + "_mm", 2 * r + b - 1))
                        apart(pool)
                        P.tensor_copy(L[b][0][:, 0:1024], RAW[:, b, :]).then_inc(sem(ph + "_sh"), 1)
                        pool.wait_ge(sem(ph + "_sh"), nth(ph + "_sh", 2 * r + b + 1))
                        P.tensor_tensor(L[b][1][:, 0:1024], RAW[:, b, :], L[b][0][:, 0:1024].bitcast(F32),
                                        ALU.subtract).then_inc(sem(ph + "_split"), 1)

            split_resident("k", io["Wk"], wk, 8)
            enter(pool, "ln")
            split_slabs("q", 8)
            enter(pool, "q")
            split_resident("h", io["Wg"], wg, 8)
            enter(pool, "m1")
            split_slabs("m2", 8)
            split_resident("m3", io["Wo"], wo, 8)
            enter(pool, "mix")
            P.iota(iota[:, :], [[1, N]], base=0, channel_multiplier=0, allow_small_or_imprecise_dtypes=True)\
                .then_inc(sem("iota"), 1)
            enter(pool, "gnn")
            split_slabs("qk", 16)
            enter(pool, "qk")
            split_resident("v", io["Wv2"], wv2, 8)
            enter(pool, "v")
            for r in rounds(pool, HEADS // 2):
                for j in range(2 * TT):
                    b = j % 2
                    t = r * (2 * TT) + j
                    pool.wait_ge(sem("att_rr"), nth("att_rr", t + 1))
                    apart(pool)
                    P.tensor_scalar(prob[b][0:TP, :], prob[b][0:TP, :], rr[0:TP, b:b + 1], 1.0, ALU.mult, ALU.mult)\
                        .then_inc(sem("att_norm"), 1)
            enter(pool, "att")
            split_resident("op", io["Wo2"], wo2, 8)
            enter(pool, "op")
            P.iota(eight[:, :], [[1, 8]], base=0, channel_multiplier=0, allow_small_or_imprecise_dtypes=True)\
                .then_inc(sem("gate_iota"), 1)
            pool.wait_ge(sem("gate_raw0"), nth("gate_raw0", 16))
            P.tensor_copy(L[0][0][:, 0:1024], RAW[:, 0, :]).then_inc(sem("gate_sh"), 1)
            pool.wait_ge(sem("gate_sh"), nth("gate_sh", 1))
            P.tensor_tensor(L[0][1][:, 0:1024], RAW[:, 0, :], L[0][0][:, 0:1024].bitcast(F32),
                            ALU.subtract).then_inc(sem("gate_split"), 1)
            enter(pool, "gate")
            for r in rounds(pool, EXPERTS):
                for j in range(2):
                    for b in (0, 1):
                        pool.wait_ge(sem(f"ex_raw{b}"), nth(f"ex_raw{b}", 32 * r + 16 * j + 16))
                        if begun(4 * r + 2 * j + b - 1):
                            pool.wait_ge(sem("ex_mm"), nth("ex_mm", 4 * r + 2 * j + b - 1))
                        apart(pool)
                        P.tensor_copy(L[b][0][:, 0:1024], RAW[:, b, :]).then_inc(sem("ex_sh"), 1)
                        pool.wait_ge(sem("ex_sh"), nth("ex_sh", 4 * r + 2 * j + b + 1))
                        P.tensor_tensor(L[b][1][:, 0:1024], RAW[:, b, :], L[b][0][:, 0:1024].bitcast(F32),
                                        ALU.subtract).then_inc(sem("ex_split"), 1)
            enter(pool, "ex")
            pool.dma_start(b3r[0:EXPERTS, :], io["b3"]).then_inc(sem("b3_in"), 16)
            split_resident("w3", io["W3"], w3, 16)

        @block.tensor
        def _(pe):
            def slabs(ph, n, slab_unit, kts, kp, m, rhs, rw, chunks, per_ev, ev, split):
                for r in rounds(pe, n // 2):
                    for b in (0, 1):
                        if split:
                            pe.wait_ge(sem(ph + "_split"), nth(ph + "_split", 2 * r + b + 1))
                        else:
                            pe.wait_ge(sem(f"{ph}_slab{b}"), nth(f"{ph}_slab{b}", slab_unit * r + slab_unit))
                        if begun(per_ev * (2 * r + b - 1)):
                            pe.wait_ge(sem(ph + ev), nth(ph + ev, per_ev * (2 * r + b - 1)))
                        ins = product(PS[:, b, :], L[b], rhs, kts, kp, m, chunks, rw)
                        ins.then_inc(sem(ph + "_mm"), 1)

            pe.wait_ge(sem("consts"), nth("consts", 16 * 8))

            def transposes(ph, src, t):
                pe.wait_ge(sem(ph + "_nb"), nth(ph + "_nb", t + 1))
                if begun(t):
                    pe.wait_ge(sem(ph + "_tv"), nth(ph + "_tv", t))
                for f in range(KT):
                    ins = TE.transpose(PX[:, f // 4, (f % 4) * TP:(f % 4) * TP + TP],
                                       src[0:TP, f * 128:f * 128 + 128], ident[0:TP, 0:TP])
                ins.then_inc(sem(ph + "_tr"), 1)
            for t in range(TT):
                transposes("ln", nb[t % 2], t)
            enter(pe, "ln")
            slabs("q", 8, 0, KT, 128, 128, xnT, N, CH_N, 3, "_psf", True)
            enter(pe, "q")
            pe.wait_ge(sem("k_res"), nth("k_res", 16))
            slabs("k", 10, 32, KT, 128, TP, wk, D, CH_D, 2, "_psf", False)
            enter(pe, "k")
            pe.wait_ge(sem("h_res"), nth("h_res", 16))
            slabs("h", 10, 32, KT, 128, TP, wg, D, CH_D, 2, "_val", False)
            enter(pe, "h")
            pe.wait_ge(sem("m1_full"), nth("m1_full", 32))
            pe.wait_ge(sem("ones_ready"), nth("ones_ready", 1))
            for off, n in CH_D:
                for kt in range(TT):
                    for part in (0, 1):
                        ins = TE.matmul(PS[:, 0, off:off + n], ones_r[0:TP, :], kres[part][0:TP, kt * D + off:kt * D + off + n],
                                        start=kt == 0 and part == 0, stop=kt == TT - 1 and part == 1)
            ins.then_inc(sem("ks_mm"), 1)
            pe.wait_ge(sem("ks_v"), nth("ks_v", 1))
            slabs("m1", 8, 32, TT, TP, 128, kres, D, CH_D, 2, "_lo", False)
            enter(pe, "m1")
            slabs("m2", 8, 0, KT, 128, 128, m1T, D, CH_D, 2, "_val", True)
            enter(pe, "m2")
            for f in range(KT):
                ins = TE.transpose(PX[:, f // 4, (f % 4) * 128:(f % 4) * 128 + 128], ksb[:, f * 128:f * 128 + 128],
                                   ident[:, :])
            ins.then_inc(sem("ks_tr"), 1)
            pe.wait_ge(sem("m3_res"), nth("m3_res", 16))
            slabs("m3", 8, 32, KT, 128, 128, wo, D, CH_D, 2, "_lo", False)
            enter(pe, "m3")
            for r in rounds(pe, TT // 2):
                for b in (0, 1):
                    pe.wait_ge(sem(f"mix_slab{b}"), nth(f"mix_slab{b}", 32 * r + 32))
                    if begun(2 * (2 * r + b - 1)):
                        pe.wait_ge(sem("mix_v"), nth("mix_v", 2 * (2 * r + b - 1)))
                    for kt in range(KT):
                        for n3, (l, rk) in enumerate(((0, ksT_hi), (0, ksT_lo), (1, ksT_hi))):
                            TE.matmul(PS[0:TP, b, 1024:1026], L[b][l][:, kt * TP:kt * TP + TP], rk[:, 2 * kt:2 * kt + 2],
                                      start=kt == 0 and n3 == 0, stop=kt == KT - 1 and n3 == 2)
                    product(PS[:, b, :], L[b], m3, KT, 128, TP, CH_D, D).then_inc(sem("mix_mm"), 1)
            enter(pe, "mix")
            for g in range(PAIRS):
                if g:
                    if begun(g):
                        pe.wait_ge(sem("adj_ev"), nth("adj_ev", g))


                def edge_column(c, b, start, stop, ready):
                    pe.wait_ge(sem("oh_ready"), nth("oh_ready", ready))
                    for h in range(2):
                        for off, n in CH_N:
                            ins = TE.matmul(PS[0:TP, h, off:off + n], oh_dst[0:TP, b, h * 128:h * 128 + TP],
                                            oh_src[0:TP, b, off:off + n], start=start, stop=stop)
                    ins.then_inc(sem("oh_used"), 1)
                edge_column(0, 0, True, False, g * EC + 1)
                edge_column(1, 1, False, False, g * EC + 2)
                with pe.Fori(1, EC // 2 - 1) as i:
                    for b in (0, 1):
                        edge_column(None, b, False, False, 2 * i + (g * EC + b + 1))
                edge_column(0, 0, False, False, g * EC + EC - 1)
                edge_column(0, 1, False, True, g * EC + EC)
            enter(pe, "adj")
            pe.wait_ge(sem("loops_in"), nth("loops_in", 1))
            for i in range(TT):
                for j in range(TT):
                    ins = TE.matmul(PX[0:TP, 0, 2 * i:2 * i + 2], counts[0:TP, j, i * TP:i * TP + TP],
                                    ones2[0:TP, :], start=j == 0, stop=j == TT - 1)
            ins.then_inc(sem("deg_mm"), 1)
            enter(pe, "deg")
            pe.wait_ge(sem("gnn_full"), nth("gnn_full", 32))
            for t in range(TT + 1):
                if t < TT:
                    b = t % 2
                    pe.wait_ge(sem("gnn_slab"), nth("gnn_slab", t + 1))
                    if begun(t - 1):
                        pe.wait_ge(sem("gnn_x1"), nth("gnn_x1", t - 1))
                    product(PS[:, b, :], L[b], hres, TT, TP, TP, CH_D, D).then_inc(sem("gnn_mm"), 1)
                if t >= 1:
                    transposes("gnn", nb9[(t - 1) % 2], t - 1)
            enter(pe, "gnn")
            pe.wait_ge(sem("qk_full"), nth("qk_full", 32))
            slabs("qk", 16, 0, KT, 128, 128, rT, N, CH_N, 3, "_psf", True)
            enter(pe, "qk")
            pe.wait_ge(sem("v_res"), nth("v_res", 16))
            slabs("v", 10, 32, KT, 128, TP, wv2, D, CH_D, 2, "_val", False)
            enter(pe, "v")

            def scores(hb, t, n):
                b = t % 2
                if begun(n - 1):
                    pe.wait_ge(sem("att_exp"), nth("att_exp", n - 1))
                for part in (0, 1):
                    for off, w in CH_N:
                        ins = TE.matmul(PS[0:TP, b, off:off + w], q_st[hb][:, t * TP:t * TP + TP],
                                        k_st[hb][part][:, off:off + w], start=part == 0, stop=part == 1)
                ins.then_inc(sem("att_sc"), 1)
            for r in rounds(pe, HEADS // 2):
                for hb in (0, 1):
                    pe.wait_ge(sem(f"head{hb}"), nth(f"head{hb}", 112 * r + 112))
                    n0 = r * (2 * TT) + hb * TT
                    scores(hb, 0, n0)
                    for t in range(TT):
                        b = t % 2
                        if t + 1 < TT:
                            scores(hb, t + 1, n0 + t + 1)
                        pe.wait_ge(sem("att_norm"), nth("att_norm", n0 + t + 1))
                        for g, (k0, k1) in enumerate(((0, 4), (4, 8), (8, 10))):
                            if begun(3 * (n0 + t) + g):
                                pe.wait_ge(sem("att_plo"), nth("att_plo", 3 * (n0 + t) + g))
                            for k in range(k0, k1):
                                ins = TE.transpose(PX[0:TP, 0, (k - k0) * TP:(k - k0) * TP + TP],
                                                   prob[b][0:TP, k * TP:k * TP + TP], ident[0:TP, 0:TP])
                            ins.then_inc(sem("att_tr"), 1)
                        if b == 1:
                            g = t // 2
                            ng = r * TT + hb * 5 + g
                            pb = (hb * 5 + g) % 2
                            if begun(3 * (n0 + t) + 3):
                                pe.wait_ge(sem("att_plo"), nth("att_plo", 3 * (n0 + t) + 3))
                            if begun(ng):
                                pe.wait_ge(sem("att_osum"), nth("att_osum", ng))
                            for k in range(TT):
                                for part in (0, 1):
                                    ins = TE.matmul(PX[:, 1, 0:250], v_st[hb][0:TP, k * 128:k * 128 + 128],
                                                    pT[pb][part][0:TP, k * 250:k * 250 + 250],
                                                    start=k == 0 and part == 0, stop=k == TT - 1 and part == 1)
                            ins.then_inc(sem("att_pv"), 1)
            enter(pe, "att")
            pe.wait_ge(sem("op_res"), nth("op_res", 16))
            for t in range(TT + 1):
                if t < TT:
                    b = t % 2
                    pe.wait_ge(sem(f"op_slab{b}"), nth(f"op_slab{b}", 32 * (t // 2 + 1)))
                    if begun(t - 1):
                        pe.wait_ge(sem("op_y"), nth("op_y", t - 1))
                    product(PS[:, b, :], L[b], wo2, KT, 128, TP, CH_D, D).then_inc(sem("op_mm"), 1)
                if t >= 1:
                    transposes("op", nb13[0], t - 1)
            enter(pe, "op")
            pe.wait_ge(sem("gate_split"), nth("gate_split", 1))
            product(PS[:, 0, :], L[0], zT, KT, 128, 128, CH_N, N).then_inc(sem("gate_mm"), 1)
            for t in range(TT):
                pe.wait_ge(sem("gate_log"), nth("gate_log", 1))
                if begun(t):
                    pe.wait_ge(sem("gate_lg"), nth("gate_lg", t))
                TE.transpose(PX[0:TP, 0, 0:8], logT[0:8, t * TP:t * TP + TP], ident[0:8, 0:8]).then_inc(sem("gate_tr"), 1)
                pe.wait_ge(sem("gate_comb"), nth("gate_comb", t + 1))
                if begun(t):
                    pe.wait_ge(sem("gate_ct"), nth("gate_ct", t))
                TE.transpose(PX[0:8, 1, 0:TP], comb[0:TP, :], ident[0:TP, 0:TP]).then_inc(sem("gate_tc"), 1)
            pe.wait_ge(sem("gate_ct"), nth("gate_ct", TT))
            pe.wait_ge(sem("gate_sel"), nth("gate_sel", 16))
            for j in range(3 * EXPERTS):
                e, c = j // 3, j % 3
                off, n = CH_N[c]
                if begun(j - 1):
                    pe.wait_ge(sem("gate_cb"), nth("gate_cb", j - 1))
                TE.matmul(PX[:, j % 2, 0:n], sel[0:EXPERTS, e * 128:e * 128 + 128], combT[0:EXPERTS, off:off + n],
                          start=True, stop=True).then_inc(sem("gate_cm"), 1)
            enter(pe, "gate")
            for r in rounds(pe, EXPERTS):
                for j in range(2):
                    for b in (0, 1):
                        pe.wait_ge(sem("ex_split"), nth("ex_split", 4 * r + 2 * j + b + 1))
                        if begun(3 * (2 * r + j)):
                            pe.wait_ge(sem(("ex_a", "ex_b")[b]), nth(("ex_a", "ex_b")[b], 3 * (2 * r + j)))
                        product(PS[:, b, :], L[b], zT, KT, 128, 128, CH_N, N).then_inc(sem("ex_mm"), 1)
            enter(pe, "ex")
            pe.wait_ge(sem("w3_res"), nth("w3_res", 32))
            pe.wait_ge(sem("b3_in"), nth("b3_in", 16))
            for r in rounds(pe, TT // 2):
                for b in (0, 1):
                    pe.wait_ge(sem(f"w3_slab{b}"), nth(f"w3_slab{b}", 48 * r + 48))
                    if begun(2 * (2 * r + b - 1)):
                        pe.wait_ge(sem("w3_v"), nth("w3_v", 2 * (2 * r + b - 1)))
                    product(PS[:, b, :], LG[b], w3, 2 * KT, 128, TP, CH_D, D, last=False)
                    for off, n in CH_D:
                        ins = TE.matmul(PS[0:TP, b, off:off + n], ct_tile[b][0:EXPERTS, 0:TP],
                                        b3r[0:EXPERTS, off:off + n], start=False, stop=True)
                    ins.then_inc(sem("w3_mm"), 1)

        @block.scalar
        def _(act):
            def stage_hi(ph, n, chunks, src):
                per = len(chunks)
                for r in rounds(act, n // 2):
                    for b in (0, 1):
                        for c in range(per):
                            q, h = per * b + c, (per * b + c) % 2
                            g = r * (2 * per) + q
                            w = chunks[c][1]
                            rows = TP if chunks is CH_D and ph not in ("m2",) else 128
                            act.wait_ge(sem(ph + "_val"), nth(ph + "_val", g + 1))
                            if begun(32 * (r * per + q // 2)):
                                act.wait_ge(sem(f"{ph}_st{h}"), nth(f"{ph}_st{h}", 32 * (r * per + q // 2)))
                            S.copy(HI[0:rows, 512 * h:512 * h + w], src[0:rows, 512 * h:512 * h + w])\
                                .then_inc(sem(ph + "_hi"), 1)

            for t in range(TT):
                act.wait_ge(sem("ln_var"), nth("ln_var", t + 1))
                S.activation(rstd[0:TP, :], small[0:TP, 0:1], ACT.Sqrt).then_inc(sem("ln_sd"), 1)
                act.wait_ge(sem("ln_nb"), nth("ln_nb", t + 1))
                if begun(64 * t):
                    act.wait_ge(sem("ln_st"), nth("ln_st", 64 * t))
                S.copy(HI[0:TP, :], nb[t % 2][0:TP, :]).then_inc(sem("ln_hi"), 1)
                act.wait_ge(sem("ln_tv"), nth("ln_tv", t + 1))
                S.copy(xnT[0][:, :].rearrange("p (k c) -> p k c", k=KT)[:, :, t * TP:(t + 1) * TP],
                       tv[:, :].rearrange("p (k c) -> p k c", k=KT)).then_inc(sem("ln_nh"), 1)
            enter(act, "ln")

            def stage_elu(ph, n, chunks, rows):
                per = len(chunks)
                for r in rounds(act, n // 2):
                    for b in (0, 1):
                        for c in range(per):
                            q, h = per * b + c, (per * b + c) % 2
                            g = r * (2 * per) + q
                            w = chunks[c][1]
                            cols = slice(512 * h, 512 * h + w)
                            act.wait_ge(sem(ph + "_m"), nth(ph + "_m", g + 1))
                            S.activation(T2[0:rows, cols], T2[0:rows, cols], ACT.Exp).then_inc(sem(ph + "_e"), 1)
                            act.wait_ge(sem(ph + "_val"), nth(ph + "_val", g + 1))
                            if begun(32 * (r * per + q // 2)):
                                act.wait_ge(sem(f"{ph}_st{h}"), nth(f"{ph}_st{h}", 32 * (r * per + q // 2)))
                            S.copy(HI[0:rows, cols], T1[0:rows, cols]).then_inc(sem(ph + "_hi"), 1)
            stage_elu("q", 8, CH_N, 128)
            enter(act, "q")
            stage_elu("k", 10, CH_D, TP)
            enter(act, "k")
            stage_hi("h", 10, CH_D, T1)
            enter(act, "h")

            def resident_hi(ph, dst):
                for r in rounds(act, 4):
                    for b in (0, 1):
                        act.wait_ge(sem(ph + "_mm"), nth(ph + "_mm", 2 * r + b + 1))
                        for c, (off, w) in enumerate(CH_D):
                            S.copy(dst[0][:, bass.ds(r * (2 * D) + (b * D + off), w)], PS[:, b, off:off + w])\
                                .then_inc(sem(ph + "_hi"), 1)
            resident_hi("m1", m1T)
            enter(act, "m1")
            stage_hi("m2", 8, CH_D, T1)
            enter(act, "m2")
            resident_hi("m3", m3)
            enter(act, "mix")
            for g in range(PAIRS):
                act.wait_ge(sem("oh_used"), nth("oh_used", (g + 1) * EC))
                S.copy(counts[0:TP, 2 * g, :], PS[0:TP, 0, 0:N]).then_inc(sem("adj_a"), 1)
            act.wait_ge(sem("deg_mm"), nth("deg_mm", 1))
            S.activation(dis[0:TP, :], PX[0:TP, 0, 0:2 * TT].rearrange("p (t e) -> p t e", e=2)[:, :, 0],
                         ACT.Sqrt).then_inc(sem("deg_sd"), 1)
            enter(act, "deg")

            cv = counts[:, :, :]

            def gnn_slab(t):
                b = t % 2
                if begun(t - 1):
                    act.wait_ge(sem("gnn_mm"), nth("gnn_mm", t - 1))
                S.copy(L[b][0][0:TP, 0:TT * TP].rearrange("p (k c) -> p k c", k=TT),
                       cv[0:TP, :, t * TP:t * TP + TP]).then_inc(sem("gnn_sh"), 1)

            gnn_slab(0)
            for t in range(TT):
                if t + 1 < TT:
                    gnn_slab(t + 1)
                act.wait_ge(sem("gnn_var"), nth("gnn_var", t + 1))
                S.activation(rstd[0:TP, :], small[0:TP, 0:1], ACT.Sqrt).then_inc(sem("gnn_sd"), 1)
                act.wait_ge(sem("gnn_u"), nth("gnn_u", t + 1))
                if begun(t - 1):
                    act.wait_ge(sem("gnn_tr"), nth("gnn_tr", t - 1))
                S.activation(nb9[t % 2][0:TP, :], u9[0:TP, :], ACT.Square, accum_out=small[0:TP, 2:3])\
                    .then_inc(sem("gnn_sq"), 1)
                act.wait_ge(sem("gnn_ms"), nth("gnn_ms", t + 1))
                S.activation(small[0:TP, 4:5], small[0:TP, 3:4], ACT.Sqrt).then_inc(sem("gnn_rsd"), 1)
                act.wait_ge(sem("gnn_tv"), nth("gnn_tv", t + 1))
                if begun(48 * t):
                    act.wait_ge(sem("gnn_st"), nth("gnn_st", 48 * t))
                S.copy(HI[:, 0:KT * TP], tv9[:, :]).then_inc(sem("gnn_nh"), 1)
            enter(act, "gnn")
            act.wait_ge(sem("consts"), nth("consts", 128))
            for r in rounds(act, 8):
                for b in (0, 1):
                    for c, (off, w) in enumerate(CH_N):
                        q, h = 3 * b + c, (3 * b + c) % 2
                        g = r * 6 + q
                        cols = slice(512 * h, 512 * h + w)
                        if c == 0:
                            act.wait_ge(sem("qk_mm"), nth("qk_mm", 2 * r + b + 1))
                        if begun(g - 1):
                            act.wait_ge(sem("qk_lo"), nth("qk_lo", g - 1))
                        apart(act)
                        S.activation(T1[:, cols], PS[:, b, off:off + w], ACT.Identity,
                                     bias=bqk[:, bass.ds(2 * r + b, 1)]).then_inc(sem("qk_psf"), 1)
                        act.wait_ge(sem("qk_psf"), nth("qk_psf", g + 1))
                        for k in range(4):
                            o = k + 1 if k % 2 == 0 else k - 1
                            ins = S.copy(T3[32 * k:32 * k + 32, cols], T1[32 * o:32 * o + 32, cols])
                        ins.then_inc(sem("qk_rot"), 1)
                        act.wait_ge(sem("qk_val"), nth("qk_val", g + 1))
                        if begun(32 * (r * 3 + q // 2)):
                            act.wait_ge(sem(f"qk_st{h}"), nth(f"qk_st{h}", 32 * (r * 3 + q // 2)))
                        S.copy(HI[:, cols], T2[:, cols]).then_inc(sem("qk_hi"), 1)
            enter(act, "qk")
            stage_hi("v", 10, CH_D, T1)
            enter(act, "v")
            def exp_tile(j, n):
                b = j % 2
                act.wait_ge(sem("att_nm"), nth("att_nm", n + 1))
                if begun(3 * (n - 1)):
                    act.wait_ge(sem("att_tr"), nth("att_tr", 3 * (n - 1)))
                S.activation(prob[b][0:TP, :], PS[0:TP, b, 0:N], ACT.Exp, bias=nmx[0:TP, b:b + 1],
                             scale=HD ** -0.5, accum_out=rs[0:TP, b:b + 1]).then_inc(sem("att_exp"), 1)
            for r in rounds(act, HEADS // 2):
                for j in range(2 * TT):
                    n = r * (2 * TT) + j
                    exp_tile(j, n)
                    gl = j // 2
                    pb = gl % 2
                    for g, (k0, k1) in enumerate(((0, 4), (4, 8), (8, 10))):
                        act.wait_ge(sem("att_tr"), nth("att_tr", 3 * n + g + 1))
                        if g == 0 and j % 2 == 0:
                            if begun(r * TT + gl - 1):
                                act.wait_ge(sem("att_pv"), nth("att_pv", r * TT + gl - 1))
                        dst = pT[pb][0][0:TP, :].rearrange("p (k c) -> p k c", k=TT)[:, k0:k1, (j % 2) * TP:(j % 2) * TP + TP]
                        S.copy(dst, PX[0:TP, 0, 0:(k1 - k0) * TP].rearrange("p (k c) -> p k c", k=k1 - k0))\
                            .then_inc(sem("att_phi"), 1)
                    if j % 2 == 1:
                        ng = r * TT + gl
                        oc = slice(250 * pb, 250 * pb + 250)
                        act.wait_ge(sem("att_pv"), nth("att_pv", ng + 1))
                        if begun(ng - 1):
                            act.wait_ge(sem("att_osum"), nth("att_osum", ng - 1))
                        S.copy(o_tmp[0:64, oc], PX[64:128, 1, 0:250]).then_inc(sem("att_oc"), 1)
                        act.wait_ge(sem("att_osum"), nth("att_osum", ng + 1))
                        if begun(32 * (r * 5 + gl // 2)):
                            act.wait_ge(sem(f"att_st{pb}"), nth(f"att_st{pb}", 32 * (r * 5 + gl // 2)))
                        S.copy(o_hi[0:64, oc], o_sum[0:64, oc]).then_inc(sem("att_ohi"), 1)
            enter(act, "att")
            for t in range(TT):
                act.wait_ge(sem("op_y"), nth("op_y", t + 1))
                if begun(t):
                    act.wait_ge(sem("op_tr"), nth("op_tr", t))
                S.activation(nb13[0][0:TP, :], T1[0:TP, :], ACT.Square, accum_out=small[0:TP, 2:3])\
                    .then_inc(sem("op_sq"), 1)
                act.wait_ge(sem("op_ms"), nth("op_ms", t + 1))
                S.activation(small[0:TP, 4:5], small[0:TP, 3:4], ACT.Sqrt).then_inc(sem("op_rsd"), 1)
                act.wait_ge(sem("op_tv"), nth("op_tv", t + 1))
                S.copy(zT[0][:, :].rearrange("p (k c) -> p k c", k=KT)[:, :, t * TP:(t + 1) * TP],
                       tv13[:, :].rearrange("p (k c) -> p k c", k=KT)).then_inc(sem("op_nh"), 1)
            enter(act, "op")
            act.wait_ge(sem("gate_mm"), nth("gate_mm", 1))
            S.copy(logT[0:8, :], PS[0:8, 0, 0:N]).then_inc(sem("gate_log"), 1)
            for t in range(TT):
                act.wait_ge(sem("gate_top"), nth("gate_top", t + 1))
                S.activation(ex8[0:TP, :], lg[0:TP, :], ACT.Exp, bias=nm1[0:TP, 0:1]).then_inc(sem("gate_e8"), 1)
                act.wait_ge(sem("gate_tc"), nth("gate_tc", t + 1))
                S.copy(combT[0:8, t * TP:t * TP + TP], PX[0:8, 1, 0:TP]).then_inc(sem("gate_ct"), 1)
            for j in range(3 * EXPERTS):
                off, n = CH_N[j % 3]
                act.wait_ge(sem("gate_cm"), nth("gate_cm", j + 1))
                S.copy(combB[:, j // 3, off:off + n], PX[:, j % 2, 0:n]).then_inc(sem("gate_cb"), 1)
            enter(act, "gate")
            for r in rounds(act, EXPERTS):
                for j in range(2):
                    for c, (off, w) in enumerate(CH_N):
                        q, h = 3 * j + c, (3 * j + c) % 2
                        g = r * 6 + q
                        cols = slice(512 * h, 512 * h + w)
                        if c == 0:
                            act.wait_ge(sem("ex_mm"), nth("ex_mm", 4 * r + 2 * j + 1))
                        if begun(g - 1):
                            act.wait_ge(sem("ex_b"), nth("ex_b", g - 1))
                        apart(act)
                        S.activation(T1[:, cols], PS[:, 0, off:off + w], ACT.Silu,
                                     bias=b1[:, bass.ds(2 * r + j, 1)]).then_inc(sem("ex_a"), 1)
                        act.wait_ge(sem("ex_val"), nth("ex_val", g + 1))
                        if begun(32 * (r * 3 + q // 2)):
                            act.wait_ge(sem(f"ex_st{h}"), nth(f"ex_st{h}", 32 * (r * 3 + q // 2)))
                        S.copy(HI[:, cols], T2[:, cols]).then_inc(sem("ex_hi"), 1)


        @block.vector
        def _(dve):
            P_SUB = ALU.subtract

            V.memset(ones2[:, :], 1.0).then_inc(sem("ones2_ready"), 1)

            def stage_lo(ph, r, per, q, g, src, cols, rows):
                dve.wait_ge(sem(ph + "_hi"), nth(ph + "_hi", g + 1))
                if begun(32 * (r * per + q // 2)):
                    dve.wait_ge(sem(f"{ph}_st{q % 2}"), nth(f"{ph}_st{q % 2}", 32 * (r * per + q // 2)))
                V.tensor_tensor(LO[0:rows, cols], src[0:rows, cols], HI[0:rows, cols].bitcast(F32), P_SUB)\
                    .then_inc(sem(ph + "_lo"), 1)

            def stats(ph, t, src, cols0=0):
                for k in range(2):
                    V.bn_stats(stat6[0:TP, 6 * k:6 * k + 6], src[0:TP, 512 * k:512 * k + 512]).then_inc(sem(ph + "_bn"), 1)
                dve.wait_ge(sem(ph + "_bn"), nth(ph + "_bn", 2 * t + 2))
                V.bn_aggr(mv[0:TP, :], stat6[0:TP, :]).then_inc(sem(ph + "_ag"), 1)
                dve.wait_ge(sem(ph + "_ag"), nth(ph + "_ag", t + 1))
                V.tensor_scalar(small[0:TP, 0:1], mv[0:TP, 1:2], LN_EPS, None, ALU.add).then_inc(sem(ph + "_var"), 1)
                dve.wait_ge(sem(ph + "_sd"), nth(ph + "_sd", t + 1))
                V.reciprocal(small[0:TP, 1:2], rstd[0:TP, :]).then_inc(sem(ph + "_rc"), 1)
                dve.wait_ge(sem(ph + "_rc"), nth(ph + "_rc", t + 1))

            def ln_tail(t):
                dve.wait_ge(sem("ln_hi"), nth("ln_hi", t + 1))
                if begun(64 * t):
                    dve.wait_ge(sem("ln_st"), nth("ln_st", 64 * t))
                V.tensor_tensor(LO[0:TP, :], nb[t % 2][0:TP, :], HI[0:TP, :].bitcast(F32), P_SUB).then_inc(sem("ln_lo"), 1)
                dve.wait_ge(sem("ln_tr"), nth("ln_tr", t + 1))
                if begun(t):
                    dve.wait_ge(sem("ln_rt"), nth("ln_rt", t))
                px = PX[:, :, 0:4 * TP]
                V.tensor_copy(tv[:, :].rearrange("p (a c) -> p a c", a=2), px).then_inc(sem("ln_tv"), 1)
                dve.wait_ge(sem("ln_nh"), nth("ln_nh", t + 1))
                tile = slice(t * TP, (t + 1) * TP)
                V.tensor_tensor(xnT[1][:, :].rearrange("p (k c) -> p k c", k=KT)[:, :, tile],
                                tv[:, :].rearrange("p (k c) -> p k c", k=KT),
                                xnT[0][:, :].rearrange("p (k c) -> p k c", k=KT)[:, :, tile].bitcast(F32), P_SUB)\
                    .then_inc(sem("ln_rt"), 1)
            for t in range(TT):
                b = t % 2
                src = [T1, T2][b]
                dve.wait_ge(sem(f"ln_x{b}"), nth(f"ln_x{b}", 16 * (t // 2 + 1)))
                stats("ln", t, src)
                V.tensor_scalar(nb[b][0:TP, :], src[0:TP, :], mv[0:TP, 0:1], small[0:TP, 1:2], ALU.subtract, ALU.mult)\
                    .then_inc(sem("ln_nb"), 1)
                ln_tail(t)
            enter(dve, "ln")

            def elu(ph, n, chunks, rows, first):
                per = len(chunks)
                for r in rounds(dve, n // 2):
                    for b in (0, 1):
                        for c, (off, w) in enumerate(chunks):
                            q = per * b + c
                            h = q % 2
                            g = r * (2 * per) + q
                            cols = slice(512 * h, 512 * h + w)
                            if c == 0:
                                dve.wait_ge(sem(ph + "_mm"), nth(ph + "_mm", 2 * r + b + 1))
                            first(r, b, off, w, cols)
                            dve.wait_ge(sem(ph + "_psf"), nth(ph + "_psf", g + 1))
                            V.tensor_scalar(T2[0:rows, cols], T1[0:rows, cols], 0.0, None, ALU.min).then_inc(sem(ph + "_m"), 1)
                            dve.wait_ge(sem(ph + "_e"), nth(ph + "_e", g + 1))
                            V.scalar_tensor_tensor(T1[0:rows, cols], T1[0:rows, cols], 0.0, T2[0:rows, cols],
                                                   ALU.max, ALU.add).then_inc(sem(ph + "_val"), 1)
                            dve.wait_ge(sem(ph + "_val"), nth(ph + "_val", g + 1))
                            stage_lo(ph, r, per, q, g, T1, cols, rows)

            dve.wait_ge(sem("consts"), nth("consts", 128))

            def q_first(r, b, off, w, cols):
                V.tensor_scalar(T1[:, cols], PS[:, b, off:off + w], bq[:, bass.ds(2 * r + b, 1)], None, ALU.add)\
                    .then_inc(sem("q_psf"), 1)
            elu("q", 8, CH_N, 128, q_first)
            enter(dve, "q")
            V.memset(ones_r[:, :].bitcast(F32), 1.0).then_inc(sem("ones_ready"), 1)
            dve.wait_ge(sem("k_bias"), nth("k_bias", 16))

            def k_first(r, b, off, w, cols):
                V.tensor_tensor(T1[0:TP, cols], PS[0:TP, b, off:off + w], bias_b[0:TP, off:off + w], ALU.add)\
                    .then_inc(sem("k_psf"), 1)
            elu("k", 10, CH_D, TP, k_first)
            enter(dve, "k")

            def plain(ph, n, chunks, rows, first):
                per = len(chunks)
                for r in rounds(dve, n // 2):
                    for b in (0, 1):
                        for c, (off, w) in enumerate(chunks):
                            q = per * b + c
                            g = r * (2 * per) + q
                            cols = slice(512 * (q % 2), 512 * (q % 2) + w)
                            if c == 0:
                                dve.wait_ge(sem(ph + "_mm"), nth(ph + "_mm", 2 * r + b + 1))
                            first(r, b, off, w, cols)
                            dve.wait_ge(sem(ph + "_val"), nth(ph + "_val", g + 1))
                            stage_lo(ph, r, per, q, g, T1, cols, rows)

            def add_rows(ph, bias):
                def first(r, b, off, w, cols):
                    V.tensor_tensor(T1[0:TP, cols], PS[0:TP, b, off:off + w], bias[0:TP, off:off + w], ALU.add)\
                        .then_inc(sem(ph + "_val"), 1)
                return first
            dve.wait_ge(sem("g_bias"), nth("g_bias", 16))
            plain("h", 10, CH_D, TP, add_rows("h", bias_a))
            enter(dve, "h")
            dve.wait_ge(sem("ks_mm"), nth("ks_mm", 1))
            V.tensor_copy(ksb[:, :], PS[:, 0, 0:D]).then_inc(sem("ks_v"), 1)

            def resident_lo(ph, dst):
                for r in rounds(dve, 4):
                    for b in (0, 1):
                        for c, (off, w) in enumerate(CH_D):
                            dve.wait_ge(sem(ph + "_hi"), nth(ph + "_hi", 4 * r + 2 * b + c + 1))
                            cols = bass.ds(r * (2 * D) + (b * D + off), w)
                            V.tensor_tensor(dst[1][:, cols], PS[:, b, off:off + w], dst[0][:, cols].bitcast(F32), P_SUB)\
                                .then_inc(sem(ph + "_lo"), 1)
            resident_lo("m1", m1T)
            enter(dve, "m1")

            def m2_first(r, b, off, w, cols):
                V.scalar_tensor_tensor(T1[:, cols], ksb[:, off:off + w], bv[:, bass.ds(2 * r + b, 1)],
                                       PS[:, b, off:off + w], ALU.mult, ALU.add).then_inc(sem("m2_val"), 1)
            plain("m2", 8, CH_D, 128, m2_first)
            enter(dve, "m2")
            dve.wait_ge(sem("ks_tr"), nth("ks_tr", 1))
            V.tensor_scalar(T1[:, 0:2 * KT].rearrange("p (k e) -> p k e", e=2),
                            PX[:, :, :].rearrange("p a (k c) -> p (a k) c", c=128)[:, :, 0:2], 1e-6, None, ALU.add)\
                .then_inc(sem("ks_c1"), 1)
            dve.wait_ge(sem("ks_c1"), nth("ks_c1", 1))
            V.tensor_copy(ksT_hi[:, :], T1[:, 0:2 * KT]).then_inc(sem("ks_c2"), 1)
            dve.wait_ge(sem("ks_c2"), nth("ks_c2", 1))
            V.tensor_tensor(ksT_lo[:, :], T1[:, 0:2 * KT], ksT_hi[:, :].bitcast(F32), P_SUB).then_inc(sem("ks_col"), 1)
            resident_lo("m3", m3)
            enter(dve, "m3")
            dve.wait_ge(sem("o_bias"), nth("o_bias", 16))
            for r in rounds(dve, TT // 2):
                for b in (0, 1):
                    dve.wait_ge(sem("mix_mm"), nth("mix_mm", 2 * r + b + 1))
                    V.reciprocal(zr[0:TP, b:b + 1], PS[0:TP, b, 1024:1025]).then_inc(sem("mix_z"), 1)
                    for c in (0, 1):
                        g = 4 * r + 2 * b + c
                        cols = slice(512 * c, 512 * c + 512)
                        dve.wait_ge(sem(f"mix_in{c}"), nth(f"mix_in{c}", 32 * r + 16 * b + 16))
                        if begun(32 * r + 16 * b):
                            dve.wait_ge(sem(f"mix_st{c}"), nth(f"mix_st{c}", 32 * r + 16 * b))
                        V.tensor_tensor(T1[0:TP, cols], T2[0:TP, cols], bias_a[0:TP, cols], ALU.add).then_inc(sem("mix_xb"), 1)
                        dve.wait_ge(sem("mix_xb"), nth("mix_xb", g + 1))
                        dve.wait_ge(sem("mix_z"), nth("mix_z", 2 * r + b + 1))
                        V.scalar_tensor_tensor(T1[0:TP, cols], PS[0:TP, b, cols], zr[0:TP, b:b + 1], T1[0:TP, cols],
                                               ALU.mult, ALU.add).then_inc(sem("mix_v"), 1)
            enter(dve, "mix")
            dve.wait_ge(sem("edges"), nth("edges", 32))
            dve.wait_ge(sem("iota"), nth("iota", 1))
            V.tensor_copy(edge_src[0:TP, :], edge_src_i[0:TP, :]).then_inc(sem("edge_f"), 1)
            V.tensor_copy(edge_dst[0:TP, :], edge_dst_i[0:TP, :]).then_inc(sem("edge_f"), 1)
            dve.wait_ge(sem("edge_f"), nth("edge_f", 2))

            def onehots(g, b, col, used):
                if used is not None:
                    dve.wait_ge(sem("oh_used"), nth("oh_used", used))
                V.tensor_scalar(oh_src[0:TP, b, :], iota[0:TP, :], edge_src[0:TP, col], None, ALU.is_equal)
                V.tensor_scalar(oh_dst[0:TP, b, :].rearrange("p (h c) -> p h c", h=2)[:, :, 0:TP],
                                iota[0:TP, 2 * g * TP:2 * (g + 1) * TP].rearrange("p (h c) -> p h c", h=2),
                                edge_dst[0:TP, col], None, ALU.is_equal).then_inc(sem("oh_ready"), 1)
            for g in range(PAIRS):
                for b in (0, 1):
                    onehots(g, b, slice(b, b + 1), g * EC + b - 1 if g else None)
                with dve.Fori(1, EC // 2) as i:
                    for b in (0, 1):
                        onehots(g, b, bass.ds(2 * i + b, 1), 2 * i + (g * EC + b - 1))
                dve.wait_ge(sem("oh_used"), nth("oh_used", (g + 1) * EC))
                dve.wait_ge(sem("adj_a"), nth("adj_a", g + 1))
                V.tensor_copy(counts[0:TP, 2 * g + 1, :], PS[0:TP, 1, 0:N]).then_inc(sem("adj_ev"), 1)
            dve.wait_ge(sem("adj_ev"), nth("adj_ev", PAIRS))
            for j in range(TT):
                ins = V.tensor_tensor(counts[0:TP, j, j * TP:(j + 1) * TP], counts[0:TP, j, j * TP:(j + 1) * TP],
                                      ident[0:TP, 0:TP], ALU.add)
            ins.then_inc(sem("loops_in"), 1)
            dve.wait_ge(sem("loops_in"), nth("loops_in", 1))
            dve.wait_ge(sem("deg_sd"), nth("deg_sd", 1))
            V.reciprocal(dis[0:TP, :], dis[0:TP, :]).then_inc(sem("deg_r"), 1)
            dve.wait_ge(sem("deg_r"), nth("deg_r", 1))
            for j in range(TT):
                ins = V.tensor_scalar(counts[0:TP, j, :], counts[0:TP, j, :], dis[0:TP, j:j + 1], None, ALU.mult)
            ins.then_inc(sem("deg_scaled"), 1)
            enter(dve, "deg")

            def gnn_slab(t):
                b = t % 2
                dve.wait_ge(sem("gnn_sh"), nth("gnn_sh", t + 1))
                V.tensor_tensor(L[b][1][0:TP, 0:TT * TP].rearrange("p (k c) -> p k c", k=TT),
                                counts[0:TP, :, t * TP:t * TP + TP],
                                L[b][0][0:TP, 0:TT * TP].rearrange("p (k c) -> p k c", k=TT).bitcast(F32), P_SUB)\
                    .then_inc(sem("gnn_slab"), 1)

            def rms(ph, t, src, dst):
                dve.wait_ge(sem(ph + "_sq"), nth(ph + "_sq", t + 1))
                V.tensor_scalar(small[0:TP, 3:4], small[0:TP, 2:3], 1.0 / D, RMS_EPS, ALU.mult, ALU.add)\
                    .then_inc(sem(ph + "_ms"), 1)
                dve.wait_ge(sem(ph + "_rsd"), nth(ph + "_rsd", t + 1))
                V.reciprocal(small[0:TP, 5:6], small[0:TP, 4:5]).then_inc(sem(ph + "_rmsr"), 1)
                dve.wait_ge(sem(ph + "_rmsr"), nth(ph + "_rmsr", t + 1))
                V.tensor_scalar(dst[0:TP, :], src[0:TP, :], small[0:TP, 5:6], None, ALU.mult).then_inc(sem(ph + "_nb"), 1)

            def weighted(ph, t, w, dst):
                dve.wait_ge(sem(ph + "_tr"), nth(ph + "_tr", t + 1))
                if begun(t):
                    dve.wait_ge(sem(ph + "_rt"), nth(ph + "_rt", t))
                V.tensor_tensor(dst[:, :].rearrange("p (a k c) -> p a k c", a=2, k=4),
                                PX[:, :, 0:4 * TP].rearrange("p a (k c) -> p a k c", k=4),
                                w[:, :].rearrange("p (a k) -> p a k", a=2).unsqueeze(3).broadcast_to([128, 2, 4, TP]),
                                ALU.mult).then_inc(sem(ph + "_tv"), 1)
            gnn_slab(0)
            for t in range(TT):
                if t + 1 < TT:
                    gnn_slab(t + 1)
                b = t % 2
                dve.wait_ge(sem("gnn_acc"), nth("gnn_acc", 16 * (t + 1)))
                dve.wait_ge(sem("gnn_mm"), nth("gnn_mm", t + 1))
                if begun(48 * t):
                    dve.wait_ge(sem("gnn_st"), nth("gnn_st", 48 * t))
                V.scalar_tensor_tensor(T1[0:TP, :], PS[0:TP, b, 0:D], dis[0:TP, t:t + 1], T2[0:TP, :],
                                       ALU.mult, ALU.add).then_inc(sem("gnn_x1"), 1)
                dve.wait_ge(sem("gnn_x1"), nth("gnn_x1", t + 1))
                stats("gnn", t, T1)
                V.tensor_copy(mean_all[0:TP, t:t + 1], mv[0:TP, 0:1])
                V.tensor_copy(rstd_all[0:TP, t:t + 1], small[0:TP, 1:2])
                V.tensor_scalar(u9[0:TP, :], T1[0:TP, :], mv[0:TP, 0:1], small[0:TP, 1:2], ALU.subtract, ALU.mult)\
                    .then_inc(sem("gnn_u"), 1)
                rms("gnn", t, u9, nb9[b])
                weighted("gnn", t, n1w, tv9)
                dve.wait_ge(sem("gnn_nh"), nth("gnn_nh", t + 1))
                V.tensor_tensor(LO[:, 0:KT * TP], tv9[:, :], HI[:, 0:KT * TP].bitcast(F32), P_SUB).then_inc(sem("gnn_rt"), 1)
            enter(dve, "gnn")
            dve.wait_ge(sem("rope_tables"), nth("rope_tables", 32))
            for r in rounds(dve, 8):
                for b in (0, 1):
                    for c, (off, w) in enumerate(CH_N):
                        q = 3 * b + c
                        g = r * 6 + q
                        cols = slice(512 * (q % 2), 512 * (q % 2) + w)
                        dve.wait_ge(sem("qk_psf"), nth("qk_psf", g + 1))
                        V.tensor_tensor(T2[:, cols], T1[:, cols], cosT[:, off:off + w], ALU.mult).then_inc(sem("qk_c"), 1)
                        dve.wait_ge(sem("qk_rot"), nth("qk_rot", g + 1))
                        V.tensor_tensor(T3[:, cols], T3[:, cols], sinT[:, off:off + w], ALU.mult).then_inc(sem("qk_s"), 1)
                        dve.wait_ge(sem("qk_s"), nth("qk_s", g + 1))
                        V.tensor_tensor(T2[:, cols], T2[:, cols], T3[:, cols], ALU.add).then_inc(sem("qk_val"), 1)
                        dve.wait_ge(sem("qk_val"), nth("qk_val", g + 1))
                        stage_lo("qk", r, 3, q, g, T2, cols, 128)
            enter(dve, "qk")
            dve.wait_ge(sem("v2_bias"), nth("v2_bias", 16))
            plain("v", 10, CH_D, TP, add_rows("v", bias_a))
            enter(dve, "v")

            def max_tile(j, n):
                b = j % 2
                dve.wait_ge(sem("att_sc"), nth("att_sc", n + 1))
                V.reduce_max(mx[0:TP, b:b + 1], PS[0:TP, b, 0:N], AX.X).then_inc(sem("att_mx"), 1)
                dve.wait_ge(sem("att_mx"), nth("att_mx", n + 1))
                V.tensor_scalar(nmx[0:TP, b:b + 1], mx[0:TP, b:b + 1], -(HD ** -0.5), None, ALU.mult)\
                    .then_inc(sem("att_nm"), 1)
            for r in rounds(dve, HEADS // 2):
                for j in range(2 * TT):
                    n = r * (2 * TT) + j
                    gl, pb, b = j // 2, j // 2 % 2, j % 2
                    max_tile(j, n)
                    dve.wait_ge(sem("att_exp"), nth("att_exp", n + 1))
                    V.reciprocal(rr[0:TP, b:b + 1], rs[0:TP, b:b + 1]).then_inc(sem("att_rr"), 1)
                    for g, (k0, k1) in enumerate(((0, 4), (4, 8), (8, 10))):
                        dve.wait_ge(sem("att_phi"), nth("att_phi", 3 * n + g + 1))
                        view = [x[0:TP, :].rearrange("p (k c) -> p k c", k=TT)[:, k0:k1, b * TP:b * TP + TP] for x in pT[pb]]
                        V.tensor_tensor(view[1], PX[0:TP, 0, 0:(k1 - k0) * TP].rearrange("p (k c) -> p k c", k=k1 - k0),
                                        view[0].bitcast(F32), P_SUB).then_inc(sem("att_plo"), 1)
                    if b == 1:
                        ng = r * TT + gl
                        oc = slice(250 * pb, 250 * pb + 250)
                        dve.wait_ge(sem("att_oc"), nth("att_oc", ng + 1))
                        V.tensor_tensor(o_sum[0:64, oc], PX[0:64, 1, 0:250], o_tmp[0:64, oc], ALU.add)\
                            .then_inc(sem("att_osum"), 1)
                        dve.wait_ge(sem("att_ohi"), nth("att_ohi", ng + 1))
                        if begun(32 * (r * 5 + gl // 2)):
                            dve.wait_ge(sem(f"att_st{pb}"), nth(f"att_st{pb}", 32 * (r * 5 + gl // 2)))
                        V.tensor_tensor(o_lo[0:64, oc], o_sum[0:64, oc], o_hi[0:64, oc].bitcast(F32), P_SUB)\
                            .then_inc(sem("att_olo"), 1)
            enter(dve, "att")
            dve.wait_ge(sem("ob_bias"), nth("ob_bias", 16))
            for t in range(TT):
                b = t % 2
                dve.wait_ge(sem("op_x1"), nth("op_x1", 16 * (t + 1)))
                V.tensor_scalar(T1[0:TP, :], T2[0:TP, :], mean_all[0:TP, t:t + 1], rstd_all[0:TP, t:t + 1],
                                ALU.subtract, ALU.mult).then_inc(sem("op_u"), 1)
                dve.wait_ge(sem("op_u"), nth("op_u", t + 1))
                V.tensor_tensor(T1[0:TP, :], T1[0:TP, :], bias_a2[0:TP, :], ALU.add).then_inc(sem("op_ub"), 1)
                dve.wait_ge(sem("op_ub"), nth("op_ub", t + 1))
                dve.wait_ge(sem("op_mm"), nth("op_mm", t + 1))
                V.tensor_tensor(T1[0:TP, :], T1[0:TP, :], PS[0:TP, b, 0:D], ALU.add).then_inc(sem("op_y"), 1)
                dve.wait_ge(sem("op_y"), nth("op_y", t + 1))
                V.tensor_tensor(T2[0:TP, :], T2[0:TP, :], T1[0:TP, :], ALU.add).then_inc(sem("op_xy"), 1)
                rms("op", t, T1, nb13[0])
                weighted("op", t, n2w, tv13)
                dve.wait_ge(sem("op_nh"), nth("op_nh", t + 1))
                tile = slice(t * TP, (t + 1) * TP)
                V.tensor_tensor(zT[1][:, :].rearrange("p (k c) -> p k c", k=KT)[:, :, tile],
                                tv13[:, :].rearrange("p (k c) -> p k c", k=KT),
                                zT[0][:, :].rearrange("p (k c) -> p k c", k=KT)[:, :, tile].bitcast(F32), P_SUB)\
                    .then_inc(sem("op_rt"), 1)
            enter(dve, "op")
            dve.wait_ge(sem("gate_iota"), nth("gate_iota", 1))
            for t in range(TT):
                dve.wait_ge(sem("gate_tr"), nth("gate_tr", t + 1))
                if begun(t):
                    dve.wait_ge(sem("gate_e8"), nth("gate_e8", t))
                V.tensor_copy(lg[0:TP, :], PX[0:TP, 0, 0:8]).then_inc(sem("gate_lg"), 1)
                dve.wait_ge(sem("gate_lg"), nth("gate_lg", t + 1))
                V.max(m8[0:TP, :], lg[0:TP, :]).then_inc(sem("gate_c"), 1)
                dve.wait_ge(sem("gate_c"), nth("gate_c", 8 * t + 1))
                V.tensor_scalar(nm1[0:TP, 0:1], m8[0:TP, 0:1], -1.0, None, ALU.mult).then_inc(sem("gate_top"), 1)
                V.max_index(top_i[0:TP, :], m8[0:TP, :], lg[0:TP, :]).then_inc(sem("gate_c"), 1)
                dve.wait_ge(sem("gate_c"), nth("gate_c", 8 * t + 2))
                V.tensor_copy(top_f[0:TP, :], top_i[0:TP, :]).then_inc(sem("gate_c"), 1)
                if begun(8 * t + 3):
                    dve.wait_ge(sem("gate_c"), nth("gate_c", 8 * t + 3))
                V.tensor_scalar(mask[0:TP, :], eight[0:TP, :], top_f[0:TP, 0:1], None, ALU.is_equal).then_inc(sem("gate_c"), 1)
                if begun(8 * t + 4):
                    dve.wait_ge(sem("gate_c"), nth("gate_c", 8 * t + 4))
                V.scalar_tensor_tensor(mask[0:TP, :], eight[0:TP, :], top_f[0:TP, 1:2], mask[0:TP, :],
                                       ALU.is_equal, ALU.add).then_inc(sem("gate_c"), 1)
                if begun(8 * t + 5):
                    dve.wait_ge(sem("gate_c"), nth("gate_c", 8 * t + 5))
                dve.wait_ge(sem("gate_e8"), nth("gate_e8", t + 1))
                V.tensor_tensor(comb[0:TP, :], ex8[0:TP, :], mask[0:TP, :], ALU.mult).then_inc(sem("gate_c"), 1)
                if begun(8 * t + 6):
                    dve.wait_ge(sem("gate_c"), nth("gate_c", 8 * t + 6))
                V.reduce_sum(small[0:TP, 0:1], comb[0:TP, :], AX.X).then_inc(sem("gate_c"), 1)
                if begun(8 * t + 7):
                    dve.wait_ge(sem("gate_c"), nth("gate_c", 8 * t + 7))
                V.reciprocal(small[0:TP, 1:2], small[0:TP, 0:1]).then_inc(sem("gate_c"), 1)
                if begun(8 * t + 8):
                    dve.wait_ge(sem("gate_c"), nth("gate_c", 8 * t + 8))
                V.tensor_scalar(comb[0:TP, :], comb[0:TP, :], small[0:TP, 1:2], None, ALU.mult).then_inc(sem("gate_comb"), 1)
                dve.wait_ge(sem("gate_tc"), nth("gate_tc", t + 1))
            enter(dve, "gate")
            for r in rounds(dve, EXPERTS):
                for j in range(2):
                    for c, (off, w) in enumerate(CH_N):
                        q = 3 * j + c
                        g = r * 6 + q
                        cols = slice(512 * (q % 2), 512 * (q % 2) + w)
                        if c == 0:
                            dve.wait_ge(sem("ex_mm"), nth("ex_mm", 4 * r + 2 * j + 2))
                        dve.wait_ge(sem("ex_a"), nth("ex_a", g + 1))
                        V.scalar_tensor_tensor(T2[:, cols], PS[:, 1, off:off + w], b2[:, bass.ds(2 * r + j, 1)], T1[:, cols],
                                               ALU.add, ALU.mult).then_inc(sem("ex_b"), 1)
                        dve.wait_ge(sem("ex_b"), nth("ex_b", g + 1))
                        V.tensor_tensor(T2[:, cols], T2[:, cols], combB[:, r, off:off + w], ALU.mult)\
                            .then_inc(sem("ex_val"), 1)
                        dve.wait_ge(sem("ex_val"), nth("ex_val", g + 1))
                        stage_lo("ex", r, 3, q, g, T2, cols, 128)
            enter(dve, "ex")
            for r in rounds(dve, TT // 2):
                for b in (0, 1):
                    dve.wait_ge(sem("w3_mm"), nth("w3_mm", 2 * r + b + 1))
                    for c in (0, 1):
                        cols = slice(512 * c, 512 * c + 512)
                        dve.wait_ge(sem(f"w3_in{c}"), nth(f"w3_in{c}", 32 * r + 16 * b + 16))
                        if begun(32 * r + 16 * b):
                            dve.wait_ge(sem(f"w3_st{c}"), nth(f"w3_st{c}", 32 * r + 16 * b))
                        V.tensor_tensor(T1[0:TP, cols], T2[0:TP, cols], PS[0:TP, b, cols], ALU.add).then_inc(sem("w3_v"), 1)
        print("semaphores", len(sems), "const end", cpos[0])


_CONST = ("cos", "sin", "ident", "sel")


def _shape_constants():
    inv = (1.0 / 10000.0 ** (np.arange(0, HD, 2, dtype=np.float32) / HD)).astype(np.float32)
    angle = inv[np.arange(128) % 32][:, None] * np.arange(N, dtype=np.float32)[None, :]
    sign = np.where(np.arange(128) % HD < 32, -1.0, 1.0)[:, None]
    sel = np.zeros((EXPERTS, EXPERTS * 128), np.float32)
    for e in range(EXPERTS):
        sel[e, e * 128:(e + 1) * 128] = 1.0
    return {"cos": np.cos(angle).astype(np.float32), "sin": (sign * np.sin(angle)).astype(np.float32),
            "ident": np.eye(128, dtype=np.float32), "sel": sel}


def kernel(x, src, dst, L0_gnn_W, L0_gnn_b, L0_mix_Wq, L0_mix_bq, L0_mix_Wk, L0_mix_bk, L0_mix_Wv, L0_mix_bv,
           L0_mix_Wo, L0_mix_bo, L0_ffn_norm1_w, L0_ffn_norm2_w, L0_ffn_qkv_w, L0_ffn_qkv_b, L0_ffn_out_w,
           L0_ffn_out_b, L0_ffn_gate_w, L0_ffn_w1, L0_ffn_b1, L0_ffn_w2, L0_ffn_b2, L0_ffn_w3, L0_ffn_b3):
    import concourse.bacc as _bacc
    from concourse.bass_utils import run_bass_kernel_spmd as _run

    def slabs(w):
        w = np.asarray(w)
        return w.reshape(-1, 128, KT, 128).transpose(0, 3, 2, 1)

    def cols(v):
        return np.asarray(v).reshape(-1, 128).T

    w12 = np.stack([np.asarray(L0_ffn_w1), np.asarray(L0_ffn_w2)], axis=1)
    w12 = w12.reshape(EXPERTS, 2, 2, 128, KT, 128).transpose(0, 2, 1, 5, 4, 3).reshape(4 * EXPERTS, 128, KT, 128)
    gate = np.tile(np.asarray(L0_ffn_gate_w).T, (1, 128 // EXPERTS))
    qkv_w, qkv_b = np.asarray(L0_ffn_qkv_w), np.asarray(L0_ffn_qkv_b)
    arrays = {
        "x": x, "src": src, "dst": dst,
        "Wq": slabs(L0_mix_Wq), "Wk": np.asarray(L0_mix_Wk).T, "Wg": np.asarray(L0_gnn_W).T, "Wv": slabs(L0_mix_Wv),
        "Wo": np.asarray(L0_mix_Wo).T, "Wqk": slabs(qkv_w[:2 * D]), "Wv2": qkv_w[2 * D:].T,
        "Wo2": np.asarray(L0_ffn_out_w).T, "gate": gate.reshape(KT, 128, 128).transpose(1, 0, 2), "W12": w12,
        "W3": np.asarray(L0_ffn_w3).transpose(0, 2, 1).reshape(EXPERTS * HID, D),
        "bq": cols(L0_mix_bq), "bv": cols(L0_mix_bv), "bqk": cols(qkv_b[:2 * D]), "b1": cols(np.asarray(L0_ffn_b1).ravel()),
        "b2": cols(np.asarray(L0_ffn_b2).ravel()), "n1": cols(L0_ffn_norm1_w), "n2": cols(L0_ffn_norm2_w),
        "bk": L0_mix_bk, "bg": L0_gnn_b, "bo": L0_mix_bo, "bv2": qkv_b[2 * D:], "ob": L0_ffn_out_b, "b3": L0_ffn_b3,
        **_shape_constants(),
    }
    nc = _bacc.Bacc("TRN2", target_bir_lowering=False, num_devices=1)
    io, feed = {}, {}
    for name, a in arrays.items():
        a = np.ascontiguousarray(a)
        feed["in_" + name] = a
        io[name] = nc.dram_tensor("in_" + name, a.shape, mybir.dt.from_np(a.dtype), kind="ExternalInput").ap()
    io["out"] = nc.dram_tensor("out_rows", (N, D), F32, kind="ExternalOutput").ap()
    build(nc, io)
    return _run(nc, [feed], core_ids=[0]).results[0]["out_rows"]
```

```python
import numpy as np
import concourse.bass as bass
from concourse import mybir
from contextlib import ExitStack

F32 = mybir.dt.float32
F32R = mybir.dt.float32r
F16 = mybir.dt.float16
I32 = mybir.dt.int32
ALU = mybir.AluOpType
ACT = mybir.ActivationFunctionType
AX = mybir.AxisListType

N = 1250
D = 1024
TT, TP = 10, 125
KT = D // 128
EDGES = 21250
EC = EDGES // TP
HEADS, HD = 16, 64
EXPERTS, HID = 8, 256
CH_N = [(0, 512), (512, 512), (1024, 226)]
CH_D = [(0, 512), (512, 512)]
GC = 4
GRANULE = GC * 128
GRANULES = (EDGES // GRANULE + TT + 1) // 2 * 2
SC = GRANULES * GC
LN_EPS, RMS_EPS = 1e-5, 1e-6


def build(nc, io):
    ctx = ExitStack()
    with ctx:
        sems = {}

        per_phase = {
            "mm": (("q", 8), ("k", 10), ("h", 10), ("m1", 8), ("m2", 8), ("m3", 8), ("mix", 10), ("gnn", 10), ("qk", 16),
                   ("v", 10), ("op", 10), ("gate", 1), ("ex", 32), ("w3", 10)),
            "lo": (("ln", 10), ("q", 24), ("k", 20), ("h", 20), ("m1", 16), ("m2", 16), ("m3", 16), ("qk", 48), ("v", 20),
                   ("ex", 48)),
            "val": (("q", 24), ("k", 20), ("h", 20), ("m2", 16), ("qk", 48), ("v", 20), ("ex", 48)),
            "psf": (("q", 24), ("k", 20), ("qk", 48)),
            "m": (("q", 24), ("k", 20)),
            "st0": (("q", 384), ("k", 320), ("h", 320), ("m2", 256), ("mix", 160), ("qk", 768), ("v", 320), ("att", 1280),
                    ("ex", 768), ("w3", 160)),
            "slab0": (("k", 160), ("h", 160), ("m1", 128), ("m3", 128), ("mix", 160), ("v", 160), ("op", 160), ("w3", 240)),
            "raw0": (("q", 64), ("m2", 64), ("qk", 128), ("gate", 16), ("ex", 256)),
            "raw1": (("q", 64), ("m2", 64), ("qk", 128), ("ex", 256)),
            "split": (("q", 8), ("m2", 8), ("qk", 16), ("gate", 1), ("ex", 32)),
            "rr0": (("k", 128), ("h", 128), ("m3", 128), ("v", 128), ("op", 128), ("w3", 256)),
            "res": (("k", 16), ("h", 16), ("m3", 16), ("v", 16), ("op", 16), ("w3", 32)),
            "v": (("mix", 20), ("w3", 20)),
            "in0": (("mix", 160), ("w3", 160)),
            "tr": (("ln", 10), ("gnn", 10), ("op", 10)),
            "sq": (("gnn", 10), ("op", 10)),
            "bn": (("ln", 20), ("gnn", 20)),
            "var": (("ln", 10), ("gnn", 10)),
        }
        for signal, like in (("hi", "lo"), ("e", "m"), ("st1", "st0"), ("slab1", "slab0"), ("sh", "split"), ("rr1", "rr0"),
                             ("rh", "res"), ("in1", "in0"), ("tv", "tr"), ("nb", "tr"), ("rt", "tr"), ("nh", "tr"), ("ms", "sq"),
                             ("rsd", "sq"), ("rmsr", "sq"), ("ag", "var"), ("sd", "var"), ("rc", "var")):
            per_phase[signal] = per_phase[like]

        def before(name):
            ph, _, signal = name.partition("_")
            count = 0
            for p, n in per_phase.get(signal, ()):
                if p == ph:
                    return signal, count
                count += n
            return name, 0

        def sem(name):
            name = before(name)[0]
            if name not in sems:
                sems[name] = ctx.enter_context(nc.semaphore(name))
            return sems[name]

        base = nc.sbuf_base + (-nc.sbuf_base) % 32
        A0 = base
        B0 = A0 + 80000
        L0 = B0 + 81920
        RAW0 = L0 + 20480
        W0 = RAW0 + 8192
        S0 = W0 + 16384
        C0 = S0 + 4096
        cpos = [C0]

        def at(name, shape, dt, off):
            return nc.alloc_sbuf_tensor_at(name, shape, dt, offset=off, align_bytes=16)

        def const(name, cols, dt=F32):
            t = at(name, [128, cols], dt, cpos[0])
            cpos[0] += (cols * 4 + 31) // 32 * 32
            return t

        def pair(name, cols, off):
            return at(name + "_hi", [128, cols], F32R, off), at(name + "_lo", [128, cols], F32R, off + 4 * cols)

        def scratch(name, rows, cols, dt=F32):
            return nc.dram_tensor(name, [rows, cols], dt, kind="Internal").ap()

        def scratch_pair(name, rows, cols):
            return scratch(name + "_hi", rows, cols), scratch(name + "_lo", rows, cols)

        PS = ctx.enter_context(nc.psum_tensor("products", [128, 2, 1536], F32))
        PX = ctx.enter_context(nc.psum_tensor("small_products", [128, 2, 512], F32))

        T1 = at("work1", [128, 1024], F32, W0)
        T2 = at("work2", [128, 1024], F32, W0 + 4096)
        HI = at("stage_hi", [128, 1024], F32R, W0 + 8192)
        LO = at("stage_lo", [128, 1024], F32R, W0 + 12288)
        RAW = at("raw_slab", [128, 2, 1024], F32, RAW0)
        RAWR = at("raw_resident", [128, 2, 512], F32, S0)
        L = [pair(f"slab{b}", 1280, L0 + 10240 * b) for b in range(2)]
        ident = const("ident", 128)
        bq = const("bq_col", KT)
        bv = const("bv_col", KT)
        bqk = const("bqk_col", 16)
        b1 = const("b1_col", 16)
        b2 = const("b2_col", 16)
        n1w = const("norm1_col", KT)
        n2w = const("norm2_col", KT)
        stat6 = const("stat6", 12)
        mv = const("mean_var", 2)
        rstd = const("rstd", 1)
        mean_all = const("x1_mean", TT)
        rstd_all = const("x1_rstd", TT)
        dis = const("deg_inv_sqrt", TT)
        zr = const("z_recip", 2)
        small = const("small", 8)
        ksT_hi = const("ksum_col_hi", 2 * KT, F32R)
        ksT_lo = const("ksum_col_lo", 2 * KT, F32R)
        ones2 = const("ones2", 2)
        assert cpos[0] <= 229344, cpos[0]

        xnT = pair("xnT", KT * N, A0)
        wk = pair("wk", KT * D, B0)
        wg = pair("wg", KT * D, A0)
        kres = pair("k_resident", TT * D, B0)
        m1T = pair("m1T", KT * D, A0)
        wo = pair("wo", KT * D, B0)
        m3 = pair("m3", KT * D, A0 + 0)
        ksb = at("ksum_bcast", [128, D], F32, A0 + 65536)
        counts = at("counts", [128, TT, N], F32, A0)
        hres = pair("h_resident", TT * D, B0)
        rT = pair("rT", KT * N, A0)
        wv2 = pair("wv2", KT * D, B0)
        wo2 = pair("wo2", KT * D, A0)
        zT = pair("zT", KT * N, B0)
        w3 = pair("w3", 2 * KT * D, A0)
        cosT = at("cos", [128, N], F32, B0 + 65536)
        sinT = at("sin", [128, N], F32, B0 + 65536 + 5024)
        bias_a = at("bias_rows_a", [128, D], F32, A0 + 65536 + 4096)
        bias_b = at("bias_rows_b", [128, D], F32, B0 + 65536 + 12288)

        T3 = at("work3", [128, 1024], F32, B0 + 65536 + 10048)
        ones_r = at("ones_r", [128, 128], F32R, A0 + 65536 + 8192)

        XN = scratch_pair("xn_rows", N, D)
        XNT = scratch_pair("xn_cols", D, N)
        QT = scratch_pair("q_cols", D, N)
        KR = scratch_pair("k_rows", N, D)
        HR = scratch_pair("h_rows", N, D)
        M2T = scratch_pair("m2_cols", D, D)
        ACC = scratch("acc_rows", N, D, F32)
        X1 = scratch("x1_rows", N, D, F32)
        RT = scratch_pair("r_cols", D, N)
        QK = scratch_pair("qk_cols", 2 * D, N)
        VR = scratch("v_rows", N, HEADS * 128)
        AT = scratch_pair("att_cols", D, N)
        XY = scratch("xy_rows", N, D, F32)
        CTS = scratch("comb_cols", EXPERTS, N, F32)
        G = scratch_pair("g_cols", 2 * D, N)
        SORTED = scratch("sorted_rows", 128 * SC, 2)

        V, S, P, SP, TE = nc.vector, nc.scalar, nc.gpsimd, nc.sync, nc.tensor

        def nth(name, count):
            return before(name)[1] + count

        def begun(count):
            return not isinstance(count, int) or count > 0

        def apart(eng):
            eng.sem_inc(sem("apart"), 1)

        def rounds(eng, n):
            yield 0
            with eng.Fori(1, n) as i:
                yield i

        def ring(eng, n):
            yield 0, True, False
            with eng.Fori(1, n - 1) as i:
                yield i, False, False
            yield n - 1, False, True

        def product(out, lhs, rhs, kts, kp, m, chunks, rw, lw=None, last=True):
            lw = lw or m
            first, ins = True, None
            for kt in range(kts):
                for l, rs in ((lhs[0], (rhs[0], rhs[1])), (lhs[1], (rhs[0],))):
                    for r in rs:
                        for off, n in chunks:
                            end = kt == kts - 1 and l is lhs[1] and last
                            ins = TE.matmul(out[0:m, off:off + n], l[0:kp, kt * lw:kt * lw + m],
                                            r[0:kp, kt * rw + off:kt * rw + off + n], start=first, stop=end)
                        first = False
            return ins

        ends = {}

        def enter(eng, ph):
            for name, value in ends[ph]:
                eng.wait_ge(sem(name), nth(name, value))

        def stage_ends(ph, n, per):
            return [(ph + "_mm", n), (ph + "_lo", n * per), (ph + "_st0", 32 * ((n * per + 1) // 2)),
                    (ph + "_st1", 32 * (n * per // 2))]

        ends["ln"] = [("ln_rt", TT), ("ln_st", 64 * TT)]
        ends["q"] = stage_ends("q", 8, 3)
        ends["k"] = stage_ends("k", 10, 2)
        ends["h"] = stage_ends("h", 10, 2)
        ends["m1"] = [("m1_mm", 8), ("m1_lo", 16)]
        ends["m2"] = stage_ends("m2", 8, 2)
        ends["m3"] = [("m3_mm", 8), ("m3_lo", 16), ("ks_col", 1)]
        ends["mix"] = [("mix_mm", 10), ("mix_v", 20), ("mix_st0", 160), ("mix_st1", 160)]
        ends["adj"] = [("adj_ev", GRANULES)]
        ends["deg"] = [("deg_scaled", 1)]
        ends["gnn"] = [("gnn_mm", 10), ("gnn_rt", 10), ("gnn_st", 16 * 30)]
        ends["qk"] = stage_ends("qk", 16, 3)
        ends["v"] = stage_ends("v", 10, 2)
        ends["att"] = [("att_pv", 80), ("att_olo", 80), ("att_st0", 32 * 40), ("att_st1", 32 * 40)]
        ends["op"] = [("op_mm", 10), ("op_rt", 10), ("op_st", 160)]
        ends["gate"] = [("gate_cb", 24), ("gate_st", 16)]
        ends["ex"] = [("ex_mm", 32), ("ex_lo", 48), ("ex_st0", 32 * 24), ("ex_st1", 32 * 24)]

        def copy_words(eng, out, in_):
            ap = [v.bitcast(F32) if v.dtype == F32R else v for v in (out, in_)]
            return eng.dma_start(ap[0], ap[1])

        def ln_store(sp, t):
            sp.wait_ge(sem("ln_lo"), nth("ln_lo", t + 1))
            for part, buf in ((0, HI), (1, LO)):
                copy_words(sp, XN[part][t * TP:(t + 1) * TP, :], buf[0:TP, :]).then_inc(sem("ln_st"), 16)
            sp.wait_ge(sem("ln_rt"), nth("ln_rt", t + 1))
            for part in (0, 1):
                copy_words(sp, XNT[part].rearrange("(k p) c -> p k c", p=128)[:, :, t * TP:(t + 1) * TP],
                             xnT[part][:, :].rearrange("p (k c) -> p k c", k=KT)[:, :, t * TP:(t + 1) * TP])\
                    .then_inc(sem("ln_st"), 16)

        def store_tile_pair(sp, dst, t, name):
            for part, buf in ((0, HI), (1, LO)):
                copy_words(sp, dst[part].rearrange("(k p) c -> p k c", p=128)[:, :, t * TP:(t + 1) * TP],
                             buf[:, 0:KT * TP].rearrange("p (k c) -> p k c", k=KT)).then_inc(sem(name), 16)

        def row_stream(sp, ph, load, rows_in, rows_out):
            def rows(s, b, c):
                if begun(2 * s + c - 1):
                    sp.wait_ge(sem(ph + "_v"), nth(ph + "_v", 2 * s + c - 1))
                copy_words(sp, T2[0:TP, 512 * c:512 * c + 512],
                             rows_in[bass.ds(s * TP, TP), 512 * c:512 * c + 512]).then_inc(sem(f"{ph}_in{c}"), 16)
                sp.wait_ge(sem(ph + "_v"), nth(ph + "_v", 2 * s + c + 1))
                copy_words(sp, rows_out[bass.ds(s * TP, TP), 512 * c:512 * c + 512],
                             T1[0:TP, 512 * c:512 * c + 512]).then_inc(sem(f"{ph}_st{c}"), 16)
            load(0, 0)
            load(1, 1)
            rows(0, 0, 0)
            rows(0, 0, 1)
            rows(1, 1, 0)
            rows(1, 1, 1)
            with sp.Fori(1, TT // 2) as i:
                for b in (0, 1):
                    if begun(2 * i + b - 1):
                        sp.wait_ge(sem(ph + "_mm"), nth(ph + "_mm", 2 * i + b - 1))
                    load(2 * i + b, b)
                for b in (0, 1):
                    for c in (0, 1):
                        rows(2 * i + b, b, c)

        EX1 = B0 + 65536
        nb = [at(f"norm{b}", [128, D], F32, EX1 + 4096 * b) for b in range(2)]
        tv = at("transposed", [128, KT * TP], F32, EX1 + 8192)
        EX2 = A0 + 50016 + (-(A0 + 50016)) % 32
        nb9 = [at(f"rnorm{b}", [128, D], F32, EX2 + 4096 * b) for b in range(2)]
        tv9 = at("rtransposed", [128, KT * TP], F32, EX2 + 8192)
        u9 = at("u_rows", [128, D], F32, EX2 + 12288)
        EX3 = A0 + 65536
        nb13 = [at("znorm", [128, D], F32, EX3)] * 2
        tv13 = at("ztransposed", [128, KT * TP], F32, EX3 + 4096)
        bias_a2 = at("bias_rows_a2", [128, D], F32, EX3 + 8192)
        SA = A0 + 65536 + 8192 + 512
        edge_row = at("edge_row", [128, EC], I32, SA)
        edge_pair = at("edge_pair", [128, EC, 2], F32, SA + 704)
        below = at("below", [128, 128], F32, SA + 704 + 1376)
        sorted_e = at("sorted_edges", [128, SC, 2], F32, SA + 2592)
        gran_at = at("granule_columns", [128, GRANULES], I32, SA + 2592 + 8 * SC)
        gran_no = at("granule_number", [128, GRANULES], F32, SA + 2592 + 8 * SC + 4 * GRANULES)
        SM = SA + 2592 + 8 * SC + 8 * GRANULES
        tile_n, gran_f, gran_sum, gran_start, tile_off = [at(f"tile_{k}", [128, TT], F32, SM + 48 * k) for k in range(5)]
        gran_i = at("tile_granules_i", [128, 2, TT], I32, SM + 240)
        assert SM + 320 <= A0 + 80000
        SX = B0 + 65536
        reached = at("reached", [128, TT + 1, EC], F16, SX)
        member = at("member", [128, TT, EC], F16, SX + 3744)
        rank = at("rank", [128, TT, EC], F16, SX)
        edge_src_i, edge_dst_i, edge_pos_i, edge_col_i, edge_part_i = \
            [at(f"edge_i{k}", [128, EC], I32, SX + 7168 + 704 * k) for k in range(5)]
        edge_dst = at("edge_dst", [128, EC], F32, SX + 7168 + 704 * 5)
        edge_tile = at("edge_tile", [128, EC], F32, SX + 7168 + 704 * 6)
        assert 7168 + 704 * 7 <= 12288
        place = at("place", [128, TT, EC], F32, W0)
        edge_pos, edge_col = [at(f"edge_f{k}", [128, EC], F32, W0 + 6816 + 704 * k) for k in range(2)]
        gran_ge = at("granule_reached", [128, TT - 1, GRANULES], F32, W0 + 8256)
        AD = A0 + 50016 + (-(A0 + 50016)) % 32
        iota = at("iota", [128, N], F16, AD)
        oh_src = at("onehot_src", [128, GC, N], F16, AD + 2528)
        oh_dst = at("onehot_dst", [128, GC, 128], F16, AD + 2528 + 2528 * GC)
        assert AD + 2528 * (GC + 1) + 256 * GC <= SA
        q_st = [at(f"q_stack{b}", [128, N], F32R, A0 + 5024 * b) for b in range(2)]
        k_st = [[at(f"k_stack{b}{p}", [128, N], F32R, A0 + 5024 * (2 + 2 * b + p)) for p in range(2)] for b in range(2)]
        v_st = [at(f"v_stack{b}", [128, TT * 128], F32R, A0 + 5024 * 6 + 5120 * b) for b in range(2)]
        A1 = A0 + 5024 * 6 + 10240
        prob = [at(f"prob{b}", [128, N], F32, A1 + 5024 * b) for b in range(4)]
        B1 = B0
        pT = [pair(f"pT{b}", TT * 250, B1 + 20000 * b) for b in range(2)]
        AC = B1 + 40000
        o_tmp = at("o_tmp", [128, 512], F32, AC)
        o_sum = at("o_sum", [128, 512], F32, AC + 2048)
        o_hi = at("o_hi", [128, 512], F32R, AC + 4096)
        o_lo = at("o_lo", [128, 512], F32R, AC + 6144)
        mx = at("att_max", [128, 2], F32, AC + 8192)
        nmx = at("att_negmax", [128, 2], F32, AC + 8224)
        rs = at("att_sum", [128, 2], F32, AC + 8256)
        rr = at("att_rsum", [128, 2], F32, AC + 8288)
        combB = at("comb_bcast", [128, EXPERTS, N], F32, A0)
        combT = at("combT", [128, N], F32, A0 + 40032)
        logT = at("logitsT", [128, N], F32, A0 + 45056)
        lg = at("logits", [128, 8], F32, A0 + 50112)
        m8 = at("top8", [128, 8], F32, A0 + 50144)
        top_i = at("top_index", [128, 8], mybir.dt.uint32, A0 + 50176)
        top_f = at("top_index_f", [128, 8], F32, A0 + 50208)
        eight = at("expert_number", [128, 8], F32, A0 + 54608)
        mask = at("mask", [128, 8], F32, A0 + 50240)
        ex8 = at("exp8", [128, 8], F32, A0 + 50272)
        nm1 = at("neg_top", [128, 8], F32, A0 + 50304)
        sel = at("select", [128, EXPERTS * 128], F32, A0 + 50336)
        comb = at("comb", [128, 8], F32, A0 + 50336 + 4096)
        LG = [pair(f"gslab{b}", 16 * TP, A0 + 131072 + 16000 * b) for b in range(2)]
        ct_tile = [at(f"ct_tile{b}", [128, 128], F32, A0 + 131072 + 32000 + 512 * b) for b in range(2)]
        b3r = at("b3_rows", [128, D], F32, A0 + 131072 + 33024)
        assert A0 + 131072 + 33024 + 4096 <= RAW0

        NT = 2 * TT
        GROUPS = {"c": (8, 10), "b": (4, 8), "a": (0, 4)}

        def group_bank(g, b, k):
            if g == "c":
                return PS[0:TP, b, 1250 + k * TP:1250 + k * TP + TP]
            return PX[0:TP, "ab".index(g), k * TP:k * TP + TP]

        def group_read(g, b):
            k0, k1 = GROUPS[g]
            v = PS[0:TP, b, 1250:1500] if g == "c" else PX[0:TP, "ab".index(g), 0:4 * TP]
            return v.rearrange("p (k c) -> p k c", k=k1 - k0)

        def pT_part(pb, part, g, j):
            k0, k1 = GROUPS[g]
            return pT[pb][part][0:TP, :].rearrange("p (k c) -> p k c", k=TT)[:, k0:k1, (j % 2) * TP:(j % 2) * TP + TP]

        block = ctx.enter_context(nc.Block())

        @block.sync
        def _(sp):
            def load_slab_raw(ph, src, s, b, idx):
                copy_words(sp, RAW[:, b, :], src[s].rearrange("p k m -> p (k m)")).then_inc(sem(f"{ph}_raw{b}"), 16)

            def load_slab(ph, src, s, b, kts, kp, m, rows_are_k):
                for part in (0, 1):
                    v = src[part].rearrange("(k p) c -> p k c", p=kp)[:, :, bass.ds(s * m, m)]
                    copy_words(sp, L[b][part][0:kp, 0:kts * m].rearrange("p (k c) -> p k c", k=kts), v)\
                        .then_inc(sem(f"{ph}_slab{b}"), 16)

            def stream(ph, n, load, store, chunks, used="_mm"):
                load(0, 0)
                load(1, 1)
                per = len(chunks)

                def store_slab(s, b):
                    for c in range(per):
                        q = per * b + c
                        sp.wait_ge(sem(ph + "_lo"), nth(ph + "_lo", s * per + c + 1))
                        store(s, c, q % 2)

                with sp.Fori(0, n // 2 - 1) as i:
                    for b in (0, 1):
                        sp.wait_ge(sem(ph + used), nth(ph + used, 2 * i + b + 1))
                        load(2 * i + b + 2, b)
                        if store:
                            store_slab(2 * i + b, b)
                if store:
                    for b in (0, 1):
                        store_slab(n - 2 + b, b)

            def store_pair(ph, dst, rows, chunks, p):
                def go(s, c, h):
                    off, n = chunks[c]
                    for part, buf in ((0, HI), (1, LO)):
                        copy_words(sp, dst[part][bass.ds(s * rows, rows), off:off + n],
                                     buf[0:rows, 512 * h:512 * h + n]).then_inc(sem(f"{ph}_st{h}"), 16)
                return go

            for t, k in ((bq, "bq"), (bv, "bv"), (bqk, "bqk"), (b1, "b1"), (b2, "b2"), (n1w, "n1"), (n2w, "n2"),
                         (ident, "ident")):
                copy_words(sp, t[:, :], io[k]).then_inc(sem("consts"), 16)
            for t in range(TT):
                b = t % 2
                if t >= 2:
                    if begun(t - 1):
                        sp.wait_ge(sem("ln_nb"), nth("ln_nb", t - 1))
                copy_words(sp, [T1, T2][b][0:TP, :], io["x"][t * TP:(t + 1) * TP, :]).then_inc(sem(f"ln_x{b}"), 16)
                if t >= 1:
                    ln_store(sp, t - 1)
            ln_store(sp, TT - 1)
            enter(sp, "ln")
            copy_words(sp, bias_b[0:TP, :], io["bk"].partition_broadcast(TP)).then_inc(sem("k_bias"), 16)
            stream("q", 8, lambda s, b: load_slab_raw("q", io["Wq"], s, b, 0),
                   store_pair("q", QT, 128, CH_N, 128), CH_N, "_split")
            enter(sp, "q")
            for k, t in (("src", edge_src_i), ("dst", edge_dst_i)):
                copy_words(sp, t[0:TP, :], io[k].rearrange("(p c) -> p c", p=TP)).then_inc(sem("edges"), 16)
            copy_words(sp, below[:, :], io["below"]).then_inc(sem("edges"), 16)
            copy_words(sp, bias_a[0:TP, :], io["bg"].partition_broadcast(TP)).then_inc(sem("g_bias"), 16)
            stream("k", 10, lambda s, b: load_slab("k", XNT, s, b, KT, 128, TP, 0),
                   store_pair("k", KR, TP, CH_D, TP), CH_D)
            enter(sp, "k")
            sp.wait_ge(sem("sort_ready"), nth("sort_ready", 1))
            copy_words(sp, SORTED.rearrange("(p c) e -> p (c e)", p=128), sorted_e[:, :, :].rearrange("p c e -> p (c e)"))\
                .then_inc(sem("sorted_blank"), 16)
            for part in (0, 1):
                copy_words(sp, kres[part][0:TP, :].rearrange("p (k c) -> p k c", k=TT),
                             KR[part].rearrange("(k p) c -> p k c", p=TP)).then_inc(sem("m1_full"), 16)
            stream("h", 10, lambda s, b: load_slab("h", XNT, s, b, KT, 128, TP, 0),
                   store_pair("h", HR, TP, CH_D, TP), CH_D)
            enter(sp, "h")
            stream("m1", 8, lambda s, b: load_slab("m1", XN, s, b, TT, TP, 128, 0), None, CH_D)
            enter(sp, "m1")
            stream("m2", 8, lambda s, b: load_slab_raw("m2", io["Wv"], s, b, 0),
                   store_pair("m2", M2T, 128, CH_D, 128), CH_D, "_split")
            enter(sp, "m2")
            stream("m3", 8, lambda s, b: load_slab("m3", M2T, s, b, KT, 128, 128, 0), None, CH_D)
            enter(sp, "m3")
            sp.wait_ge(sem("scattered"), nth("scattered", 16 * EC))
            copy_words(sp, sorted_e[:, :, :].rearrange("p c e -> p (c e)"), SORTED.rearrange("(p c) e -> p (c e)", p=128))\
                .then_inc(sem("sorted_in"), 16)
            copy_words(sp, bias_a[0:TP, :], io["bo"].partition_broadcast(TP)).then_inc(sem("o_bias"), 16)
            for part in (0, 1):
                copy_words(sp, hres[part][0:TP, :].rearrange("p (k c) -> p k c", k=TT),
                             HR[part].rearrange("(k p) c -> p k c", p=TP)).then_inc(sem("gnn_full"), 16)
            row_stream(sp, "mix", lambda s, b: load_slab("mix", QT, s, b, KT, 128, TP, 0), io["x"], ACC)
            enter(sp, "deg")
            for t in range(TT):
                b = t % 2
                if t >= 1:
                    if begun(t):
                        sp.wait_ge(sem("gnn_x1"), nth("gnn_x1", t))
                copy_words(sp, T2[0:TP, :], ACC[t * TP:(t + 1) * TP, :]).then_inc(sem("gnn_acc"), 16)
                sp.wait_ge(sem("gnn_x1"), nth("gnn_x1", t + 1))
                copy_words(sp, X1[t * TP:(t + 1) * TP, :], T1[0:TP, :]).then_inc(sem("gnn_st"), 16)
                sp.wait_ge(sem("gnn_rt"), nth("gnn_rt", t + 1))
                store_tile_pair(sp, RT, t, "gnn_st")
            enter(sp, "gnn")
            for t, k in ((cosT, "cos"), (sinT, "sin")):
                copy_words(sp, t[:, :], io[k]).then_inc(sem("rope_tables"), 16)
            for part in (0, 1):
                copy_words(sp, rT[part][:, :].rearrange("p (k c) -> p k c", k=KT),
                             RT[part].rearrange("(k p) c -> p k c", p=128)).then_inc(sem("qk_full"), 16)
            stream("qk", 16, lambda s, b: load_slab_raw("qk", io["Wqk"], s, b, 0),
                   store_pair("qk", QK, 128, CH_N, 128), CH_N, "_split")
            enter(sp, "qk")
            copy_words(sp, bias_a[0:TP, :], io["bv2"].partition_broadcast(TP)).then_inc(sem("v2_bias"), 16)

            def store_v(s, c, h):
                for part, buf in ((0, HI), (1, LO)):
                    dst = VR.rearrange("t (h e d) -> t h e d", h=HEADS, e=2)[bass.ds(s * TP, TP), 8 * c:8 * c + 8, part, :]
                    copy_words(sp, dst, buf[0:TP, 512 * h:512 * h + 512].rearrange("t (h d) -> t h d", h=8))\
                        .then_inc(sem(f"v_st{h}"), 16)
            stream("v", 10, lambda s, b: load_slab("v", RT, s, b, KT, 128, TP, 0), store_v, CH_D)
            enter(sp, "v")

            def load_head(h, b):
                for part in (0, 1):
                    half = slice(64 * part, 64 * part + 64)
                    copy_words(sp, q_st[b][half, :], QK[part][bass.ds(h * HD, HD), :]).then_inc(sem(f"head{b}"), 16)
                    for dup in (0, 1):
                        copy_words(sp, k_st[b][part][64 * dup:64 * dup + 64, :],
                                     QK[part][bass.ds(h * HD + D, HD), :]).then_inc(sem(f"head{b}"), 16)
                copy_words(sp, v_st[b][0:TP, :].rearrange("p (k c) -> p k c", k=TT),
                             VR.rearrange("(k p) c -> p k c", p=TP)[:, :, bass.ds(h * 128, 128)])\
                    .then_inc(sem(f"head{b}"), 16)

            def store_out(h, hb, g):
                pb = (hb * 5 + g) % 2
                sp.wait_ge(sem("att_olo"), nth("att_olo", h * 5 + g + 1))
                for part, buf in ((0, o_hi), (1, o_lo)):
                    copy_words(sp, AT[part][bass.ds(h * HD, HD), 250 * g:250 * g + 250],
                                 buf[0:64, 250 * pb:250 * pb + 250]).then_inc(sem(f"att_st{pb}"), 16)
            load_head(0, 0)
            load_head(1, 1)
            with sp.Fori(0, HEADS // 2 - 1) as i:
                for b in (0, 1):
                    for g in range(5):
                        store_out(2 * i + b, b, g)
                    sp.wait_ge(sem("att_pv"), nth("att_pv", (2 * i + b + 1) * 5))
                    load_head(2 * i + b + 2, b)
            for b in (0, 1):
                for g in range(5):
                    store_out(HEADS - 2 + b, b, g)
            enter(sp, "att")
            copy_words(sp, bias_a2[0:TP, :], io["ob"].partition_broadcast(TP)).then_inc(sem("ob_bias"), 16)
            load_slab("op", AT, 0, 0, KT, 128, TP, 0)
            for t in range(TT):
                if t + 1 < TT:
                    if t >= 1:
                        if begun(t):
                            sp.wait_ge(sem("op_mm"), nth("op_mm", t))
                    load_slab("op", AT, t + 1, (t + 1) % 2, KT, 128, TP, 0)
                if t >= 1:
                    if begun(t):
                        sp.wait_ge(sem("op_xy"), nth("op_xy", t))
                copy_words(sp, T2[0:TP, :], X1[t * TP:(t + 1) * TP, :]).then_inc(sem("op_x1"), 16)
                sp.wait_ge(sem("op_xy"), nth("op_xy", t + 1))
                copy_words(sp, XY[t * TP:(t + 1) * TP, :], T2[0:TP, :]).then_inc(sem("op_st"), 16)
                sp.wait_ge(sem("op_st"), nth("op_st", 16 * (t + 1)))
            enter(sp, "op")
            copy_words(sp, RAW[:, 0, :], io["gate"].rearrange("p k m -> p (k m)")).then_inc(sem("gate_raw0"), 16)
            copy_words(sp, sel[0:EXPERTS, :], io["sel"]).then_inc(sem("gate_sel"), 16)
            sp.wait_ge(sem("gate_ct"), nth("gate_ct", TT))
            copy_words(sp, CTS, combT[0:EXPERTS, :]).then_inc(sem("gate_st"), 16)
            enter(sp, "gate")

            def store_g(r, c, h):
                off, n = CH_N[c]
                for part, buf in ((0, HI), (1, LO)):
                    copy_words(sp, G[part][bass.ds(r * 128, 128), off:off + n],
                                 buf[:, 512 * h:512 * h + n]).then_inc(sem(f"ex_st{h}"), 16)

            def store_expert(e):
                for j in range(2):
                    for c in range(3):
                        sp.wait_ge(sem("ex_lo"), nth("ex_lo", e * 6 + 3 * j + c + 1))
                        store_g(2 * e + j, c, (3 * j + c) % 2)
            load_slab_raw("ex", io["W12"], 0, 0, 0)
            load_slab_raw("ex", io["W12"], 1, 1, 0)
            with sp.Fori(0, EXPERTS - 1) as e:
                for j in range(2):
                    for b in (0, 1):
                        sp.wait_ge(sem("ex_split"), nth("ex_split", e * 4 + 2 * j + b + 1))
                        load_slab_raw("ex", io["W12"], e * 4 + 2 * j + b + 2, b, 0)
                    for c in range(3):
                        sp.wait_ge(sem("ex_lo"), nth("ex_lo", e * 6 + 3 * j + c + 1))
                        store_g(2 * e + j, c, (3 * j + c) % 2)
            for b in (0, 1):
                sp.wait_ge(sem("ex_split"), nth("ex_split", 4 * EXPERTS - 4 + b + 1))
                load_slab_raw("ex", io["W12"], 4 * EXPERTS - 4 + b + 2, b, 0)
            store_expert(EXPERTS - 1)
            enter(sp, "ex")

            def load_g(s, b):
                for part in (0, 1):
                    copy_words(sp, LG[b][part][:, :].rearrange("p (k c) -> p k c", k=16),
                                 G[part].rearrange("(k p) c -> p k c", p=128)[:, :, bass.ds(s * TP, TP)])\
                        .then_inc(sem(f"w3_slab{b}"), 16)
                copy_words(sp, ct_tile[b][0:EXPERTS, 0:TP], CTS[:, bass.ds(s * TP, TP)]).then_inc(sem(f"w3_slab{b}"), 16)
            row_stream(sp, "w3", load_g, XY, io["out"])
            sp.wait_ge(sem("w3_st0"), nth("w3_st0", 160))
            sp.wait_ge(sem("w3_st1"), nth("w3_st1", 160))

        @block.gpsimd
        def _(pool):
            def split_resident(ph, src, dst, pieces, first=0):
                def fetch(j, b):
                    pool.dma_start(RAWR[:, b, :], src[j // 2 * 128:(j // 2 + 1) * 128, 512 * (j % 2):512 * (j % 2) + 512])\
                        .then_inc(sem(f"{ph}_rr{b}"), 16)
                n = 2 * pieces
                fetch(0, 0)
                fetch(1, 1)
                for j in range(n):
                    b = j % 2
                    pool.wait_ge(sem(f"{ph}_rr{b}"), nth(f"{ph}_rr{b}", 16 * (j // 2 + 1)))
                    P.tensor_copy(dst[0][:, 512 * j:512 * j + 512], RAWR[:, b, :]).then_inc(sem(ph + "_rh"), 1)
                    pool.wait_ge(sem(ph + "_rh"), nth(ph + "_rh", j + 1))
                    P.tensor_tensor(dst[1][:, 512 * j:512 * j + 512], RAWR[:, b, :],
                                    dst[0][:, 512 * j:512 * j + 512].bitcast(F32), ALU.subtract)\
                        .then_inc(sem(ph + "_res"), 1)
                    if j + 2 < n:
                        pool.wait_ge(sem(ph + "_res"), nth(ph + "_res", j + 1))
                        fetch(j + 2, b)

            def split_slabs(ph, n):
                for r in rounds(pool, n // 2):
                    for b in (0, 1):
                        pool.wait_ge(sem(f"{ph}_raw{b}"), nth(f"{ph}_raw{b}", 16 * r + 16))
                        if begun(2 * r + b - 1):
                            pool.wait_ge(sem(ph + "_mm"), nth(ph + "_mm", 2 * r + b - 1))
                        apart(pool)
                        P.tensor_copy(L[b][0][:, 0:1024], RAW[:, b, :]).then_inc(sem(ph + "_sh"), 1)
                        pool.wait_ge(sem(ph + "_sh"), nth(ph + "_sh", 2 * r + b + 1))
                        P.tensor_tensor(L[b][1][:, 0:1024], RAW[:, b, :], L[b][0][:, 0:1024].bitcast(F32),
                                        ALU.subtract).then_inc(sem(ph + "_split"), 1)

            split_resident("k", io["Wk"], wk, 8)
            enter(pool, "ln")
            split_slabs("q", 8)
            enter(pool, "q")
            P.iota(gran_no[:, :], [[1, GRANULES]], base=0, channel_multiplier=0, allow_small_or_imprecise_dtypes=True)\
                .then_inc(sem("gran_iota"), 1)
            split_resident("h", io["Wg"], wg, 8)
            pool.wait_ge(sem("sort_ready"), nth("sort_ready", 1))
            pool.wait_ge(sem("sorted_blank"), nth("sorted_blank", 16))
            for c in range(EC):
                pool.indirect_dma_start(SORTED, bass.IndirectOffsetOnAxis(ap=edge_row[0:TP, c:c + 1], axis=0),
                                        edge_pair[0:TP, c, :], None).then_inc(sem("scattered"), 16)
            enter(pool, "m1")
            split_slabs("m2", 8)
            split_resident("m3", io["Wo"], wo, 8)
            enter(pool, "mix")
            P.iota(iota[:, :], [[1, N]], base=0, channel_multiplier=0, allow_small_or_imprecise_dtypes=True)\
                .then_inc(sem("iota"), 1)
            P.memset(counts[:, TT // 2:, :], 0.0).then_inc(sem("counts_zero"), 1)
            enter(pool, "gnn")
            split_slabs("qk", 16)
            enter(pool, "qk")
            split_resident("v", io["Wv2"], wv2, 8)
            enter(pool, "v")
            for r in rounds(pool, HEADS // 2):
                for j in range(2 * TT):
                    b = j % 2
                    t = r * (2 * TT) + j
                    pool.wait_ge(sem("att_rr"), nth("att_rr", t + 1))
                    apart(pool)
                    P.tensor_scalar(prob[j % 4][0:TP, :], prob[j % 4][0:TP, :], rr[0:TP, b:b + 1], 1.0, ALU.mult, ALU.mult)\
                        .then_inc(sem("att_norm"), 1)
            enter(pool, "att")
            split_resident("op", io["Wo2"], wo2, 8)
            enter(pool, "op")
            P.iota(eight[:, :], [[1, 8]], base=0, channel_multiplier=0, allow_small_or_imprecise_dtypes=True)\
                .then_inc(sem("gate_iota"), 1)
            pool.wait_ge(sem("gate_raw0"), nth("gate_raw0", 16))
            P.tensor_copy(L[0][0][:, 0:1024], RAW[:, 0, :]).then_inc(sem("gate_sh"), 1)
            pool.wait_ge(sem("gate_sh"), nth("gate_sh", 1))
            P.tensor_tensor(L[0][1][:, 0:1024], RAW[:, 0, :], L[0][0][:, 0:1024].bitcast(F32),
                            ALU.subtract).then_inc(sem("gate_split"), 1)
            enter(pool, "gate")
            for r in rounds(pool, EXPERTS):
                for j in range(2):
                    for b in (0, 1):
                        pool.wait_ge(sem(f"ex_raw{b}"), nth(f"ex_raw{b}", 32 * r + 16 * j + 16))
                        if begun(4 * r + 2 * j + b - 1):
                            pool.wait_ge(sem("ex_mm"), nth("ex_mm", 4 * r + 2 * j + b - 1))
                        apart(pool)
                        P.tensor_copy(L[b][0][:, 0:1024], RAW[:, b, :]).then_inc(sem("ex_sh"), 1)
                        pool.wait_ge(sem("ex_sh"), nth("ex_sh", 4 * r + 2 * j + b + 1))
                        P.tensor_tensor(L[b][1][:, 0:1024], RAW[:, b, :], L[b][0][:, 0:1024].bitcast(F32),
                                        ALU.subtract).then_inc(sem("ex_split"), 1)
            enter(pool, "ex")
            pool.dma_start(b3r[0:EXPERTS, :], io["b3"]).then_inc(sem("b3_in"), 16)
            split_resident("w3", io["W3"], w3, 16)

        @block.tensor
        def _(pe):
            def slabs(ph, n, slab_unit, kts, kp, m, rhs, rw, chunks, per_ev, ev, split):
                for r in rounds(pe, n // 2):
                    for b in (0, 1):
                        if split:
                            pe.wait_ge(sem(ph + "_split"), nth(ph + "_split", 2 * r + b + 1))
                        else:
                            pe.wait_ge(sem(f"{ph}_slab{b}"), nth(f"{ph}_slab{b}", slab_unit * r + slab_unit))
                        if begun(per_ev * (2 * r + b - 1)):
                            pe.wait_ge(sem(ph + ev), nth(ph + ev, per_ev * (2 * r + b - 1)))
                        ins = product(PS[:, b, :], L[b], rhs, kts, kp, m, chunks, rw)
                        ins.then_inc(sem(ph + "_mm"), 1)

            pe.wait_ge(sem("consts"), nth("consts", 16 * 8))

            def transposes(ph, src, t):
                pe.wait_ge(sem(ph + "_nb"), nth(ph + "_nb", t + 1))
                if begun(t):
                    pe.wait_ge(sem(ph + "_tv"), nth(ph + "_tv", t))
                for f in range(KT):
                    ins = TE.transpose(PX[:, f // 4, (f % 4) * TP:(f % 4) * TP + TP],
                                       src[0:TP, f * 128:f * 128 + 128], ident[0:TP, 0:TP])
                ins.then_inc(sem(ph + "_tr"), 1)
            for t in range(TT):
                transposes("ln", nb[t % 2], t)
            enter(pe, "ln")
            slabs("q", 8, 0, KT, 128, 128, xnT, N, CH_N, 3, "_psf", True)
            enter(pe, "q")
            pe.wait_ge(sem("edges"), nth("edges", 48))
            pe.wait_ge(sem("sort_tile_n"), nth("sort_tile_n", 1))
            TE.matmul(PX[0:TP, 0, 0:TT], below[0:TP, 0:TP], tile_n[0:TP, :], start=True, stop=True)
            TE.matmul(PX[0:TP, 1, 0:TT], ones_r[0:TP, 0:TP].bitcast(F32), tile_n[0:TP, :], start=True, stop=True)\
                .then_inc(sem("sort_sums"), 1)
            pe.wait_ge(sem("k_res"), nth("k_res", 16))
            slabs("k", 10, 32, KT, 128, TP, wk, D, CH_D, 2, "_psf", False)
            enter(pe, "k")
            pe.wait_ge(sem("h_res"), nth("h_res", 16))
            slabs("h", 10, 32, KT, 128, TP, wg, D, CH_D, 2, "_val", False)
            enter(pe, "h")
            pe.wait_ge(sem("m1_full"), nth("m1_full", 32))
            pe.wait_ge(sem("ones_ready"), nth("ones_ready", 1))
            for off, n in CH_D:
                for kt in range(TT):
                    for part in (0, 1):
                        ins = TE.matmul(PS[:, 0, off:off + n], ones_r[0:TP, :], kres[part][0:TP, kt * D + off:kt * D + off + n],
                                        start=kt == 0 and part == 0, stop=kt == TT - 1 and part == 1)
            ins.then_inc(sem("ks_mm"), 1)
            pe.wait_ge(sem("ks_v"), nth("ks_v", 1))
            slabs("m1", 8, 32, TT, TP, 128, kres, D, CH_D, 2, "_lo", False)
            enter(pe, "m1")
            slabs("m2", 8, 0, KT, 128, 128, m1T, D, CH_D, 2, "_val", True)
            enter(pe, "m2")
            for f in range(KT):
                ins = TE.transpose(PX[:, f // 4, (f % 4) * 128:(f % 4) * 128 + 128], ksb[:, f * 128:f * 128 + 128],
                                   ident[:, :])
            ins.then_inc(sem("ks_tr"), 1)
            pe.wait_ge(sem("m3_res"), nth("m3_res", 16))
            slabs("m3", 8, 32, KT, 128, 128, wo, D, CH_D, 2, "_lo", False)
            enter(pe, "m3")
            for r in rounds(pe, TT // 2):
                for b in (0, 1):
                    pe.wait_ge(sem(f"mix_slab{b}"), nth(f"mix_slab{b}", 32 * r + 32))
                    if begun(2 * (2 * r + b - 1)):
                        pe.wait_ge(sem("mix_v"), nth("mix_v", 2 * (2 * r + b - 1)))
                    for kt in range(KT):
                        for n3, (l, rk) in enumerate(((0, ksT_hi), (0, ksT_lo), (1, ksT_hi))):
                            TE.matmul(PS[0:TP, b, 1024:1026], L[b][l][:, kt * TP:kt * TP + TP], rk[:, 2 * kt:2 * kt + 2],
                                      start=kt == 0 and n3 == 0, stop=kt == KT - 1 and n3 == 2)
                    product(PS[:, b, :], L[b], m3, KT, 128, TP, CH_D, D).then_inc(sem("mix_mm"), 1)
            enter(pe, "mix")
            for r in rounds(pe, GRANULES // 2):
                for b in (0, 1):
                    if begun(2 * r + b - 1):
                        pe.wait_ge(sem("adj_ev"), nth("adj_ev", 2 * r + b - 1))
                    for k in range(GC):
                        pe.wait_ge(sem("oh_ready"), nth("oh_ready", GC * (2 * r + b) + (k + 1)))
                        for off, n in CH_N:
                            ins = TE.matmul(PS[0:TP, b, off:off + n], oh_dst[:, k, 0:TP], oh_src[:, k, off:off + n],
                                            start=k == 0, stop=k == GC - 1)
                        ins.then_inc(sem("oh_used"), 1)
            enter(pe, "adj")
            pe.wait_ge(sem("loops_in"), nth("loops_in", 1))
            for i in range(TT):
                for j in range(TT):
                    ins = TE.matmul(PX[0:TP, 0, 2 * i:2 * i + 2], counts[0:TP, j, i * TP:i * TP + TP],
                                    ones2[0:TP, :], start=j == 0, stop=j == TT - 1)
            ins.then_inc(sem("deg_mm"), 1)
            enter(pe, "deg")
            pe.wait_ge(sem("gnn_full"), nth("gnn_full", 32))
            for t in range(TT + 1):
                if t < TT:
                    b = t % 2
                    pe.wait_ge(sem("gnn_slab"), nth("gnn_slab", t + 1))
                    if begun(t - 1):
                        pe.wait_ge(sem("gnn_x1"), nth("gnn_x1", t - 1))
                    product(PS[:, b, :], L[b], hres, TT, TP, TP, CH_D, D).then_inc(sem("gnn_mm"), 1)
                if t >= 1:
                    transposes("gnn", nb9[(t - 1) % 2], t - 1)
            enter(pe, "gnn")
            pe.wait_ge(sem("qk_full"), nth("qk_full", 32))
            slabs("qk", 16, 0, KT, 128, 128, rT, N, CH_N, 3, "_psf", True)
            enter(pe, "qk")
            pe.wait_ge(sem("v_res"), nth("v_res", 16))
            slabs("v", 10, 32, KT, 128, TP, wv2, D, CH_D, 2, "_val", False)
            enter(pe, "v")

            def scores(r, j):
                n, b, hb = r * NT + j, j % 2, j // TT % 2
                if j % TT == 0:
                    if begun(112 * r + 112 * (j // NT + 1)):
                        pe.wait_ge(sem(f"head{hb}"), nth(f"head{hb}", 112 * r + 112 * (j // NT + 1)))
                if begun(n - 1):
                    pe.wait_ge(sem("att_exp"), nth("att_exp", n - 1))
                if begun(n - 1):
                    pe.wait_ge(sem("att_loc"), nth("att_loc", n - 1))
                for part in (0, 1):
                    for off, w in CH_N:
                        ins = TE.matmul(PS[0:TP, b, off:off + w], q_st[hb][:, j % TT * TP:j % TT * TP + TP],
                                        k_st[hb][part][:, off:off + w], start=part == 0, stop=part == 1)
                ins.then_inc(sem("att_sc"), 1)

            def transpose_probs(r, j, g):
                n, b = r * NT + j, j % 2
                k0, k1 = GROUPS[g]
                pe.wait_ge(sem("att_norm"), nth("att_norm", n + 1))
                if begun(n):
                    pe.wait_ge(sem("att_lo" + g), nth("att_lo" + g, n))
                if g == "a":
                    if begun(r * TT + j // 2):
                        pe.wait_ge(sem("att_osum"), nth("att_osum", r * TT + j // 2))
                for k in range(k0, k1):
                    ins = TE.transpose(group_bank(g, b, k - k0), prob[j % 4][0:TP, k * TP:k * TP + TP], ident[0:TP, 0:TP])
                ins.then_inc(sem("att_tr" + g), 1)

            def values(r, j):
                n, hb, pb = r * NT + j, j // TT % 2, j // 2 % 2
                for g in GROUPS:
                    pe.wait_ge(sem("att_lo" + g), nth("att_lo" + g, n + 1))
                for k in range(TT):
                    for part in (0, 1):
                        ins = TE.matmul(PX[:, 0, 0:250], v_st[hb][0:TP, k * 128:k * 128 + 128],
                                        pT[pb][part][0:TP, k * 250:k * 250 + 250],
                                        start=k == 0 and part == 0, stop=k == TT - 1 and part == 1)
                ins.then_inc(sem("att_pv"), 1)
            scores(0, 0)
            for r, first, last in ring(pe, HEADS // 2):
                for j in range(NT):
                    if not (first and j < 1):
                        transpose_probs(r, j - 1, "c")
                    if j % 2 == 1 and not (first and j < 2):
                        transpose_probs(r, j - 2, "a")
                    if not (first and j < 1):
                        transpose_probs(r, j - 1, "b")
                    if not (last and j == NT - 1):
                        scores(r, j + 1)
                    if j % 2 == 1 and not (first and j < 3):
                        values(r, j - 2)
                    if j % 2 == 0 and not (first and j < 2):
                        transpose_probs(r, j - 2, "a")
            end = HEADS // 2 - 1
            transpose_probs(end, NT - 1, "c")
            transpose_probs(end, NT - 1, "b")
            transpose_probs(end, NT - 2, "a")
            transpose_probs(end, NT - 1, "a")
            values(end, NT - 1)
            enter(pe, "att")
            pe.wait_ge(sem("op_res"), nth("op_res", 16))
            for t in range(TT + 1):
                if t < TT:
                    b = t % 2
                    pe.wait_ge(sem(f"op_slab{b}"), nth(f"op_slab{b}", 32 * (t // 2 + 1)))
                    if begun(t - 1):
                        pe.wait_ge(sem("op_y"), nth("op_y", t - 1))
                    product(PS[:, b, :], L[b], wo2, KT, 128, TP, CH_D, D).then_inc(sem("op_mm"), 1)
                if t >= 1:
                    transposes("op", nb13[0], t - 1)
            enter(pe, "op")
            pe.wait_ge(sem("gate_split"), nth("gate_split", 1))
            product(PS[:, 0, :], L[0], zT, KT, 128, 128, CH_N, N).then_inc(sem("gate_mm"), 1)
            for t in range(TT):
                pe.wait_ge(sem("gate_log"), nth("gate_log", 1))
                if begun(t):
                    pe.wait_ge(sem("gate_lg"), nth("gate_lg", t))
                TE.transpose(PX[0:TP, 0, 0:8], logT[0:8, t * TP:t * TP + TP], ident[0:8, 0:8]).then_inc(sem("gate_tr"), 1)
                pe.wait_ge(sem("gate_comb"), nth("gate_comb", t + 1))
                if begun(t):
                    pe.wait_ge(sem("gate_ct"), nth("gate_ct", t))
                TE.transpose(PX[0:8, 1, 0:TP], comb[0:TP, :], ident[0:TP, 0:TP]).then_inc(sem("gate_tc"), 1)
            pe.wait_ge(sem("gate_ct"), nth("gate_ct", TT))
            pe.wait_ge(sem("gate_sel"), nth("gate_sel", 16))
            for j in range(3 * EXPERTS):
                e, c = j // 3, j % 3
                off, n = CH_N[c]
                if begun(j - 1):
                    pe.wait_ge(sem("gate_cb"), nth("gate_cb", j - 1))
                TE.matmul(PX[:, j % 2, 0:n], sel[0:EXPERTS, e * 128:e * 128 + 128], combT[0:EXPERTS, off:off + n],
                          start=True, stop=True).then_inc(sem("gate_cm"), 1)
            enter(pe, "gate")
            for r in rounds(pe, EXPERTS):
                for j in range(2):
                    for b in (0, 1):
                        pe.wait_ge(sem("ex_split"), nth("ex_split", 4 * r + 2 * j + b + 1))
                        if begun(3 * (2 * r + j)):
                            pe.wait_ge(sem(("ex_a", "ex_b")[b]), nth(("ex_a", "ex_b")[b], 3 * (2 * r + j)))
                        product(PS[:, b, :], L[b], zT, KT, 128, 128, CH_N, N).then_inc(sem("ex_mm"), 1)
            enter(pe, "ex")
            pe.wait_ge(sem("w3_res"), nth("w3_res", 32))
            pe.wait_ge(sem("b3_in"), nth("b3_in", 16))
            for r in rounds(pe, TT // 2):
                for b in (0, 1):
                    pe.wait_ge(sem(f"w3_slab{b}"), nth(f"w3_slab{b}", 48 * r + 48))
                    if begun(2 * (2 * r + b - 1)):
                        pe.wait_ge(sem("w3_v"), nth("w3_v", 2 * (2 * r + b - 1)))
                    product(PS[:, b, :], LG[b], w3, 2 * KT, 128, TP, CH_D, D, last=False)
                    for off, n in CH_D:
                        ins = TE.matmul(PS[0:TP, b, off:off + n], ct_tile[b][0:EXPERTS, 0:TP],
                                        b3r[0:EXPERTS, off:off + n], start=False, stop=True)
                    ins.then_inc(sem("w3_mm"), 1)

        @block.scalar
        def _(act):
            def stage_hi(ph, n, chunks, src):
                per = len(chunks)
                for r in rounds(act, n // 2):
                    for b in (0, 1):
                        for c in range(per):
                            q, h = per * b + c, (per * b + c) % 2
                            g = r * (2 * per) + q
                            w = chunks[c][1]
                            rows = TP if chunks is CH_D and ph not in ("m2",) else 128
                            act.wait_ge(sem(ph + "_val"), nth(ph + "_val", g + 1))
                            if begun(32 * (r * per + q // 2)):
                                act.wait_ge(sem(f"{ph}_st{h}"), nth(f"{ph}_st{h}", 32 * (r * per + q // 2)))
                            S.copy(HI[0:rows, 512 * h:512 * h + w], src[0:rows, 512 * h:512 * h + w])\
                                .then_inc(sem(ph + "_hi"), 1)

            for t in range(TT):
                act.wait_ge(sem("ln_var"), nth("ln_var", t + 1))
                S.activation(rstd[0:TP, :], small[0:TP, 0:1], ACT.Sqrt).then_inc(sem("ln_sd"), 1)
                act.wait_ge(sem("ln_nb"), nth("ln_nb", t + 1))
                if begun(64 * t):
                    act.wait_ge(sem("ln_st"), nth("ln_st", 64 * t))
                S.copy(HI[0:TP, :], nb[t % 2][0:TP, :]).then_inc(sem("ln_hi"), 1)
                act.wait_ge(sem("ln_tv"), nth("ln_tv", t + 1))
                S.copy(xnT[0][:, :].rearrange("p (k c) -> p k c", k=KT)[:, :, t * TP:(t + 1) * TP],
                       tv[:, :].rearrange("p (k c) -> p k c", k=KT)).then_inc(sem("ln_nh"), 1)
            enter(act, "ln")

            def stage_elu(ph, n, chunks, rows):
                per = len(chunks)
                for r in rounds(act, n // 2):
                    for b in (0, 1):
                        for c in range(per):
                            q, h = per * b + c, (per * b + c) % 2
                            g = r * (2 * per) + q
                            w = chunks[c][1]
                            cols = slice(512 * h, 512 * h + w)
                            act.wait_ge(sem(ph + "_m"), nth(ph + "_m", g + 1))
                            S.activation(T2[0:rows, cols], T2[0:rows, cols], ACT.Exp).then_inc(sem(ph + "_e"), 1)
                            act.wait_ge(sem(ph + "_val"), nth(ph + "_val", g + 1))
                            if begun(32 * (r * per + q // 2)):
                                act.wait_ge(sem(f"{ph}_st{h}"), nth(f"{ph}_st{h}", 32 * (r * per + q // 2)))
                            S.copy(HI[0:rows, cols], T1[0:rows, cols]).then_inc(sem(ph + "_hi"), 1)
            stage_elu("q", 8, CH_N, 128)
            enter(act, "q")
            stage_elu("k", 10, CH_D, TP)
            enter(act, "k")
            stage_hi("h", 10, CH_D, T1)
            enter(act, "h")

            def resident_hi(ph, dst):
                for r in rounds(act, 4):
                    for b in (0, 1):
                        act.wait_ge(sem(ph + "_mm"), nth(ph + "_mm", 2 * r + b + 1))
                        for c, (off, w) in enumerate(CH_D):
                            S.copy(dst[0][:, bass.ds(r * (2 * D) + (b * D + off), w)], PS[:, b, off:off + w])\
                                .then_inc(sem(ph + "_hi"), 1)
            resident_hi("m1", m1T)
            enter(act, "m1")
            stage_hi("m2", 8, CH_D, T1)
            enter(act, "m2")
            resident_hi("m3", m3)
            enter(act, "mix")
            act.wait_ge(sem("deg_mm"), nth("deg_mm", 1))
            S.activation(dis[0:TP, :], PX[0:TP, 0, 0:2 * TT].rearrange("p (t e) -> p t e", e=2)[:, :, 0],
                         ACT.Sqrt).then_inc(sem("deg_sd"), 1)
            enter(act, "deg")

            cv = counts[:, :, :]

            def gnn_slab(t):
                b = t % 2
                if begun(t - 1):
                    act.wait_ge(sem("gnn_mm"), nth("gnn_mm", t - 1))
                S.copy(L[b][0][0:TP, 0:TT * TP].rearrange("p (k c) -> p k c", k=TT),
                       cv[0:TP, :, t * TP:t * TP + TP]).then_inc(sem("gnn_sh"), 1)

            gnn_slab(0)
            for t in range(TT):
                if t + 1 < TT:
                    gnn_slab(t + 1)
                act.wait_ge(sem("gnn_var"), nth("gnn_var", t + 1))
                S.activation(rstd[0:TP, :], small[0:TP, 0:1], ACT.Sqrt).then_inc(sem("gnn_sd"), 1)
                act.wait_ge(sem("gnn_u"), nth("gnn_u", t + 1))
                if begun(t - 1):
                    act.wait_ge(sem("gnn_tr"), nth("gnn_tr", t - 1))
                S.activation(nb9[t % 2][0:TP, :], u9[0:TP, :], ACT.Square, accum_out=small[0:TP, 2:3])\
                    .then_inc(sem("gnn_sq"), 1)
                act.wait_ge(sem("gnn_ms"), nth("gnn_ms", t + 1))
                S.activation(small[0:TP, 4:5], small[0:TP, 3:4], ACT.Sqrt).then_inc(sem("gnn_rsd"), 1)
                act.wait_ge(sem("gnn_tv"), nth("gnn_tv", t + 1))
                if begun(48 * t):
                    act.wait_ge(sem("gnn_st"), nth("gnn_st", 48 * t))
                S.copy(HI[:, 0:KT * TP], tv9[:, :]).then_inc(sem("gnn_nh"), 1)
            enter(act, "gnn")
            act.wait_ge(sem("consts"), nth("consts", 128))
            for r in rounds(act, 8):
                for b in (0, 1):
                    for c, (off, w) in enumerate(CH_N):
                        q, h = 3 * b + c, (3 * b + c) % 2
                        g = r * 6 + q
                        cols = slice(512 * h, 512 * h + w)
                        if c == 0:
                            act.wait_ge(sem("qk_mm"), nth("qk_mm", 2 * r + b + 1))
                        if begun(g - 1):
                            act.wait_ge(sem("qk_lo"), nth("qk_lo", g - 1))
                        apart(act)
                        S.activation(T1[:, cols], PS[:, b, off:off + w], ACT.Identity,
                                     bias=bqk[:, bass.ds(2 * r + b, 1)]).then_inc(sem("qk_psf"), 1)
                        act.wait_ge(sem("qk_psf"), nth("qk_psf", g + 1))
                        for k in range(4):
                            o = k + 1 if k % 2 == 0 else k - 1
                            ins = S.copy(T3[32 * k:32 * k + 32, cols], T1[32 * o:32 * o + 32, cols])
                        ins.then_inc(sem("qk_rot"), 1)
                        act.wait_ge(sem("qk_val"), nth("qk_val", g + 1))
                        if begun(32 * (r * 3 + q // 2)):
                            act.wait_ge(sem(f"qk_st{h}"), nth(f"qk_st{h}", 32 * (r * 3 + q // 2)))
                        S.copy(HI[:, cols], T2[:, cols]).then_inc(sem("qk_hi"), 1)
            enter(act, "qk")
            stage_hi("v", 10, CH_D, T1)
            enter(act, "v")
            def exponentials(r, j):
                n, b = r * NT + j, j % 2
                act.wait_ge(sem("att_nm"), nth("att_nm", n + 1))
                for g in GROUPS:
                    if begun(n - 3):
                        act.wait_ge(sem("att_tr" + g), nth("att_tr" + g, n - 3))
                S.activation(prob[j % 4][0:TP, :], PS[0:TP, b, 0:N], ACT.Exp, bias=nmx[0:TP, b:b + 1],
                             scale=HD ** -0.5, accum_out=rs[0:TP, b:b + 1]).then_inc(sem("att_exp"), 1)

            def upper_part(r, j, g):
                n = r * NT + j
                act.wait_ge(sem("att_tr" + g), nth("att_tr" + g, n + 1))
                if g == "c" and j % 2 == 0:
                    if begun(r * TT + j // 2 - 1):
                        act.wait_ge(sem("att_pv"), nth("att_pv", r * TT + j // 2 - 1))
                S.copy(pT_part(j // 2 % 2, 0, g, j), group_read(g, j % 2)).then_inc(sem("att_hi" + g), 1)

            def output_copy(r, j):
                pair, pb = r * TT + j // 2, j // 2 % 2
                act.wait_ge(sem("att_pv"), nth("att_pv", pair + 1))
                if begun(pair - 1):
                    act.wait_ge(sem("att_osum"), nth("att_osum", pair - 1))
                S.copy(o_tmp[0:64, 250 * pb:250 * pb + 250], PX[64:128, 0, 0:250]).then_inc(sem("att_oc"), 1)

            def output_hi(r, j):
                pair, pb = r * TT + j // 2, j // 2 % 2
                oc = slice(250 * pb, 250 * pb + 250)
                act.wait_ge(sem("att_osum"), nth("att_osum", pair + 1))
                if begun(32 * (r * (TT // 2) + j // 4)):
                    act.wait_ge(sem(f"att_st{pb}"), nth(f"att_st{pb}", 32 * (r * (TT // 2) + j // 4)))
                S.copy(o_hi[0:64, oc], o_sum[0:64, oc]).then_inc(sem("att_ohi"), 1)
            for r, first, last in ring(act, HEADS // 2):
                for j in range(NT):
                    exponentials(r, j)
                    if not (first and j < 1):
                        upper_part(r, j - 1, "c")
                    if j % 2 == 1 and not (first and j < 2):
                        upper_part(r, j - 2, "a")
                    if not (first and j < 1):
                        upper_part(r, j - 1, "b")
                    if j % 2 == 0 and not (first and j < 4):
                        output_copy(r, j - 3)
                        output_hi(r, j - 3)
                    if j % 2 == 0 and not (first and j < 2):
                        upper_part(r, j - 2, "a")
            end = HEADS // 2 - 1
            upper_part(end, NT - 1, "c")
            upper_part(end, NT - 1, "b")
            output_copy(end, NT - 3)
            output_hi(end, NT - 3)
            upper_part(end, NT - 2, "a")
            upper_part(end, NT - 1, "a")
            output_copy(end, NT - 1)
            output_hi(end, NT - 1)
            enter(act, "att")
            for t in range(TT):
                act.wait_ge(sem("op_y"), nth("op_y", t + 1))
                if begun(t):
                    act.wait_ge(sem("op_tr"), nth("op_tr", t))
                S.activation(nb13[0][0:TP, :], T1[0:TP, :], ACT.Square, accum_out=small[0:TP, 2:3])\
                    .then_inc(sem("op_sq"), 1)
                act.wait_ge(sem("op_ms"), nth("op_ms", t + 1))
                S.activation(small[0:TP, 4:5], small[0:TP, 3:4], ACT.Sqrt).then_inc(sem("op_rsd"), 1)
                act.wait_ge(sem("op_tv"), nth("op_tv", t + 1))
                S.copy(zT[0][:, :].rearrange("p (k c) -> p k c", k=KT)[:, :, t * TP:(t + 1) * TP],
                       tv13[:, :].rearrange("p (k c) -> p k c", k=KT)).then_inc(sem("op_nh"), 1)
            enter(act, "op")
            act.wait_ge(sem("gate_mm"), nth("gate_mm", 1))
            S.copy(logT[0:8, :], PS[0:8, 0, 0:N]).then_inc(sem("gate_log"), 1)
            for t in range(TT):
                act.wait_ge(sem("gate_top"), nth("gate_top", t + 1))
                S.activation(ex8[0:TP, :], lg[0:TP, :], ACT.Exp, bias=nm1[0:TP, 0:1]).then_inc(sem("gate_e8"), 1)
                act.wait_ge(sem("gate_tc"), nth("gate_tc", t + 1))
                S.copy(combT[0:8, t * TP:t * TP + TP], PX[0:8, 1, 0:TP]).then_inc(sem("gate_ct"), 1)
            for j in range(3 * EXPERTS):
                off, n = CH_N[j % 3]
                act.wait_ge(sem("gate_cm"), nth("gate_cm", j + 1))
                S.copy(combB[:, j // 3, off:off + n], PX[:, j % 2, 0:n]).then_inc(sem("gate_cb"), 1)
            enter(act, "gate")
            for r in rounds(act, EXPERTS):
                for j in range(2):
                    for c, (off, w) in enumerate(CH_N):
                        q, h = 3 * j + c, (3 * j + c) % 2
                        g = r * 6 + q
                        cols = slice(512 * h, 512 * h + w)
                        if c == 0:
                            act.wait_ge(sem("ex_mm"), nth("ex_mm", 4 * r + 2 * j + 1))
                        if begun(g - 1):
                            act.wait_ge(sem("ex_b"), nth("ex_b", g - 1))
                        apart(act)
                        S.activation(T1[:, cols], PS[:, 0, off:off + w], ACT.Silu,
                                     bias=b1[:, bass.ds(2 * r + j, 1)]).then_inc(sem("ex_a"), 1)
                        act.wait_ge(sem("ex_val"), nth("ex_val", g + 1))
                        if begun(32 * (r * 3 + q // 2)):
                            act.wait_ge(sem(f"ex_st{h}"), nth(f"ex_st{h}", 32 * (r * 3 + q // 2)))
                        S.copy(HI[:, cols], T2[:, cols]).then_inc(sem("ex_hi"), 1)


        @block.vector
        def _(dve):
            P_SUB = ALU.subtract

            V.memset(ones2[:, :], 1.0).then_inc(sem("ones2_ready"), 1)

            def stage_lo(ph, r, per, q, g, src, cols, rows):
                dve.wait_ge(sem(ph + "_hi"), nth(ph + "_hi", g + 1))
                if begun(32 * (r * per + q // 2)):
                    dve.wait_ge(sem(f"{ph}_st{q % 2}"), nth(f"{ph}_st{q % 2}", 32 * (r * per + q // 2)))
                V.tensor_tensor(LO[0:rows, cols], src[0:rows, cols], HI[0:rows, cols].bitcast(F32), P_SUB)\
                    .then_inc(sem(ph + "_lo"), 1)

            def stats(ph, t, src, cols0=0):
                for k in range(2):
                    V.bn_stats(stat6[0:TP, 6 * k:6 * k + 6], src[0:TP, 512 * k:512 * k + 512]).then_inc(sem(ph + "_bn"), 1)
                dve.wait_ge(sem(ph + "_bn"), nth(ph + "_bn", 2 * t + 2))
                V.bn_aggr(mv[0:TP, :], stat6[0:TP, :]).then_inc(sem(ph + "_ag"), 1)
                dve.wait_ge(sem(ph + "_ag"), nth(ph + "_ag", t + 1))
                V.tensor_scalar(small[0:TP, 0:1], mv[0:TP, 1:2], LN_EPS, None, ALU.add).then_inc(sem(ph + "_var"), 1)
                dve.wait_ge(sem(ph + "_sd"), nth(ph + "_sd", t + 1))
                V.reciprocal(small[0:TP, 1:2], rstd[0:TP, :]).then_inc(sem(ph + "_rc"), 1)
                dve.wait_ge(sem(ph + "_rc"), nth(ph + "_rc", t + 1))

            def ln_tail(t):
                dve.wait_ge(sem("ln_hi"), nth("ln_hi", t + 1))
                if begun(64 * t):
                    dve.wait_ge(sem("ln_st"), nth("ln_st", 64 * t))
                V.tensor_tensor(LO[0:TP, :], nb[t % 2][0:TP, :], HI[0:TP, :].bitcast(F32), P_SUB).then_inc(sem("ln_lo"), 1)
                dve.wait_ge(sem("ln_tr"), nth("ln_tr", t + 1))
                if begun(t):
                    dve.wait_ge(sem("ln_rt"), nth("ln_rt", t))
                px = PX[:, :, 0:4 * TP]
                V.tensor_copy(tv[:, :].rearrange("p (a c) -> p a c", a=2), px).then_inc(sem("ln_tv"), 1)
                dve.wait_ge(sem("ln_nh"), nth("ln_nh", t + 1))
                tile = slice(t * TP, (t + 1) * TP)
                V.tensor_tensor(xnT[1][:, :].rearrange("p (k c) -> p k c", k=KT)[:, :, tile],
                                tv[:, :].rearrange("p (k c) -> p k c", k=KT),
                                xnT[0][:, :].rearrange("p (k c) -> p k c", k=KT)[:, :, tile].bitcast(F32), P_SUB)\
                    .then_inc(sem("ln_rt"), 1)
            for t in range(TT):
                b = t % 2
                src = [T1, T2][b]
                dve.wait_ge(sem(f"ln_x{b}"), nth(f"ln_x{b}", 16 * (t // 2 + 1)))
                stats("ln", t, src)
                V.tensor_scalar(nb[b][0:TP, :], src[0:TP, :], mv[0:TP, 0:1], small[0:TP, 1:2], ALU.subtract, ALU.mult)\
                    .then_inc(sem("ln_nb"), 1)
                ln_tail(t)
            enter(dve, "ln")

            def elu(ph, n, chunks, rows, first):
                per = len(chunks)
                for r in rounds(dve, n // 2):
                    for b in (0, 1):
                        for c, (off, w) in enumerate(chunks):
                            q = per * b + c
                            h = q % 2
                            g = r * (2 * per) + q
                            cols = slice(512 * h, 512 * h + w)
                            if c == 0:
                                dve.wait_ge(sem(ph + "_mm"), nth(ph + "_mm", 2 * r + b + 1))
                            first(r, b, off, w, cols)
                            dve.wait_ge(sem(ph + "_psf"), nth(ph + "_psf", g + 1))
                            V.tensor_scalar(T2[0:rows, cols], T1[0:rows, cols], 0.0, None, ALU.min).then_inc(sem(ph + "_m"), 1)
                            dve.wait_ge(sem(ph + "_e"), nth(ph + "_e", g + 1))
                            V.scalar_tensor_tensor(T1[0:rows, cols], T1[0:rows, cols], 0.0, T2[0:rows, cols],
                                                   ALU.max, ALU.add).then_inc(sem(ph + "_val"), 1)
                            dve.wait_ge(sem(ph + "_val"), nth(ph + "_val", g + 1))
                            stage_lo(ph, r, per, q, g, T1, cols, rows)

            dve.wait_ge(sem("consts"), nth("consts", 128))

            def q_first(r, b, off, w, cols):
                V.tensor_scalar(T1[:, cols], PS[:, b, off:off + w], bq[:, bass.ds(2 * r + b, 1)], None, ALU.add)\
                    .then_inc(sem("q_psf"), 1)
            elu("q", 8, CH_N, 128, q_first)
            enter(dve, "q")
            V.memset(ones_r[:, :].bitcast(F32), 1.0).then_inc(sem("ones_ready"), 1)
            V.memset(sorted_e[:, :, :], -1.0)
            dve.wait_ge(sem("edges"), nth("edges", 48))
            V.tensor_copy(edge_pair[0:TP, :, 0], edge_src_i[0:TP, :])
            V.tensor_copy(edge_dst[0:TP, :], edge_dst_i[0:TP, :]).then_inc(sem("sort_step"), 1)
            V.memset(reached[0:TP, 0, :], 1.0)
            V.memset(reached[0:TP, TT, :], 0.0)
            dve.wait_ge(sem("sort_step"), nth("sort_step", 1))
            for b in range(1, TT):
                ins = V.tensor_scalar(reached[0:TP, b, :], edge_dst[0:TP, :], float(b * TP), None, ALU.is_ge)
            ins.then_inc(sem("sort_step"), 1)
            dve.wait_ge(sem("sort_step"), nth("sort_step", 2))
            V.tensor_tensor(member[0:TP, :, :], reached[0:TP, 0:TT, :], reached[0:TP, 1:TT + 1, :], P_SUB)
            V.reduce_sum(edge_tile[0:TP, :], reached[0:TP, 1:TT, :].rearrange("p b c -> p c b"), AX.X)\
                .then_inc(sem("sort_step"), 1)
            dve.wait_ge(sem("sort_step"), nth("sort_step", 3))
            V.scalar_tensor_tensor(edge_pair[0:TP, :, 1], edge_tile[0:TP, :], -float(TP), edge_dst[0:TP, :],
                                   ALU.mult, ALU.add)
            flat = member[0:TP, :, :].rearrange("p b c -> p (b c)")
            V.tensor_tensor_scan(rank[0:TP, :, :].rearrange("p b c -> p (b c)"), flat, flat, 0.0, ALU.add, ALU.max)\
                .then_inc(sem("sort_step"), 1)
            dve.wait_ge(sem("sort_step"), nth("sort_step", 4))
            V.tensor_copy(tile_n[0:TP, 0:1], rank[0:TP, 0, EC - 1:EC])
            V.tensor_tensor(tile_n[0:TP, 1:TT], rank[0:TP, 1:TT, EC - 1], rank[0:TP, 0:TT - 1, EC - 1], P_SUB)\
                .then_inc(sem("sort_tile_n"), 1)
            dve.wait_ge(sem("sort_sums"), nth("sort_sums", 1))
            V.tensor_scalar(gran_i[0:TP, 0, :], PX[0:TP, 1, 0:TT], float(GRANULE - 1), None, ALU.add)\
                .then_inc(sem("sort_step"), 1)
            dve.wait_ge(sem("sort_step"), nth("sort_step", 5))
            V.tensor_scalar(gran_i[0:TP, 1, :], gran_i[0:TP, 0, :], GRANULE.bit_length() - 1, None,
                            ALU.logical_shift_right).then_inc(sem("sort_step"), 1)
            dve.wait_ge(sem("sort_step"), nth("sort_step", 6))
            V.tensor_copy(gran_f[0:TP, :], gran_i[0:TP, 1, :]).then_inc(sem("sort_step"), 1)
            dve.wait_ge(sem("sort_step"), nth("sort_step", 7))
            V.tensor_tensor_scan(gran_sum[0:TP, :], gran_f[0:TP, :], gran_f[0:TP, :], 0.0, ALU.add, ALU.max)\
                .then_inc(sem("sort_step"), 1)
            dve.wait_ge(sem("sort_step"), nth("sort_step", 8))
            V.tensor_tensor(gran_start[0:TP, :], gran_sum[0:TP, :], gran_f[0:TP, :], P_SUB).then_inc(sem("sort_step"), 1)
            dve.wait_ge(sem("sort_step"), nth("sort_step", 9))
            V.scalar_tensor_tensor(tile_off[0:TP, :], gran_start[0:TP, :], float(GRANULE), PX[0:TP, 0, 0:TT],
                                   ALU.mult, ALU.add).then_inc(sem("sort_step"), 1)
            dve.wait_ge(sem("sort_step"), nth("sort_step", 10))
            V.tensor_tensor(tile_off[0:TP, 1:TT], tile_off[0:TP, 1:TT], rank[0:TP, 0:TT - 1, EC - 1], P_SUB)\
                .then_inc(sem("sort_step"), 1)
            dve.wait_ge(sem("sort_step"), nth("sort_step", 11))
            for b in range(TT):
                ins = V.scalar_tensor_tensor(place[0:TP, b, :], rank[0:TP, b, :], tile_off[0:TP, b:b + 1],
                                             member[0:TP, b, :], ALU.add, ALU.mult)
            ins.then_inc(sem("sort_step"), 1)
            dve.wait_ge(sem("sort_step"), nth("sort_step", 12))
            V.reduce_sum(edge_pos[0:TP, :], place[0:TP, :, :].rearrange("p b c -> p c b"), AX.X)\
                .then_inc(sem("sort_step"), 1)
            dve.wait_ge(sem("sort_step"), nth("sort_step", 13))
            V.tensor_scalar(edge_pos_i[0:TP, :], edge_pos[0:TP, :], -1.0, None, ALU.add).then_inc(sem("sort_step"), 1)
            dve.wait_ge(sem("sort_step"), nth("sort_step", 14))
            V.tensor_scalar(edge_col_i[0:TP, :], edge_pos_i[0:TP, :], 7, None, ALU.logical_shift_right)
            V.tensor_scalar(edge_part_i[0:TP, :], edge_pos_i[0:TP, :], 127, None, ALU.bitwise_and)\
                .then_inc(sem("sort_step"), 1)
            dve.wait_ge(sem("sort_step"), nth("sort_step", 15))
            V.tensor_copy(edge_col[0:TP, :], edge_col_i[0:TP, :])
            V.tensor_copy(edge_dst[0:TP, :], edge_part_i[0:TP, :]).then_inc(sem("sort_step"), 1)
            dve.wait_ge(sem("sort_step"), nth("sort_step", 16))
            V.scalar_tensor_tensor(edge_row[0:TP, :], edge_dst[0:TP, :], float(SC), edge_col[0:TP, :], ALU.mult, ALU.add)
            dve.wait_ge(sem("gran_iota"), nth("gran_iota", 1))
            V.tensor_tensor(gran_ge[0:1, :, :], gran_no[0:1, :].unsqueeze(1).broadcast_to([1, TT - 1, GRANULES]),
                            gran_start[0:1, 1:TT].unsqueeze(2).broadcast_to([1, TT - 1, GRANULES]), ALU.is_ge)\
                .then_inc(sem("sort_step"), 1)
            dve.wait_ge(sem("sort_step"), nth("sort_step", 17))
            V.reduce_sum(gran_no[0:1, :], gran_ge[0:1, :, :].rearrange("p b g -> p g b"), AX.X)\
                .then_inc(sem("sort_step"), 1)
            dve.wait_ge(sem("sort_step"), nth("sort_step", 18))
            V.tensor_scalar(gran_at[0:1, :], gran_no[0:1, :], float(N), None, ALU.mult).then_inc(sem("sort_ready"), 1)
            dve.wait_ge(sem("sort_ready"), nth("sort_ready", 1))
            dve.wait_ge(sem("k_bias"), nth("k_bias", 16))

            def k_first(r, b, off, w, cols):
                V.tensor_tensor(T1[0:TP, cols], PS[0:TP, b, off:off + w], bias_b[0:TP, off:off + w], ALU.add)\
                    .then_inc(sem("k_psf"), 1)
            elu("k", 10, CH_D, TP, k_first)
            enter(dve, "k")

            def plain(ph, n, chunks, rows, first):
                per = len(chunks)
                for r in rounds(dve, n // 2):
                    for b in (0, 1):
                        for c, (off, w) in enumerate(chunks):
                            q = per * b + c
                            g = r * (2 * per) + q
                            cols = slice(512 * (q % 2), 512 * (q % 2) + w)
                            if c == 0:
                                dve.wait_ge(sem(ph + "_mm"), nth(ph + "_mm", 2 * r + b + 1))
                            first(r, b, off, w, cols)
                            dve.wait_ge(sem(ph + "_val"), nth(ph + "_val", g + 1))
                            stage_lo(ph, r, per, q, g, T1, cols, rows)

            def add_rows(ph, bias):
                def first(r, b, off, w, cols):
                    V.tensor_tensor(T1[0:TP, cols], PS[0:TP, b, off:off + w], bias[0:TP, off:off + w], ALU.add)\
                        .then_inc(sem(ph + "_val"), 1)
                return first
            dve.wait_ge(sem("g_bias"), nth("g_bias", 16))
            plain("h", 10, CH_D, TP, add_rows("h", bias_a))
            enter(dve, "h")
            dve.wait_ge(sem("ks_mm"), nth("ks_mm", 1))
            V.tensor_copy(ksb[:, :], PS[:, 0, 0:D]).then_inc(sem("ks_v"), 1)

            def resident_lo(ph, dst):
                for r in rounds(dve, 4):
                    for b in (0, 1):
                        for c, (off, w) in enumerate(CH_D):
                            dve.wait_ge(sem(ph + "_hi"), nth(ph + "_hi", 4 * r + 2 * b + c + 1))
                            cols = bass.ds(r * (2 * D) + (b * D + off), w)
                            V.tensor_tensor(dst[1][:, cols], PS[:, b, off:off + w], dst[0][:, cols].bitcast(F32), P_SUB)\
                                .then_inc(sem(ph + "_lo"), 1)
            resident_lo("m1", m1T)
            enter(dve, "m1")

            def m2_first(r, b, off, w, cols):
                V.scalar_tensor_tensor(T1[:, cols], ksb[:, off:off + w], bv[:, bass.ds(2 * r + b, 1)],
                                       PS[:, b, off:off + w], ALU.mult, ALU.add).then_inc(sem("m2_val"), 1)
            plain("m2", 8, CH_D, 128, m2_first)
            enter(dve, "m2")
            dve.wait_ge(sem("ks_tr"), nth("ks_tr", 1))
            V.tensor_scalar(T1[:, 0:2 * KT].rearrange("p (k e) -> p k e", e=2),
                            PX[:, :, :].rearrange("p a (k c) -> p (a k) c", c=128)[:, :, 0:2], 1e-6, None, ALU.add)\
                .then_inc(sem("ks_c1"), 1)
            dve.wait_ge(sem("ks_c1"), nth("ks_c1", 1))
            V.tensor_copy(ksT_hi[:, :], T1[:, 0:2 * KT]).then_inc(sem("ks_c2"), 1)
            dve.wait_ge(sem("ks_c2"), nth("ks_c2", 1))
            V.tensor_tensor(ksT_lo[:, :], T1[:, 0:2 * KT], ksT_hi[:, :].bitcast(F32), P_SUB).then_inc(sem("ks_col"), 1)
            resident_lo("m3", m3)
            enter(dve, "m3")
            dve.wait_ge(sem("o_bias"), nth("o_bias", 16))
            for r in rounds(dve, TT // 2):
                for b in (0, 1):
                    dve.wait_ge(sem("mix_mm"), nth("mix_mm", 2 * r + b + 1))
                    V.reciprocal(zr[0:TP, b:b + 1], PS[0:TP, b, 1024:1025]).then_inc(sem("mix_z"), 1)
                    for c in (0, 1):
                        g = 4 * r + 2 * b + c
                        cols = slice(512 * c, 512 * c + 512)
                        dve.wait_ge(sem(f"mix_in{c}"), nth(f"mix_in{c}", 32 * r + 16 * b + 16))
                        if begun(32 * r + 16 * b):
                            dve.wait_ge(sem(f"mix_st{c}"), nth(f"mix_st{c}", 32 * r + 16 * b))
                        V.tensor_tensor(T1[0:TP, cols], T2[0:TP, cols], bias_a[0:TP, cols], ALU.add).then_inc(sem("mix_xb"), 1)
                        dve.wait_ge(sem("mix_xb"), nth("mix_xb", g + 1))
                        dve.wait_ge(sem("mix_z"), nth("mix_z", 2 * r + b + 1))
                        V.scalar_tensor_tensor(T1[0:TP, cols], PS[0:TP, b, cols], zr[0:TP, b:b + 1], T1[0:TP, cols],
                                               ALU.mult, ALU.add).then_inc(sem("mix_v"), 1)
            enter(dve, "mix")
            V.memset(counts[:, 0:TT // 2, :], 0.0).then_inc(sem("counts_zero"), 1)
            dve.wait_ge(sem("sorted_in"), nth("sorted_in", 16))
            dve.wait_ge(sem("iota"), nth("iota", 1))

            def onehots(g, k):
                if begun(GC * g + (k + 1 - GC)):
                    dve.wait_ge(sem("oh_used"), nth("oh_used", GC * g + (k + 1 - GC)))
                col = GC * g + k
                src, dst = [sorted_e[:, bass.ds(col, 1) if not isinstance(col, int) else slice(col, col + 1), e]
                            for e in (0, 1)]
                V.tensor_scalar(oh_src[:, k, :], iota[:, :], src, None, ALU.is_equal)
                V.tensor_scalar(oh_dst[:, k, 0:TP], iota[:, 0:TP], dst, None, ALU.is_equal).then_inc(sem("oh_ready"), 1)

            def add_granule(g, b):
                column = dve.value_load(gran_at[0:1, bass.ds(g, 1)], min_val=0, max_val=(TT - 1) * N)
                flat = counts[0:TP, :, :].rearrange("p t c -> p (t c)")[:, bass.ds(column, N)]
                dve.wait_ge(sem("oh_used"), nth("oh_used", GC * g + GC))
                if begun(g):
                    dve.wait_ge(sem("adj_ev"), nth("adj_ev", g))
                V.tensor_tensor(flat, PS[0:TP, b, 0:N], flat, ALU.add).then_inc(sem("adj_ev"), 1)
            dve.wait_ge(sem("counts_zero"), nth("counts_zero", 2))
            for r in rounds(dve, GRANULES // 2):
                for b in (0, 1):
                    for k in range(GC):
                        onehots(2 * r + b, k)
                    if not (isinstance(r, int) and b == 0):
                        add_granule(2 * r + (b - 1), 1 - b)
            add_granule(GRANULES - 1, 1)
            dve.wait_ge(sem("adj_ev"), nth("adj_ev", GRANULES))
            for j in range(TT):
                ins = V.tensor_tensor(counts[0:TP, j, j * TP:(j + 1) * TP], counts[0:TP, j, j * TP:(j + 1) * TP],
                                      ident[0:TP, 0:TP], ALU.add)
            ins.then_inc(sem("loops_in"), 1)
            dve.wait_ge(sem("loops_in"), nth("loops_in", 1))
            dve.wait_ge(sem("deg_sd"), nth("deg_sd", 1))
            V.reciprocal(dis[0:TP, :], dis[0:TP, :]).then_inc(sem("deg_r"), 1)
            dve.wait_ge(sem("deg_r"), nth("deg_r", 1))
            for j in range(TT):
                ins = V.tensor_scalar(counts[0:TP, j, :], counts[0:TP, j, :], dis[0:TP, j:j + 1], None, ALU.mult)
            ins.then_inc(sem("deg_scaled"), 1)
            enter(dve, "deg")

            def gnn_slab(t):
                b = t % 2
                dve.wait_ge(sem("gnn_sh"), nth("gnn_sh", t + 1))
                V.tensor_tensor(L[b][1][0:TP, 0:TT * TP].rearrange("p (k c) -> p k c", k=TT),
                                counts[0:TP, :, t * TP:t * TP + TP],
                                L[b][0][0:TP, 0:TT * TP].rearrange("p (k c) -> p k c", k=TT).bitcast(F32), P_SUB)\
                    .then_inc(sem("gnn_slab"), 1)

            def rms(ph, t, src, dst):
                dve.wait_ge(sem(ph + "_sq"), nth(ph + "_sq", t + 1))
                V.tensor_scalar(small[0:TP, 3:4], small[0:TP, 2:3], 1.0 / D, RMS_EPS, ALU.mult, ALU.add)\
                    .then_inc(sem(ph + "_ms"), 1)
                dve.wait_ge(sem(ph + "_rsd"), nth(ph + "_rsd", t + 1))
                V.reciprocal(small[0:TP, 5:6], small[0:TP, 4:5]).then_inc(sem(ph + "_rmsr"), 1)
                dve.wait_ge(sem(ph + "_rmsr"), nth(ph + "_rmsr", t + 1))
                V.tensor_scalar(dst[0:TP, :], src[0:TP, :], small[0:TP, 5:6], None, ALU.mult).then_inc(sem(ph + "_nb"), 1)

            def weighted(ph, t, w, dst):
                dve.wait_ge(sem(ph + "_tr"), nth(ph + "_tr", t + 1))
                if begun(t):
                    dve.wait_ge(sem(ph + "_rt"), nth(ph + "_rt", t))
                V.tensor_tensor(dst[:, :].rearrange("p (a k c) -> p a k c", a=2, k=4),
                                PX[:, :, 0:4 * TP].rearrange("p a (k c) -> p a k c", k=4),
                                w[:, :].rearrange("p (a k) -> p a k", a=2).unsqueeze(3).broadcast_to([128, 2, 4, TP]),
                                ALU.mult).then_inc(sem(ph + "_tv"), 1)
            gnn_slab(0)
            for t in range(TT):
                if t + 1 < TT:
                    gnn_slab(t + 1)
                b = t % 2
                dve.wait_ge(sem("gnn_acc"), nth("gnn_acc", 16 * (t + 1)))
                dve.wait_ge(sem("gnn_mm"), nth("gnn_mm", t + 1))
                if begun(48 * t):
                    dve.wait_ge(sem("gnn_st"), nth("gnn_st", 48 * t))
                V.scalar_tensor_tensor(T1[0:TP, :], PS[0:TP, b, 0:D], dis[0:TP, t:t + 1], T2[0:TP, :],
                                       ALU.mult, ALU.add).then_inc(sem("gnn_x1"), 1)
                dve.wait_ge(sem("gnn_x1"), nth("gnn_x1", t + 1))
                stats("gnn", t, T1)
                V.tensor_copy(mean_all[0:TP, t:t + 1], mv[0:TP, 0:1])
                V.tensor_copy(rstd_all[0:TP, t:t + 1], small[0:TP, 1:2])
                V.tensor_scalar(u9[0:TP, :], T1[0:TP, :], mv[0:TP, 0:1], small[0:TP, 1:2], ALU.subtract, ALU.mult)\
                    .then_inc(sem("gnn_u"), 1)
                rms("gnn", t, u9, nb9[b])
                weighted("gnn", t, n1w, tv9)
                dve.wait_ge(sem("gnn_nh"), nth("gnn_nh", t + 1))
                V.tensor_tensor(LO[:, 0:KT * TP], tv9[:, :], HI[:, 0:KT * TP].bitcast(F32), P_SUB).then_inc(sem("gnn_rt"), 1)
            enter(dve, "gnn")
            dve.wait_ge(sem("rope_tables"), nth("rope_tables", 32))
            for r in rounds(dve, 8):
                for b in (0, 1):
                    for c, (off, w) in enumerate(CH_N):
                        q = 3 * b + c
                        g = r * 6 + q
                        cols = slice(512 * (q % 2), 512 * (q % 2) + w)
                        dve.wait_ge(sem("qk_psf"), nth("qk_psf", g + 1))
                        V.tensor_tensor(T2[:, cols], T1[:, cols], cosT[:, off:off + w], ALU.mult).then_inc(sem("qk_c"), 1)
                        dve.wait_ge(sem("qk_rot"), nth("qk_rot", g + 1))
                        V.tensor_tensor(T3[:, cols], T3[:, cols], sinT[:, off:off + w], ALU.mult).then_inc(sem("qk_s"), 1)
                        dve.wait_ge(sem("qk_s"), nth("qk_s", g + 1))
                        V.tensor_tensor(T2[:, cols], T2[:, cols], T3[:, cols], ALU.add).then_inc(sem("qk_val"), 1)
                        dve.wait_ge(sem("qk_val"), nth("qk_val", g + 1))
                        stage_lo("qk", r, 3, q, g, T2, cols, 128)
            enter(dve, "qk")
            dve.wait_ge(sem("v2_bias"), nth("v2_bias", 16))
            plain("v", 10, CH_D, TP, add_rows("v", bias_a))
            enter(dve, "v")

            def row_max(r, j):
                n, b = r * NT + j, j % 2
                dve.wait_ge(sem("att_sc"), nth("att_sc", n + 1))
                V.reduce_max(mx[0:TP, b:b + 1], PS[0:TP, b, 0:N], AX.X).then_inc(sem("att_mx"), 1)
                dve.wait_ge(sem("att_mx"), nth("att_mx", n + 1))
                V.tensor_scalar(nmx[0:TP, b:b + 1], mx[0:TP, b:b + 1], -(HD ** -0.5), None, ALU.mult)\
                    .then_inc(sem("att_nm"), 1)

            def lower_part(r, j, g):
                pb = j // 2 % 2
                dve.wait_ge(sem("att_hi" + g), nth("att_hi" + g, r * NT + j + 1))
                V.tensor_tensor(pT_part(pb, 1, g, j), group_read(g, j % 2), pT_part(pb, 0, g, j).bitcast(F32), P_SUB)\
                    .then_inc(sem("att_lo" + g), 1)

            def output_sum(r, j):
                pair, pb = r * TT + j // 2, j // 2 % 2
                oc = slice(250 * pb, 250 * pb + 250)
                dve.wait_ge(sem("att_oc"), nth("att_oc", pair + 1))
                V.tensor_tensor(o_sum[0:64, oc], PX[0:64, 0, 0:250], o_tmp[0:64, oc], ALU.add)\
                    .then_inc(sem("att_osum"), 1)

            def output_lo(r, j):
                pair, pb = r * TT + j // 2, j // 2 % 2
                oc = slice(250 * pb, 250 * pb + 250)
                dve.wait_ge(sem("att_ohi"), nth("att_ohi", pair + 1))
                if begun(32 * (r * (TT // 2) + j // 4)):
                    dve.wait_ge(sem(f"att_st{pb}"), nth(f"att_st{pb}", 32 * (r * (TT // 2) + j // 4)))
                V.tensor_tensor(o_lo[0:64, oc], o_sum[0:64, oc], o_hi[0:64, oc].bitcast(F32), P_SUB)\
                    .then_inc(sem("att_olo"), 1)
            row_max(0, 0)
            for r, first, last in ring(dve, HEADS // 2):
                for j in range(NT):
                    b = j % 2
                    dve.wait_ge(sem("att_exp"), nth("att_exp", r * NT + j + 1))
                    V.reciprocal(rr[0:TP, b:b + 1], rs[0:TP, b:b + 1]).then_inc(sem("att_rr"), 1)
                    if not (first and j < 1):
                        lower_part(r, j - 1, "c")
                    if j % 2 == 1 and not (first and j < 2):
                        lower_part(r, j - 2, "a")
                    if not (first and j < 1):
                        lower_part(r, j - 1, "b")
                    out = j % 2 == 0 and not (first and j < 4)
                    if out:
                        output_sum(r, j - 3)
                    if not (last and j == NT - 1):
                        row_max(r, j + 1)
                    if out:
                        output_lo(r, j - 3)
                    if j % 2 == 0 and not (first and j < 2):
                        lower_part(r, j - 2, "a")
            end = HEADS // 2 - 1
            lower_part(end, NT - 1, "c")
            lower_part(end, NT - 1, "b")
            output_sum(end, NT - 3)
            output_lo(end, NT - 3)
            lower_part(end, NT - 2, "a")
            lower_part(end, NT - 1, "a")
            output_sum(end, NT - 1)
            output_lo(end, NT - 1)
            enter(dve, "att")
            dve.wait_ge(sem("ob_bias"), nth("ob_bias", 16))
            for t in range(TT):
                b = t % 2
                dve.wait_ge(sem("op_x1"), nth("op_x1", 16 * (t + 1)))
                V.tensor_scalar(T1[0:TP, :], T2[0:TP, :], mean_all[0:TP, t:t + 1], rstd_all[0:TP, t:t + 1],
                                ALU.subtract, ALU.mult).then_inc(sem("op_u"), 1)
                dve.wait_ge(sem("op_u"), nth("op_u", t + 1))
                V.tensor_tensor(T1[0:TP, :], T1[0:TP, :], bias_a2[0:TP, :], ALU.add).then_inc(sem("op_ub"), 1)
                dve.wait_ge(sem("op_ub"), nth("op_ub", t + 1))
                dve.wait_ge(sem("op_mm"), nth("op_mm", t + 1))
                V.tensor_tensor(T1[0:TP, :], T1[0:TP, :], PS[0:TP, b, 0:D], ALU.add).then_inc(sem("op_y"), 1)
                dve.wait_ge(sem("op_y"), nth("op_y", t + 1))
                V.tensor_tensor(T2[0:TP, :], T2[0:TP, :], T1[0:TP, :], ALU.add).then_inc(sem("op_xy"), 1)
                rms("op", t, T1, nb13[0])
                weighted("op", t, n2w, tv13)
                dve.wait_ge(sem("op_nh"), nth("op_nh", t + 1))
                tile = slice(t * TP, (t + 1) * TP)
                V.tensor_tensor(zT[1][:, :].rearrange("p (k c) -> p k c", k=KT)[:, :, tile],
                                tv13[:, :].rearrange("p (k c) -> p k c", k=KT),
                                zT[0][:, :].rearrange("p (k c) -> p k c", k=KT)[:, :, tile].bitcast(F32), P_SUB)\
                    .then_inc(sem("op_rt"), 1)
            enter(dve, "op")
            dve.wait_ge(sem("gate_iota"), nth("gate_iota", 1))
            for t in range(TT):
                dve.wait_ge(sem("gate_tr"), nth("gate_tr", t + 1))
                if begun(t):
                    dve.wait_ge(sem("gate_e8"), nth("gate_e8", t))
                V.tensor_copy(lg[0:TP, :], PX[0:TP, 0, 0:8]).then_inc(sem("gate_lg"), 1)
                dve.wait_ge(sem("gate_lg"), nth("gate_lg", t + 1))
                V.max(m8[0:TP, :], lg[0:TP, :]).then_inc(sem("gate_c"), 1)
                dve.wait_ge(sem("gate_c"), nth("gate_c", 8 * t + 1))
                V.tensor_scalar(nm1[0:TP, 0:1], m8[0:TP, 0:1], -1.0, None, ALU.mult).then_inc(sem("gate_top"), 1)
                V.max_index(top_i[0:TP, :], m8[0:TP, :], lg[0:TP, :]).then_inc(sem("gate_c"), 1)
                dve.wait_ge(sem("gate_c"), nth("gate_c", 8 * t + 2))
                V.tensor_copy(top_f[0:TP, :], top_i[0:TP, :]).then_inc(sem("gate_c"), 1)
                if begun(8 * t + 3):
                    dve.wait_ge(sem("gate_c"), nth("gate_c", 8 * t + 3))
                V.tensor_scalar(mask[0:TP, :], eight[0:TP, :], top_f[0:TP, 0:1], None, ALU.is_equal).then_inc(sem("gate_c"), 1)
                if begun(8 * t + 4):
                    dve.wait_ge(sem("gate_c"), nth("gate_c", 8 * t + 4))
                V.scalar_tensor_tensor(mask[0:TP, :], eight[0:TP, :], top_f[0:TP, 1:2], mask[0:TP, :],
                                       ALU.is_equal, ALU.add).then_inc(sem("gate_c"), 1)
                if begun(8 * t + 5):
                    dve.wait_ge(sem("gate_c"), nth("gate_c", 8 * t + 5))
                dve.wait_ge(sem("gate_e8"), nth("gate_e8", t + 1))
                V.tensor_tensor(comb[0:TP, :], ex8[0:TP, :], mask[0:TP, :], ALU.mult).then_inc(sem("gate_c"), 1)
                if begun(8 * t + 6):
                    dve.wait_ge(sem("gate_c"), nth("gate_c", 8 * t + 6))
                V.reduce_sum(small[0:TP, 0:1], comb[0:TP, :], AX.X).then_inc(sem("gate_c"), 1)
                if begun(8 * t + 7):
                    dve.wait_ge(sem("gate_c"), nth("gate_c", 8 * t + 7))
                V.reciprocal(small[0:TP, 1:2], small[0:TP, 0:1]).then_inc(sem("gate_c"), 1)
                if begun(8 * t + 8):
                    dve.wait_ge(sem("gate_c"), nth("gate_c", 8 * t + 8))
                V.tensor_scalar(comb[0:TP, :], comb[0:TP, :], small[0:TP, 1:2], None, ALU.mult).then_inc(sem("gate_comb"), 1)
                dve.wait_ge(sem("gate_tc"), nth("gate_tc", t + 1))
            enter(dve, "gate")
            for r in rounds(dve, EXPERTS):
                for j in range(2):
                    for c, (off, w) in enumerate(CH_N):
                        q = 3 * j + c
                        g = r * 6 + q
                        cols = slice(512 * (q % 2), 512 * (q % 2) + w)
                        if c == 0:
                            dve.wait_ge(sem("ex_mm"), nth("ex_mm", 4 * r + 2 * j + 2))
                        dve.wait_ge(sem("ex_a"), nth("ex_a", g + 1))
                        V.scalar_tensor_tensor(T2[:, cols], PS[:, 1, off:off + w], b2[:, bass.ds(2 * r + j, 1)], T1[:, cols],
                                               ALU.add, ALU.mult).then_inc(sem("ex_b"), 1)
                        dve.wait_ge(sem("ex_b"), nth("ex_b", g + 1))
                        V.tensor_tensor(T2[:, cols], T2[:, cols], combB[:, r, off:off + w], ALU.mult)\
                            .then_inc(sem("ex_val"), 1)
                        dve.wait_ge(sem("ex_val"), nth("ex_val", g + 1))
                        stage_lo("ex", r, 3, q, g, T2, cols, 128)
            enter(dve, "ex")
            for r in rounds(dve, TT // 2):
                for b in (0, 1):
                    dve.wait_ge(sem("w3_mm"), nth("w3_mm", 2 * r + b + 1))
                    for c in (0, 1):
                        cols = slice(512 * c, 512 * c + 512)
                        dve.wait_ge(sem(f"w3_in{c}"), nth(f"w3_in{c}", 32 * r + 16 * b + 16))
                        if begun(32 * r + 16 * b):
                            dve.wait_ge(sem(f"w3_st{c}"), nth(f"w3_st{c}", 32 * r + 16 * b))
                        V.tensor_tensor(T1[0:TP, cols], T2[0:TP, cols], PS[0:TP, b, cols], ALU.add).then_inc(sem("w3_v"), 1)




def _shape_constants():
    inv = (1.0 / 10000.0 ** (np.arange(0, HD, 2, dtype=np.float32) / HD)).astype(np.float32)
    angle = inv[np.arange(128) % 32][:, None] * np.arange(N, dtype=np.float32)[None, :]
    sign = np.where(np.arange(128) % HD < 32, -1.0, 1.0)[:, None]
    sel = np.zeros((EXPERTS, EXPERTS * 128), np.float32)
    for e in range(EXPERTS):
        sel[e, e * 128:(e + 1) * 128] = 1.0
    below = np.triu(np.ones((128, 128), np.float32), 1)
    return {"below": below, "cos": np.cos(angle).astype(np.float32), "sin": (sign * np.sin(angle)).astype(np.float32),
            "ident": np.eye(128, dtype=np.float32), "sel": sel}


def kernel(x, src, dst, L0_gnn_W, L0_gnn_b, L0_mix_Wq, L0_mix_bq, L0_mix_Wk, L0_mix_bk, L0_mix_Wv, L0_mix_bv,
           L0_mix_Wo, L0_mix_bo, L0_ffn_norm1_w, L0_ffn_norm2_w, L0_ffn_qkv_w, L0_ffn_qkv_b, L0_ffn_out_w,
           L0_ffn_out_b, L0_ffn_gate_w, L0_ffn_w1, L0_ffn_b1, L0_ffn_w2, L0_ffn_b2, L0_ffn_w3, L0_ffn_b3):
    import concourse.bacc as _bacc
    from concourse.bass_utils import run_bass_kernel_spmd as _run

    def slabs(w):
        w = np.asarray(w)
        return w.reshape(-1, 128, KT, 128).transpose(0, 3, 2, 1)

    def cols(v):
        return np.asarray(v).reshape(-1, 128).T

    w12 = np.stack([np.asarray(L0_ffn_w1), np.asarray(L0_ffn_w2)], axis=1)
    w12 = w12.reshape(EXPERTS, 2, 2, 128, KT, 128).transpose(0, 2, 1, 5, 4, 3).reshape(4 * EXPERTS, 128, KT, 128)
    gate = np.tile(np.asarray(L0_ffn_gate_w).T, (1, 128 // EXPERTS))
    qkv_w, qkv_b = np.asarray(L0_ffn_qkv_w), np.asarray(L0_ffn_qkv_b)
    arrays = {
        "x": x, "src": src, "dst": dst,
        "Wq": slabs(L0_mix_Wq), "Wk": np.asarray(L0_mix_Wk).T, "Wg": np.asarray(L0_gnn_W).T, "Wv": slabs(L0_mix_Wv),
        "Wo": np.asarray(L0_mix_Wo).T, "Wqk": slabs(qkv_w[:2 * D]), "Wv2": qkv_w[2 * D:].T,
        "Wo2": np.asarray(L0_ffn_out_w).T, "gate": gate.reshape(KT, 128, 128).transpose(1, 0, 2), "W12": w12,
        "W3": np.asarray(L0_ffn_w3).transpose(0, 2, 1).reshape(EXPERTS * HID, D),
        "bq": cols(L0_mix_bq), "bv": cols(L0_mix_bv), "bqk": cols(qkv_b[:2 * D]), "b1": cols(np.asarray(L0_ffn_b1).ravel()),
        "b2": cols(np.asarray(L0_ffn_b2).ravel()), "n1": cols(L0_ffn_norm1_w), "n2": cols(L0_ffn_norm2_w),
        "bk": L0_mix_bk, "bg": L0_gnn_b, "bo": L0_mix_bo, "bv2": qkv_b[2 * D:], "ob": L0_ffn_out_b, "b3": L0_ffn_b3,
        **_shape_constants(),
    }
    nc = _bacc.Bacc("TRN2", target_bir_lowering=False, num_devices=1)
    io, feed = {}, {}
    for name, a in arrays.items():
        a = np.ascontiguousarray(a)
        feed["in_" + name] = a
        io[name] = nc.dram_tensor("in_" + name, a.shape, mybir.dt.from_np(a.dtype), kind="ExternalInput").ap()
    io["out"] = nc.dram_tensor("out_rows", (N, D), F32, kind="ExternalOutput").ap()
    build(nc, io)
    return _run(nc, [feed], core_ids=[0]).results[0]["out_rows"]
```

```python
import numpy as np
import concourse.bass as bass
from concourse import mybir
from contextlib import ExitStack

F32 = mybir.dt.float32
F32R = mybir.dt.float32r
F16 = mybir.dt.float16
I32 = mybir.dt.int32
ALU = mybir.AluOpType
ACT = mybir.ActivationFunctionType
AX = mybir.AxisListType

N = 1250
D = 1024
TT, TP = 10, 125
KT = D // 128
EDGES = 21250
EC = EDGES // TP
HEADS, HD = 16, 64
EXPERTS, HID = 8, 256
CH_N = [(0, 512), (512, 512), (1024, 226)]
CH_D = [(0, 512), (512, 512)]
GC = 4
GRANULE = GC * 128
GRANULES = (EDGES // GRANULE + TT + 1) // 2 * 2
SC = GRANULES * GC
LN_EPS, RMS_EPS = 1e-5, 1e-6


def build(nc, io):
    ctx = ExitStack()
    with ctx:
        sems = {}

        per_phase = {
            "mm": (("q", 8), ("k", 10), ("h", 10), ("m1", 8), ("m2", 8), ("m3", 8), ("mix", 10), ("gnn", 10), ("qk", 16),
                   ("v", 10), ("op", 10), ("gate", 1), ("ex", 32), ("w3", 10)),
            "lo": (("ln", 10), ("q", 24), ("k", 20), ("h", 20), ("m1", 16), ("m2", 16), ("m3", 16), ("qk", 48), ("v", 20),
                   ("ex", 48)),
            "val": (("q", 24), ("k", 20), ("h", 20), ("m2", 16), ("qk", 48), ("v", 20), ("ex", 48)),
            "psf": (("q", 24), ("k", 20), ("qk", 48)),
            "m": (("q", 24), ("k", 20)),
            "st0": (("q", 384), ("k", 320), ("h", 320), ("m2", 256), ("mix", 160), ("qk", 768), ("v", 320), ("att", 1280),
                    ("ex", 768), ("w3", 160)),
            "slab0": (("k", 160), ("h", 160), ("m1", 128), ("m3", 128), ("mix", 160), ("v", 160), ("op", 160), ("w3", 240)),
            "raw0": (("q", 64), ("m2", 64), ("qk", 128), ("gate", 16), ("ex", 256)),
            "raw1": (("q", 64), ("m2", 64), ("qk", 128), ("ex", 256)),
            "split": (("q", 8), ("m2", 8), ("qk", 16), ("gate", 1), ("ex", 32)),
            "rr0": (("k", 16), ("h", 16), ("m3", 16), ("v", 16), ("op", 16), ("w3", 16)),
            "res": (("k", 8), ("h", 8), ("m3", 8), ("v", 8), ("op", 8), ("w3", 16)),
            "v": (("mix", 20), ("w3", 20)),
            "in0": (("mix", 160), ("w3", 160)),
            "tr": (("ln", 10), ("gnn", 10), ("op", 10)),
            "sq": (("gnn", 10), ("op", 10)),
            "bn": (("ln", 20), ("gnn", 20)),
            "var": (("ln", 10), ("gnn", 10)),
        }
        for signal, like in (("hi", "lo"), ("e", "m"), ("st1", "st0"), ("slab1", "slab0"), ("sh", "split"), ("rr1", "rr0"), ("rr2", "rr0"), ("rr3", "rr0"),
                            
                             ("rh", "res"), ("in1", "in0"), ("tv", "tr"), ("nb", "tr"), ("rt", "tr"), ("nh", "tr"), ("ms", "sq"),
                             ("rsd", "sq"), ("rmsr", "sq"), ("ag", "var"), ("sd", "var"), ("rc", "var")):
            per_phase[signal] = per_phase[like]

        def before(name):
            ph, _, signal = name.partition("_")
            count = 0
            for p, n in per_phase.get(signal, ()):
                if p == ph:
                    return signal, count
                count += n
            return name, 0

        def sem(name):
            name = before(name)[0]
            if name not in sems:
                sems[name] = ctx.enter_context(nc.semaphore(name))
            return sems[name]

        base = nc.sbuf_base + (-nc.sbuf_base) % 32
        A0 = base
        B0 = A0 + 80000
        L0 = B0 + 81920
        RAW0 = L0 + 20480
        W0 = RAW0 + 8192
        C0 = W0 + 16384
        cpos = [C0]

        def at(name, shape, dt, off):
            return nc.alloc_sbuf_tensor_at(name, shape, dt, offset=off, align_bytes=16)

        def const(name, cols, dt=F32):
            t = at(name, [128, cols], dt, cpos[0])
            cpos[0] += (cols * 4 + 31) // 32 * 32
            return t

        def pair(name, cols, off):
            return at(name + "_hi", [128, cols], F32R, off), at(name + "_lo", [128, cols], F32R, off + 4 * cols)

        def weights(name, cols, off):
            return *pair(name, cols, off), at(name + "_raw", [128, cols], F32, off + 4 * cols)

        def scratch(name, rows, cols, dt=F32):
            return nc.dram_tensor(name, [rows, cols], dt, kind="Internal").ap()

        def scratch_pair(name, rows, cols):
            return scratch(name + "_hi", rows, cols), scratch(name + "_lo", rows, cols)

        PS = ctx.enter_context(nc.psum_tensor("products", [128, 2, 1536], F32))
        PX = ctx.enter_context(nc.psum_tensor("small_products", [128, 2, 512], F32))

        T1 = at("work1", [128, 1024], F32, W0)
        T2 = at("work2", [128, 1024], F32, W0 + 4096)
        HI = at("stage_hi", [128, 1024], F32R, W0 + 8192)
        LO = at("stage_lo", [128, 1024], F32R, W0 + 12288)
        RAW = at("raw_slab", [128, 2, 1024], F32, RAW0)
        L = [pair(f"slab{b}", 1280, L0 + 10240 * b) for b in range(2)]
        ident = const("ident", 128)
        bq = const("bq_col", KT)
        bv = const("bv_col", KT)
        bqk = const("bqk_col", 16)
        b1 = const("b1_col", 16)
        b2 = const("b2_col", 16)
        n1w = const("norm1_col", KT)
        n2w = const("norm2_col", KT)
        stat6 = const("stat6", 12)
        mv = const("mean_var", 2)
        rstd = const("rstd", 1)
        mean_all = const("x1_mean", TT)
        rstd_all = const("x1_rstd", TT)
        dis = const("deg_inv_sqrt", TT)
        zr = const("z_recip", 2)
        small = const("small", 8)
        ksT_hi = const("ksum_col_hi", 2 * KT, F32R)
        ksT_lo = const("ksum_col_lo", 2 * KT, F32R)
        ones2 = const("ones2", 2)
        assert cpos[0] <= 229344, cpos[0]

        xnT = pair("xnT", KT * N, A0)
        wk = weights("wk", KT * D, B0)
        wg = weights("wg", KT * D, A0)
        kres = pair("k_resident", TT * D, B0)
        m1T = pair("m1T", KT * D, A0)
        wo = weights("wo", KT * D, B0)
        m3 = pair("m3", KT * D, A0 + 0)
        ksb = at("ksum_bcast", [128, D], F32, A0 + 65536)
        counts = at("counts", [128, TT, N], F32, A0)
        hres = pair("h_resident", TT * D, B0)
        rT = pair("rT", KT * N, A0)
        wv2 = weights("wv2", KT * D, B0)
        wo2 = weights("wo2", KT * D, A0)
        zT = pair("zT", KT * N, B0)
        w3 = weights("w3", 2 * KT * D, A0)
        cosT = at("cos", [128, N], F32, B0 + 65536)
        sinT = at("sin", [128, N], F32, B0 + 65536 + 5024)
        bias_a = at("bias_rows_a", [128, D], F32, A0 + 65536 + 4096)
        bias_b = at("bias_rows_b", [128, D], F32, B0 + 65536 + 12288)

        T3 = at("work3", [128, 1024], F32, B0 + 65536 + 10048)
        ones_r = at("ones_r", [128, 128], F32R, A0 + 65536 + 8192)

        XN = scratch_pair("xn_rows", N, D)
        XNT = scratch_pair("xn_cols", D, N)
        QT = scratch_pair("q_cols", D, N)
        KR = scratch_pair("k_rows", N, D)
        HR = scratch_pair("h_rows", N, D)
        M2T = scratch_pair("m2_cols", D, D)
        ACC = scratch("acc_rows", N, D, F32)
        X1 = scratch("x1_rows", N, D, F32)
        RT = scratch_pair("r_cols", D, N)
        QK = scratch_pair("qk_cols", 2 * D, N)
        VR = scratch("v_rows", N, HEADS * 128)
        AT = scratch_pair("att_cols", D, N)
        XY = scratch("xy_rows", N, D, F32)
        CTS = scratch("comb_cols", EXPERTS, N, F32)
        G = scratch_pair("g_cols", 2 * D, N)
        SORTED = scratch("sorted_rows", 128 * SC, 2)

        V, S, P, SP, TE = nc.vector, nc.scalar, nc.gpsimd, nc.sync, nc.tensor

        def nth(name, count):
            return before(name)[1] + count

        def begun(count):
            return not isinstance(count, int) or count > 0

        def apart(eng):
            eng.sem_inc(sem("apart"), 1)

        def rounds(eng, n):
            yield 0
            with eng.Fori(1, n) as i:
                yield i

        def product(out, lhs, rhs, kts, kp, m, chunks, rw, lw=None, last=True, come=None):
            lw = lw or m
            first, ins = True, None
            for kt in range(kts):
                if come:
                    come(kt)
                for l, rs in ((lhs[0], (rhs[0], rhs[1])), (lhs[1], (rhs[0],))):
                    for r in rs:
                        for off, n in chunks:
                            end = kt == kts - 1 and l is lhs[1] and last
                            ins = TE.matmul(out[0:m, off:off + n], l[0:kp, kt * lw:kt * lw + m],
                                            r[0:kp, kt * rw + off:kt * rw + off + n], start=first, stop=end)
                        first = False
            return ins

        ends = {}

        def enter(eng, ph):
            for name, value in ends[ph]:
                eng.wait_ge(sem(name), nth(name, value))

        def stage_ends(ph, n, per):
            return [(ph + "_mm", n), (ph + "_lo", n * per), (ph + "_st0", 32 * ((n * per + 1) // 2)),
                    (ph + "_st1", 32 * (n * per // 2))]

        ends["ln"] = [("ln_rt", TT), ("ln_st0", 16 * TT), ("ln_st1", 16 * TT)]
        ends["q"] = stage_ends("q", 8, 3)
        ends["k"] = stage_ends("k", 10, 2)
        ends["h"] = stage_ends("h", 10, 2)
        ends["m1"] = [("m1_mm", 8), ("m1_lo", 16)]
        ends["m2"] = stage_ends("m2", 8, 2)
        ends["m3"] = [("m3_mm", 8), ("m3_lo", 16), ("ks_col", 1)]
        ends["mix"] = [("mix_mm", 10), ("mix_v", 20), ("mix_st0", 160), ("mix_st1", 160)]
        ends["adj"] = [("adj_ev", GRANULES)]
        ends["deg"] = [("deg_scaled", 1)]
        ends["gnn"] = [("gnn_mm", 10), ("gnn_rt", 10), ("gnn_st", 320), ("gnn_sx", 160)]
        ends["qk"] = stage_ends("qk", 16, 3)
        ends["v"] = stage_ends("v", 10, 2)
        ends["att"] = [("att_pv", 80), ("att_olo", 80), ("att_st0", 32 * 40), ("att_st1", 32 * 40)]
        ends["op"] = [("op_mm", 10), ("op_rt", 10), ("op_st", 160)]
        ends["gate"] = [("gate_ct", TT), ("gate_st", 16)]
        ends["ex"] = [("ex_mm", 32), ("ex_lo", 48), ("ex_st0", 32 * 24), ("ex_st1", 32 * 24)]

        def copy_words(eng, out, in_):
            ap = [v.bitcast(F32) if v.dtype == F32R else v for v in (out, in_)]
            return eng.dma_start(ap[0], ap[1])

        ln_stage = [(at("xn_hi", [128, D], F32R, L0 + 10240), at("xn_lo", [128, D], F32R, L0 + 14336)), (HI, LO)]

        def store_xn(sp, t):
            sp.wait_ge(sem("ln_lo"), nth("ln_lo", t + 1))
            for part in (0, 1):
                copy_words(sp, XN[part][t * TP:(t + 1) * TP, :], ln_stage[t % 2][part][0:TP, :])\
                    .then_inc(sem(f"ln_st{t % 2}"), 16)

        def store_xnT(sp, t0, t1):
            if begun(t1):
                sp.wait_ge(sem("ln_rt"), nth("ln_rt", t1))
            for part in (0, 1):
                copy_words(sp, XNT[part].rearrange("(k p) c -> p k c", p=128)[:, :, t0 * TP:t1 * TP],
                             xnT[part][:, :].rearrange("p (k c) -> p k c", k=KT)[:, :, t0 * TP:t1 * TP])\
                    .then_inc(sem("xnT_stored"), 16)

        def fetch_raw(eng, ph, src, dst, pieces):
            per = pieces // 4
            for q in range(4):
                copy_words(eng, dst[2][:, q * per * D:(q + 1) * per * D].rearrange("p (k c) -> p k c", k=per),
                           src.rearrange("(k p) c -> p k c", p=128)[:, q * per:(q + 1) * per, :])\
                    .then_inc(sem(f"{ph}_rr{q}"), 16)

        def store_tile_pair(sp, dst, t, name):
            for part, buf in ((0, HI), (1, LO)):
                copy_words(sp, dst[part].rearrange("(k p) c -> p k c", p=128)[:, :, t * TP:(t + 1) * TP],
                             buf[:, 0:KT * TP].rearrange("p (k c) -> p k c", k=KT)).then_inc(sem(name), 16)

        def row_stream(sp, ph, load, rows_in, rows_out, first=None):
            def rows(s, c):
                copy_words(sp, T2[0:TP, 512 * c:512 * c + 512], rows_in[bass.ds(s * TP, TP), 512 * c:512 * c + 512])\
                    .then_inc(sem(f"{ph}_in{c}"), 16)

            def sums(s, c):
                copy_words(sp, rows_out[bass.ds(s * TP, TP), 512 * c:512 * c + 512], T1[0:TP, 512 * c:512 * c + 512])\
                    .then_inc(sem(f"{ph}_st{c}"), 16)

            def step(s, b):
                if b is not None:
                    if begun(s + 0):
                        sp.wait_ge(sem(ph + "_mm"), nth(ph + "_mm", s + 0))
                    load(s + 1, b)
                for c in (0, 1):
                    sp.wait_ge(sem(ph + "_v"), nth(ph + "_v", 2 * (s - 1) + (c + 1)))
                    rows(s, c)
                    sums(s - 1, c)
            for c in (0, 1):
                rows(0, c)
            if first:
                first()
            with sp.Fori(0, TT // 2 - 1) as i:
                for b in (0, 1):
                    step(2 * i + (b + 1), b)
            step(TT - 1, None)
            for c in (0, 1):
                sp.wait_ge(sem(ph + "_v"), nth(ph + "_v", 2 * (TT - 1) + (c + 1)))
                sums(TT - 1, c)

        EX1 = B0 + 65536
        nb = [at(f"norm{b}", [128, D], F32, EX1 + 4096 * b) for b in range(2)]
        tv = at("transposed", [128, KT * TP], F32, EX1 + 8192)
        EX2 = A0 + 80000 - 16384
        nb9 = [at(f"rnorm{b}", [128, D], F32, EX2 + 4096 * b) for b in range(2)]
        tv9 = at("rtransposed", [128, KT * TP], F32, EX2 + 8192)
        u9 = at("u_rows", [128, D], F32, EX2 + 12288)
        EX3 = A0 + 65536
        nb13 = [at("znorm0", [128, D], F32, EX3), at("znorm1", [128, D], F32, W0 + 8192)]
        x_op = [T2, at("work2_other", [128, 1024], F32, W0 + 12288)]
        tv13 = at("ztransposed", [128, KT * TP], F32, EX3 + 4096)
        bias_a2 = at("bias_rows_a2", [128, D], F32, EX3 + 8192)
        SA = A0 + 65536 + 8192 + 512
        edge_row = at("edge_row", [128, EC], I32, SA)
        edge_pair = at("edge_pair", [128, EC, 2], F32, SA + 704)
        below = at("below", [128, 128], F32, SA + 704 + 1376)
        sorted_e = at("sorted_edges", [128, SC, 2], F32, SA + 2592)
        gran_at = at("granule_columns", [128, GRANULES], I32, SA + 2592 + 8 * SC)
        gran_no = at("granule_number", [128, GRANULES], F32, SA + 2592 + 8 * SC + 4 * GRANULES)
        SM = SA + 2592 + 8 * SC + 8 * GRANULES
        tile_n, gran_f, gran_sum, gran_start, tile_off = [at(f"tile_{k}", [128, TT], F32, SM + 48 * k) for k in range(5)]
        gran_i = at("tile_granules_i", [128, 2, TT], I32, SM + 240)
        assert SM + 320 <= A0 + 80000
        SX = B0 + 65536
        reached = at("reached", [128, TT + 1, EC], F16, SX)
        member = at("member", [128, TT, EC], F16, SX + 3744)
        rank = at("rank", [128, TT, EC], F16, SX)
        edge_src_i, edge_dst_i, edge_pos_i, edge_col_i, edge_part_i = \
            [at(f"edge_i{k}", [128, EC], I32, SX + 7168 + 704 * k) for k in range(5)]
        edge_dst = at("edge_dst", [128, EC], F32, SX + 7168 + 704 * 5)
        edge_tile = at("edge_tile", [128, EC], F32, SX + 7168 + 704 * 6)
        assert 7168 + 704 * 7 <= 12288
        place = at("place", [128, TT, EC], F32, W0)
        edge_pos, edge_col = [at(f"edge_f{k}", [128, EC], F32, W0 + 6816 + 704 * k) for k in range(2)]
        gran_ge = at("granule_reached", [128, TT - 1, GRANULES], F32, W0 + 8256)
        AD = A0 + 50016 + (-(A0 + 50016)) % 32
        iota = at("iota", [128, N], F16, AD)
        oh_src = at("onehot_src", [128, GC, N], F16, AD + 2528)
        oh_dst = at("onehot_dst", [128, GC, 128], F16, AD + 2528 + 2528 * GC)
        distance = at("distance", [128, N], F16, W0)
        neg_src = at("minus_source", [128, SC], F32, W0 + 2528)
        count_sum = at("count_sum", [128, N], F32, W0 + 4096)
        assert AD + 2528 * (GC + 1) + 256 * GC <= SA
        q_st = [at(f"q_stack{b}", [128, N], F32R, A0 + 5024 * b) for b in range(2)]
        k_st = [[at(f"k_stack{b}{p}", [128, N], F32R, A0 + 5024 * (2 + 2 * b + p)) for p in range(2)] for b in range(2)]
        v_st = [at(f"v_stack{b}", [128, TT * 128], F32R, A0 + 5024 * 6 + 5120 * b) for b in range(2)]
        A1 = A0 + 5024 * 6 + 10240
        prob = [at(f"prob{b}", [128, N], F32, A1 + 5024 * b) for b in range(4)]
        B1 = B0
        pT = [pair(f"pT{b}", TT * 250, B1 + 20000 * b) for b in range(2)]
        AC = B1 + 40000
        o_tmp = at("o_tmp", [128, 512], F32, AC)
        o_sum = at("o_sum", [128, 512], F32, AC + 2048)
        o_hi = at("o_hi", [128, 512], F32R, AC + 4096)
        o_lo = at("o_lo", [128, 512], F32R, AC + 6144)
        mx = at("att_max", [128, 2], F32, AC + 8192)
        nmx = at("att_negmax", [128, 2], F32, AC + 8224)
        rs = at("att_sum", [128, 2], F32, AC + 8256)
        rr = at("att_rsum", [128, 2], F32, AC + 8288)
        combB = at("comb_bcast", [128, EXPERTS, N], F32, A0)
        combT = at("combT", [128, N], F32, A0 + 40032)
        logT = at("logitsT", [128, N], F32, A0 + 45056)
        lg = at("logits", [128, 8], F32, A0 + 50112)
        m8 = at("top8", [128, 8], F32, A0 + 50144)
        top_i = at("top_index", [128, 8], mybir.dt.uint32, A0 + 50176)
        top_f = at("top_index_f", [128, 8], F32, A0 + 50208)
        eight = at("expert_number", [128, 8], F32, A0 + 54608)
        mask = at("mask", [128, 8], F32, A0 + 50240)
        ex8 = at("exp8", [128, 8], F32, A0 + 50272)
        nm1 = at("neg_top", [128, 8], F32, A0 + 50304)
        comb = at("comb", [128, TT, 8], F32, A0 + 50336)
        silu = [at(f"silu{j}", [128, N], F32, A0 + 54656 + 5024 * j) for j in range(2)]
        LG = [pair(f"gslab{b}", 16 * TP, A0 + 131072 + 16000 * b) for b in range(2)]
        ct_tile = [at(f"ct_tile{b}", [128, 128], F32, A0 + 131072 + 32000 + 512 * b) for b in range(2)]
        b3r = at("b3_rows", [128, D], F32, A0 + 131072 + 33024)
        assert A0 + 131072 + 33024 + 4096 <= RAW0

        NT = 2 * TT
        GROUPS = {"c": (8, 10), "b": (4, 8), "a": (0, 4)}

        def due(r, j):
            return j < NT and (j >= 0 or not isinstance(r, int))

        def windows(eng, window):
            for r in rounds(eng, HEADS // 2):
                for j in range(0, NT, 2):
                    window(r, j)
            for j in range(NT, NT + 8, 2):
                window(HEADS // 2 - 1, j)

        def group_bank(g, b, k):
            if g == "c":
                return PS[0:TP, b, 1250 + k * TP:1250 + k * TP + TP]
            return PX[0:TP, "ab".index(g), k * TP:k * TP + TP]

        def group_read(g, b):
            k0, k1 = GROUPS[g]
            v = PS[0:TP, b, 1250:1500] if g == "c" else PX[0:TP, "ab".index(g), 0:4 * TP]
            return v.rearrange("p (k c) -> p k c", k=k1 - k0)

        def pT_part(pb, part, g, j):
            k0, k1 = GROUPS[g]
            return pT[pb][part][0:TP, :].rearrange("p (k c) -> p k c", k=TT)[:, k0:k1, (j % 2) * TP:(j % 2) * TP + TP]

        block = ctx.enter_context(nc.Block())

        @block.sync
        def _(sp):
            def load_slab_raw(ph, src, s, b):
                copy_words(sp, RAW[:, b, :], src[s].rearrange("p k m -> p (k m)")).then_inc(sem(f"{ph}_raw{b}"), 16)

            def load_slab(ph, src, s, b, kts, kp, m):
                for part in (0, 1):
                    v = src[part].rearrange("(k p) c -> p k c", p=kp)[:, :, bass.ds(s * m, m)]
                    copy_words(sp, L[b][part][0:kp, 0:kts * m].rearrange("p (k c) -> p k c", k=kts), v)\
                        .then_inc(sem(f"{ph}_slab{b}"), 16)

            def stream(ph, n, load, store, chunks, used="_mm", ahead=None, late=None):
                per = len(chunks)

                def store_slab(s, b):
                    for c in range(per):
                        q = per * b + c
                        sp.wait_ge(sem(ph + "_lo"), nth(ph + "_lo", s * per + c + 1))
                        store(s, c, q % 2)

                with sp.Fori(0, n // 2 - 1) as i:
                    for b in (0, 1):
                        sp.wait_ge(sem(ph + used), nth(ph + used, 2 * i + b + 1))
                        load(2 * i + b + 2, b)
                        if store:
                            store_slab(2 * i + b, b)
                if late:
                    late()
                for b in (0, 1):
                    if ahead:
                        if begun(n - 1 + b):
                            sp.wait_ge(sem(ph + "_mm"), nth(ph + "_mm", n - 1 + b))
                        ahead(b)
                    if store:
                        store_slab(n - 2 + b, b)

            def store_pair(ph, dst, rows, chunks, p):
                def go(s, c, h):
                    off, n = chunks[c]
                    for part, buf in ((0, HI), (1, LO)):
                        copy_words(sp, dst[part][bass.ds(s * rows, rows), off:off + n],
                                     buf[0:rows, 512 * h:512 * h + n]).then_inc(sem(f"{ph}_st{h}"), 16)
                return go

            for t, k in ((bq, "bq"), (bv, "bv"), (bqk, "bqk"), (b1, "b1"), (b2, "b2"), (n1w, "n1"), (n2w, "n2"),
                         (ident, "ident")):
                copy_words(sp, t[:, :], io[k]).then_inc(sem("consts"), 16)
            for t in range(TT + 2):
                if t < TT:
                    b = t % 2
                    if t >= 2:
                        if begun(t - 1):
                            sp.wait_ge(sem("ln_nb"), nth("ln_nb", t - 1))
                    copy_words(sp, [T1, T2][b][0:TP, :], io["x"][t * TP:(t + 1) * TP, :]).then_inc(sem(f"ln_x{b}"), 16)
                if t == 1:
                    fetch_raw(sp, "k", io["Wk"], wk, 8)
                if t >= 2:
                    store_xn(sp, t - 2)
                if t == TT // 2 + 3:
                    store_xnT(sp, 0, TT // 2)
            def raw_q(s, b):
                load_slab_raw("q", io["Wq"], s, b)

            def slab_k(s, b):
                load_slab("k", XNT, s, b, KT, 128, TP)

            def slab_h(s, b):
                load_slab("h", XNT, s, b, KT, 128, TP)

            def slab_m1(s, b):
                load_slab("m1", XN, s, b, TT, TP, 128)

            def raw_m2(s, b):
                load_slab_raw("m2", io["Wv"], s, b)

            def slab_mix(s, b):
                load_slab("mix", QT, s, b, KT, 128, TP)

            def rows_resident(src, dst, t, name):
                for part in (0, 1):
                    cols = slice(t * D, t * D + D) if isinstance(t, int) else bass.ds(t * D, D)
                    copy_words(sp, dst[part][0:TP, cols], src[part][bass.ds(t * TP, TP), :]).then_inc(sem(name), 16)

            for b in (0, 1):
                raw_q(b, b)
            store_xnT(sp, TT // 2, TT)
            copy_words(sp, bias_b[0:TP, :], io["bk"].partition_broadcast(TP)).then_inc(sem("k_bias"), 16)
            stream("q", 8, raw_q, store_pair("q", QT, 128, CH_N, 128), CH_N, "_split", lambda b: slab_k(b, b),
                   lambda: sp.wait_ge(sem("xnT_stored"), nth("xnT_stored", 64)))
            for k, t in (("src", edge_src_i), ("dst", edge_dst_i)):
                copy_words(sp, t[0:TP, :], io[k].rearrange("(p c) -> p c", p=TP)).then_inc(sem("edges"), 16)
            copy_words(sp, below[:, :], io["below"]).then_inc(sem("edges"), 16)
            copy_words(sp, bias_a[0:TP, :], io["bg"].partition_broadcast(TP)).then_inc(sem("g_bias"), 16)
            fetch_raw(sp, "h", io["Wg"], wg, 8)
            stream("k", 10, slab_k, store_pair("k", KR, TP, CH_D, TP), CH_D, ahead=lambda b: slab_h(b, b))
            enter(sp, "k")
            sp.wait_ge(sem("sort_ready"), nth("sort_ready", 1))
            copy_words(sp, SORTED.rearrange("(p c) e -> p (c e)", p=128), sorted_e[:, :, :].rearrange("p c e -> p (c e)"))\
                .then_inc(sem("sorted_blank"), 16)

            def slab_h_and_keys(s, b):
                slab_h(s, b)
                rows_resident(KR, kres, s, "m1_full")
            for t in (0, 1):
                rows_resident(KR, kres, t, "m1_full")
            stream("h", 10, slab_h_and_keys, store_pair("h", HR, TP, CH_D, TP), CH_D, ahead=lambda b: slab_m1(b, b))
            stream("m1", 8, slab_m1, None, CH_D)
            for b in (0, 1):
                raw_m2(b, b)
            enter(sp, "m1")
            fetch_raw(sp, "m3", io["Wo"], wo, 8)
            stream("m2", 8, raw_m2, store_pair("m2", M2T, 128, CH_D, 128), CH_D, "_split")
            enter(sp, "m2")

            def slab_m3(s, b):
                load_slab("m3", M2T, s, b, KT, 128, 128)
            for b in (0, 1):
                slab_m3(b, b)
            stream("m3", 8, slab_m3, None, CH_D, ahead=lambda b: slab_mix(b, b))
            enter(sp, "h")

            def slab_mix_and_h(s, b):
                slab_mix(s, b)
                rows_resident(HR, hres, s, "gnn_full")

            def mix_first():
                copy_words(sp, bias_a[0:TP, :], io["bo"].partition_broadcast(TP)).then_inc(sem("o_bias"), 16)
                for t in (0, 1):
                    rows_resident(HR, hres, t, "gnn_full")
            row_stream(sp, "mix", slab_mix_and_h, io["x"], ACC, mix_first)
            sp.wait_ge(sem("scattered"), nth("scattered", 16 * EC))
            copy_words(sp, sorted_e[:, :, :].rearrange("p c e -> p (c e)"),
                       SORTED.rearrange("(p c) e -> p (c e)", p=128)).then_inc(sem("sorted_in"), 16)
            enter(sp, "deg")

            def rt_part(name, part, k0, k1, c0, c1):
                copy_words(sp, rT[part][:, :].rearrange("p (k c) -> p k c", k=KT)[:, k0:k1, c0:c1],
                           RT[part].rearrange("(k p) c -> p k c", p=128)[:, k0:k1, c0:c1]).then_inc(sem(name), 16)
            early = 7
            for t in range(TT + 2):
                if t < TT:
                    if t >= 1:
                        if begun(t):
                            sp.wait_ge(sem("gnn_x1"), nth("gnn_x1", t))
                    copy_words(sp, T2[0:TP, :], ACC[t * TP:(t + 1) * TP, :]).then_inc(sem("gnn_acc"), 16)
                    if t == early + 2:
                        sp.wait_ge(sem("gnn_slab"), nth("gnn_slab", TT))
                        if begun(32 * early):
                            sp.wait_ge(sem("gnn_st"), nth("gnn_st", 32 * early))
                        rt_part("qk_early", 0, 0, KT, 0, early * TP)
                        rt_part("qk_early", 1, 0, KT // 2, 0, early * TP)
                    sp.wait_ge(sem("gnn_x1"), nth("gnn_x1", t + 1))
                    copy_words(sp, X1[t * TP:(t + 1) * TP, :], T1[0:TP, :]).then_inc(sem("gnn_sx"), 16)
                if t >= 2:
                    if begun(t - 1):
                        sp.wait_ge(sem("gnn_rt"), nth("gnn_rt", t - 1))
                    store_tile_pair(sp, RT, t - 2, "gnn_st")
            def raw_qk(s, b):
                load_slab_raw("qk", io["Wqk"], s, b)
            for b in (0, 1):
                raw_qk(b, b)
            enter(sp, "gnn")
            for part in (0, 1):
                rt_part("qk_half", part, 0, KT // 2, early * TP, N)
            rt_part("qk_full", 0, KT // 2, KT, early * TP, N)
            rt_part("qk_full", 1, KT // 2, KT, 0, N)
            for t, k in ((cosT, "cos"), (sinT, "sin")):
                copy_words(sp, t[:, :], io[k]).then_inc(sem("rope_tables"), 16)
            def slab_v(s, b):
                load_slab("v", RT, s, b, KT, 128, TP)
            fetch_raw(sp, "v", io["Wv2"], wv2, 8)
            stream("qk", 16, raw_qk, store_pair("qk", QK, 128, CH_N, 128), CH_N, "_split", lambda b: slab_v(b, b))
            copy_words(sp, bias_a[0:TP, :], io["bv2"].partition_broadcast(TP)).then_inc(sem("v2_bias"), 16)

            def store_v(s, c, h):
                for part, buf in ((0, HI), (1, LO)):
                    dst = VR.rearrange("t (h e d) -> t h e d", h=HEADS, e=2)[bass.ds(s * TP, TP), 8 * c:8 * c + 8, part, :]
                    copy_words(sp, dst, buf[0:TP, 512 * h:512 * h + 512].rearrange("t (h d) -> t h d", h=8))\
                        .then_inc(sem(f"v_st{h}"), 16)
            stream("v", 10, slab_v, store_v, CH_D)
            enter(sp, "v")

            def load_head(h, b):
                for part in (0, 1):
                    half = slice(64 * part, 64 * part + 64)
                    copy_words(sp, q_st[b][half, :], QK[part][bass.ds(h * HD, HD), :]).then_inc(sem(f"head{b}"), 16)
                    for dup in (0, 1):
                        copy_words(sp, k_st[b][part][64 * dup:64 * dup + 64, :],
                                     QK[part][bass.ds(h * HD + D, HD), :]).then_inc(sem(f"head{b}"), 16)
                copy_words(sp, v_st[b][0:TP, :].rearrange("p (k c) -> p k c", k=TT),
                             VR.rearrange("(k p) c -> p k c", p=TP)[:, :, bass.ds(h * 128, 128)])\
                    .then_inc(sem(f"head{b}"), 16)

            def store_out(h, hb, g):
                pb = (hb * 5 + g) % 2
                sp.wait_ge(sem("att_olo"), nth("att_olo", h * 5 + g + 1))
                for part, buf in ((0, o_hi), (1, o_lo)):
                    copy_words(sp, AT[part][bass.ds(h * HD, HD), 250 * g:250 * g + 250],
                                 buf[0:64, 250 * pb:250 * pb + 250]).then_inc(sem(f"att_st{pb}"), 16)
            load_head(0, 0)
            load_head(1, 1)
            with sp.Fori(0, HEADS // 2 - 1) as i:
                for b in (0, 1):
                    for g in range(5):
                        store_out(2 * i + b, b, g)
                    sp.wait_ge(sem("att_pv"), nth("att_pv", (2 * i + b + 1) * 5))
                    load_head(2 * i + b + 2, b)
            for b in (0, 1):
                for g in range(5):
                    store_out(HEADS - 2 + b, b, g)
            enter(sp, "att")
            load_slab("op", AT, 0, 0, KT, 128, TP)
            fetch_raw(sp, "op", io["Wo2"], wo2, 8)
            copy_words(sp, bias_a2[0:TP, :], io["ob"].partition_broadcast(TP)).then_inc(sem("ob_bias"), 16)

            def load_x1(t):
                copy_words(sp, x_op[t % 2][0:TP, :], X1[t * TP:(t + 1) * TP, :]).then_inc(sem(f"op_x1{t % 2}"), 16)
            load_x1(0)
            for t in range(TT):
                if t + 1 < TT:
                    if t >= 1:
                        if begun(t):
                            sp.wait_ge(sem("op_mm"), nth("op_mm", t))
                    load_slab("op", AT, t + 1, (t + 1) % 2, KT, 128, TP)
                    if t >= 1:
                        if begun(16 * t):
                            sp.wait_ge(sem("op_st"), nth("op_st", 16 * t))
                    load_x1(t + 1)
                sp.wait_ge(sem("op_xy"), nth("op_xy", t + 1))
                copy_words(sp, XY[t * TP:(t + 1) * TP, :], x_op[t % 2][0:TP, :]).then_inc(sem("op_st"), 16)
            copy_words(sp, RAW[:, 0, :], io["gate"].rearrange("p k m -> p (k m)")).then_inc(sem("gate_raw0"), 16)
            load_slab_raw("ex", io["W12"], 1, 1)
            sp.wait_ge(sem("gate_split"), nth("gate_split", 1))
            load_slab_raw("ex", io["W12"], 0, 0)

            def spread_comb():
                sp.wait_ge(sem("gate_ct"), nth("gate_ct", TT))
                copy_words(sp, CTS, combT[0:EXPERTS, :]).then_inc(sem("gate_st"), 16)
                sp.wait_ge(sem("gate_st"), nth("gate_st", 16))
                for e in range(EXPERTS):
                    copy_words(sp, combB[:, e, :], CTS[e:e + 1, :].rearrange("a c -> (a c)").partition_broadcast(128))\
                        .then_inc(sem("comb_in" if e else "comb_first"), 16)

            def store_g(r, c, h):
                off, n = CH_N[c]
                for part, buf in ((0, HI), (1, LO)):
                    copy_words(sp, G[part][bass.ds(r * 128, 128), off:off + n],
                                 buf[:, 512 * h:512 * h + n]).then_inc(sem(f"ex_st{h}"), 16)

            def store_expert(e):
                for j in range(2):
                    for c in range(3):
                        sp.wait_ge(sem("ex_lo"), nth("ex_lo", e * 6 + 3 * j + c + 1))
                        store_g(2 * e + j, c, (3 * j + c) % 2)
            for e in rounds(sp, EXPERTS - 1):
                for j in range(2):
                    for b in (0, 1):
                        sp.wait_ge(sem("ex_split"), nth("ex_split", e * 4 + 2 * j + b + 1))
                        load_slab_raw("ex", io["W12"], e * 4 + 2 * j + b + 2, b)
                    if isinstance(e, int) and j == 0:
                        spread_comb()
                    for c in range(3):
                        sp.wait_ge(sem("ex_lo"), nth("ex_lo", e * 6 + 3 * j + c + 1))
                        store_g(2 * e + j, c, (3 * j + c) % 2)
            for b in (0, 1):
                sp.wait_ge(sem("ex_split"), nth("ex_split", 4 * EXPERTS - 4 + b + 1))
                load_slab_raw("ex", io["W12"], 4 * EXPERTS - 4 + b + 2, b)
            store_expert(EXPERTS - 1)
            enter(sp, "ex")


            def load_g(s, b):
                for part in (0, 1):
                    copy_words(sp, LG[b][part][:, :].rearrange("p (k c) -> p k c", k=16),
                                 G[part].rearrange("(k p) c -> p k c", p=128)[:, :, bass.ds(s * TP, TP)])\
                        .then_inc(sem(f"w3_slab{b}"), 16)
                copy_words(sp, ct_tile[b][0:EXPERTS, 0:TP], CTS[:, bass.ds(s * TP, TP)]).then_inc(sem(f"w3_slab{b}"), 16)
            load_g(0, 0)
            fetch_raw(sp, "w3", io["W3"], w3, 16)
            load_g(1, 1)
            row_stream(sp, "w3", load_g, XY, io["out"])
            sp.wait_ge(sem("w3_st0"), nth("w3_st0", 160))
            sp.wait_ge(sem("w3_st1"), nth("w3_st1", 160))

        @block.gpsimd
        def _(pool):
            def split_piece(ph, dst, j):
                cols = slice(j * D, (j + 1) * D) if isinstance(j, int) else bass.ds(j * D, D)
                P.tensor_copy(dst[0][:, cols], dst[2][:, cols]).then_inc(sem(ph + "_rh"), 1)
                pool.wait_ge(sem(ph + "_rh"), nth(ph + "_rh", j + 1))
                apart(pool)
                P.tensor_tensor(dst[1][:, cols], dst[2][:, cols], dst[0][:, cols].bitcast(F32),
                                ALU.subtract).then_inc(sem(ph + "_res"), 1)

            def split_slabs(ph, n, behind=None):
                for r in rounds(pool, n // 2):
                    for b in (0, 1):
                        pool.wait_ge(sem(f"{ph}_raw{b}"), nth(f"{ph}_raw{b}", 16 * r + 16))
                        if begun(2 * r + b - 1):
                            pool.wait_ge(sem(ph + "_mm"), nth(ph + "_mm", 2 * r + b - 1))
                        apart(pool)
                        P.tensor_copy(L[b][0][:, 0:1024], RAW[:, b, :]).then_inc(sem(ph + "_sh"), 1)
                        pool.wait_ge(sem(ph + "_sh"), nth(ph + "_sh", 2 * r + b + 1))
                        P.tensor_tensor(L[b][1][:, 0:1024], RAW[:, b, :], L[b][0][:, 0:1024].bitcast(F32),
                                        ALU.subtract).then_inc(sem(ph + "_split"), 1)
                    if behind:
                        behind(r)

            for j in range(KT):
                pool.wait_ge(sem(f"k_rr{j // 2}"), nth(f"k_rr{j // 2}", 16))
                split_piece("k", wk, j)
            if begun(16 * TT):
                pool.wait_ge(sem("ln_st0"), nth("ln_st0", 16 * TT))
            split_slabs("q", 8)
            enter(pool, "q")
            P.iota(gran_no[:, :], [[1, GRANULES]], base=0, channel_multiplier=0, allow_small_or_imprecise_dtypes=True)\
                .then_inc(sem("gran_iota"), 1)
            for j in range(KT):
                pool.wait_ge(sem(f"h_rr{j // 2}"), nth(f"h_rr{j // 2}", 16))
                split_piece("h", wg, j)
            pool.wait_ge(sem("m1_mm"), nth("m1_mm", 8))
            split_slabs("m2", 8)
            pool.wait_ge(sem("sort_ready"), nth("sort_ready", 1))
            pool.wait_ge(sem("sorted_blank"), nth("sorted_blank", 16))
            for c in range(EC):
                pool.indirect_dma_start(SORTED, bass.IndirectOffsetOnAxis(ap=edge_row[0:TP, c:c + 1], axis=0),
                                        edge_pair[0:TP, c, :], None).then_inc(sem("scattered"), 16)
            enter(pool, "mix")
            P.iota(iota[:, :], [[1, N]], base=0, channel_multiplier=0, allow_small_or_imprecise_dtypes=True)\
                .then_inc(sem("iota"), 1)
            P.memset(counts[:, TT // 2:, :], 0.0).then_inc(sem("counts_zero"), 1)
            pool.wait_ge(sem("gnn_mm"), nth("gnn_mm", 10))

            def wv2_piece(r):
                if isinstance(r, int):
                    for q in range(4):
                        pool.wait_ge(sem(f"v_rr{q}"), nth(f"v_rr{q}", 16))
                split_piece("v", wv2, r)
            split_slabs("qk", 16, wv2_piece)
            enter(pool, "v")
            for r in rounds(pool, HEADS // 2):
                for j in range(2 * TT):
                    b = j % 2
                    t = r * (2 * TT) + j
                    pool.wait_ge(sem("att_rr"), nth("att_rr", t + 1))
                    apart(pool)
                    P.tensor_scalar(prob[j % 4][0:TP, :], prob[j % 4][0:TP, :], rr[0:TP, b:b + 1], 1.0, ALU.mult, ALU.mult)\
                        .then_inc(sem("att_norm"), 1)
            enter(pool, "att")
            pool.wait_ge(sem("op_mm"), nth("op_mm", 10))
            P.iota(eight[:, :], [[1, 8]], base=0, channel_multiplier=0, allow_small_or_imprecise_dtypes=True)\
                .then_inc(sem("gate_iota"), 1)
            pool.wait_ge(sem("gate_raw0"), nth("gate_raw0", 16))
            P.tensor_copy(L[0][0][:, 0:1024], RAW[:, 0, :]).then_inc(sem("gate_sh"), 1)
            pool.wait_ge(sem("gate_sh"), nth("gate_sh", 1))
            P.tensor_tensor(L[0][1][:, 0:1024], RAW[:, 0, :], L[0][0][:, 0:1024].bitcast(F32),
                            ALU.subtract).then_inc(sem("gate_split"), 1)
            pool.wait_ge(sem("gate_mm"), nth("gate_mm", 1))
            for r in rounds(pool, EXPERTS):
                for j in range(2):
                    for b in (0, 1):
                        pool.wait_ge(sem(f"ex_raw{b}"), nth(f"ex_raw{b}", 32 * r + 16 * j + 16))
                        if begun(4 * r + 2 * j + b - 1):
                            pool.wait_ge(sem("ex_mm"), nth("ex_mm", 4 * r + 2 * j + b - 1))
                        apart(pool)
                        P.tensor_copy(L[b][0][:, 0:1024], RAW[:, b, :]).then_inc(sem("ex_sh"), 1)
                        pool.wait_ge(sem("ex_sh"), nth("ex_sh", 4 * r + 2 * j + b + 1))
                        P.tensor_tensor(L[b][1][:, 0:1024], RAW[:, b, :], L[b][0][:, 0:1024].bitcast(F32),
                                        ALU.subtract).then_inc(sem("ex_split"), 1)
            enter(pool, "ex")
            pool.dma_start(b3r[0:EXPERTS, :], io["b3"]).then_inc(sem("b3_in"), 16)

        @block.tensor
        def _(pe):
            def slabs(ph, n, slab_unit, kts, kp, m, rhs, rw, chunks, per_ev, ev, split, prev=None, come=None, after_first=None):
                for r in rounds(pe, n // 2):
                    for b in (0, 1):
                        if split:
                            pe.wait_ge(sem(ph + "_split"), nth(ph + "_split", 2 * r + b + 1))
                        else:
                            pe.wait_ge(sem(f"{ph}_slab{b}"), nth(f"{ph}_slab{b}", slab_unit * r + slab_unit))
                        if begun(per_ev * (2 * r + b - 1)):
                            pe.wait_ge(sem(ph + ev), nth(ph + ev, per_ev * (2 * r + b - 1)))
                        start = isinstance(r, int)
                        if prev and start:
                            if begun(prev[1] - (1 - b) * prev[2]):
                                pe.wait_ge(sem(prev[0]), nth(prev[0], prev[1] - (1 - b) * prev[2]))
                        ins = product(PS[:, b, :], L[b], rhs, kts, kp, m, chunks, rw,
                                      come=come if start and b == 0 else None)
                        ins.then_inc(sem(ph + "_mm"), 1)
                        if after_first and start and b == 0:
                            after_first()

            def made(signal, per):
                def come(kt):
                    if begun(per * (kt + 1)):
                        pe.wait_ge(sem(signal), nth(signal, per * (kt + 1)))
                return come

            pe.wait_ge(sem("consts"), nth("consts", 16 * 8))

            def transposes(ph, src, t):
                pe.wait_ge(sem(ph + "_nb"), nth(ph + "_nb", t + 1))
                if begun(t):
                    pe.wait_ge(sem(ph + "_tv"), nth(ph + "_tv", t))
                for f in range(KT):
                    ins = TE.transpose(PX[:, f // 4, (f % 4) * TP:(f % 4) * TP + TP],
                                       src[0:TP, f * 128:f * 128 + 128], ident[0:TP, 0:TP])
                ins.then_inc(sem(ph + "_tr"), 1)
            for t in range(TT):
                transposes("ln", nb[t % 2], t)
            pe.wait_ge(sem("ln_rt"), nth("ln_rt", TT))
            slabs("q", 8, 0, KT, 128, 128, xnT, N, CH_N, 3, "_psf", True)
            def sort_sums():
                pe.wait_ge(sem("edges"), nth("edges", 48))
                pe.wait_ge(sem("sort_tile_n"), nth("sort_tile_n", 1))
                TE.matmul(PX[0:TP, 0, 0:TT], below[0:TP, 0:TP], tile_n[0:TP, :], start=True, stop=True)
                TE.matmul(PX[0:TP, 1, 0:TT], ones_r[0:TP, 0:TP].bitcast(F32), tile_n[0:TP, :], start=True, stop=True)\
                    .then_inc(sem("sort_sums"), 1)
            slabs("k", 10, 32, KT, 128, TP, wk, D, CH_D, 2, "_psf", False, ("q_psf", 24, 3), made("k_res", 1),
                  sort_sums)
            slabs("h", 10, 32, KT, 128, TP, wg, D, CH_D, 2, "_val", False, ("k_psf", 20, 2), made("h_res", 1))
            pe.wait_ge(sem("h_val"), nth("h_val", 20))
            if begun(32 * TT):
                pe.wait_ge(sem("m1_full"), nth("m1_full", 32 * TT))
            pe.wait_ge(sem("ones_ready"), nth("ones_ready", 1))
            for off, n in CH_D:
                for kt in range(TT):
                    for part in (0, 1):
                        ins = TE.matmul(PS[:, 0, off:off + n], ones_r[0:TP, :], kres[part][0:TP, kt * D + off:kt * D + off + n],
                                        start=kt == 0 and part == 0, stop=kt == TT - 1 and part == 1)
            ins.then_inc(sem("ks_mm"), 1)
            pe.wait_ge(sem("ks_v"), nth("ks_v", 1))
            slabs("m1", 8, 32, TT, TP, 128, kres, D, CH_D, 2, "_lo", False)
            slabs("m2", 8, 0, KT, 128, 128, m1T, D, CH_D, 2, "_val", True, ("m1_lo", 16, 2), made("m1_lo", 2))
            for f in range(KT):
                ins = TE.transpose(PX[:, f // 4, (f % 4) * 128:(f % 4) * 128 + 128], ksb[:, f * 128:f * 128 + 128],
                                   ident[:, :])
            ins.then_inc(sem("ks_tr"), 1)
            slabs("m3", 8, 32, KT, 128, 128, wo, D, CH_D, 2, "_lo", False, ("m2_val", 16, 2), made("m3_res", 1))
            pe.wait_ge(sem("m3_lo"), nth("m3_lo", 16))
            pe.wait_ge(sem("ks_col"), nth("ks_col", 1))
            for r in rounds(pe, TT // 2):
                for b in (0, 1):
                    pe.wait_ge(sem(f"mix_slab{b}"), nth(f"mix_slab{b}", 32 * r + 32))
                    if begun(2 * (2 * r + b - 1)):
                        pe.wait_ge(sem("mix_v"), nth("mix_v", 2 * (2 * r + b - 1)))
                    for kt in range(KT):
                        for n3, (l, rk) in enumerate(((0, ksT_hi), (0, ksT_lo), (1, ksT_hi))):
                            TE.matmul(PS[0:TP, b, 1024:1026], L[b][l][:, kt * TP:kt * TP + TP], rk[:, 2 * kt:2 * kt + 2],
                                      start=kt == 0 and n3 == 0, stop=kt == KT - 1 and n3 == 2)
                    product(PS[:, b, :], L[b], m3, KT, 128, TP, CH_D, D).then_inc(sem("mix_mm"), 1)
            pe.wait_ge(sem("mix_v"), nth("mix_v", 20))
            for r in rounds(pe, GRANULES // 2):
                for b in (0, 1):
                    if begun(2 * r + b - 1):
                        pe.wait_ge(sem("adj_ev"), nth("adj_ev", 2 * r + b - 1))
                    for k in range(GC):
                        pe.wait_ge(sem("oh_ready"), nth("oh_ready", GC * (2 * r + b) + (k + 1)))
                        if k == GC - 1:
                            if begun(2 * r + (b + 1)):
                                pe.wait_ge(sem("oh_by_act"), nth("oh_by_act", 2 * r + (b + 1)))
                        for off, n in CH_N:
                            ins = TE.matmul(PS[0:TP, b, off:off + n], oh_dst[:, k, 0:TP], oh_src[:, k, off:off + n],
                                            start=k == 0, stop=k == GC - 1)
                        ins.then_inc(sem("oh_used"), 1)
            enter(pe, "adj")
            if begun(TT - 1):
                pe.wait_ge(sem("count_sum"), nth("count_sum", TT - 1))
            for i in range(TT):
                ins = TE.matmul(PX[0:TP, 0, 2 * i:2 * i + 2], count_sum[0:TP, i * TP:i * TP + TP], ones2[0:TP, :],
                                start=True, stop=True)
            ins.then_inc(sem("deg_mm"), 1)
            enter(pe, "deg")
            if begun(32 * TT):
                pe.wait_ge(sem("gnn_full"), nth("gnn_full", 32 * TT))
            for t in range(TT + 2):
                if t < TT:
                    b = t % 2
                    pe.wait_ge(sem("gnn_slab"), nth("gnn_slab", t + 1))
                    if begun(t - 1):
                        pe.wait_ge(sem("gnn_x1"), nth("gnn_x1", t - 1))
                    product(PS[:, b, :], L[b], hres, TT, TP, TP, CH_D, D).then_inc(sem("gnn_mm"), 1)
                if t >= 2:
                    transposes("gnn", nb9[t % 2], t - 2)
            pe.wait_ge(sem("gnn_x1"), nth("gnn_x1", 10))
            pe.wait_ge(sem("qk_early"), nth("qk_early", 32))
            pe.wait_ge(sem("qk_half"), nth("qk_half", 32))

            def second_half(kt):
                if kt == KT // 2:
                    pe.wait_ge(sem("qk_full"), nth("qk_full", 32))
            slabs("qk", 16, 0, KT, 128, 128, rT, N, CH_N, 3, "_psf", True, come=second_half)
            slabs("v", 10, 32, KT, 128, TP, wv2, D, CH_D, 2, "_val", False, ("qk_psf", 48, 3), made("v_res", 1))
            pe.wait_ge(sem("v_val"), nth("v_val", 20))

            def scores(r, j):
                if not due(r, j):
                    return
                n, b, hb = r * NT + j, j % 2, j // TT % 2
                if j % TT == 0:
                    if begun(112 * r + 112 * (j // NT + 1)):
                        pe.wait_ge(sem(f"head{hb}"), nth(f"head{hb}", 112 * r + 112 * (j // NT + 1)))
                if begun(n - 1):
                    pe.wait_ge(sem("att_exp"), nth("att_exp", n - 1))
                if begun(n - 1):
                    pe.wait_ge(sem("att_loc"), nth("att_loc", n - 1))
                for part in (0, 1):
                    for off, w in CH_N:
                        ins = TE.matmul(PS[0:TP, b, off:off + w], q_st[hb][:, j % TT * TP:j % TT * TP + TP],
                                        k_st[hb][part][:, off:off + w], start=part == 0, stop=part == 1)
                ins.then_inc(sem("att_sc"), 1)

            def transpose_probs(r, j, g):
                if not due(r, j):
                    return
                n, b = r * NT + j, j % 2
                k0, k1 = GROUPS[g]
                pe.wait_ge(sem("att_norm"), nth("att_norm", n + 1))
                if begun(n):
                    pe.wait_ge(sem("att_lo" + g), nth("att_lo" + g, n))
                if g == "a":
                    if begun(r * TT + j // 2):
                        pe.wait_ge(sem("att_osum"), nth("att_osum", r * TT + j // 2))
                for k in range(k0, k1):
                    ins = TE.transpose(group_bank(g, b, k - k0), prob[j % 4][0:TP, k * TP:k * TP + TP], ident[0:TP, 0:TP])
                ins.then_inc(sem("att_tr" + g), 1)

            def values(r, j):
                if not due(r, j):
                    return
                n, hb, pb = r * NT + j, j // TT % 2, j // 2 % 2
                for g in GROUPS:
                    pe.wait_ge(sem("att_lo" + g), nth("att_lo" + g, n + 1))
                for k in range(TT):
                    for part in (0, 1):
                        ins = TE.matmul(PX[:, 0, 0:250], v_st[hb][0:TP, k * 128:k * 128 + 128],
                                        pT[pb][part][0:TP, k * 250:k * 250 + 250],
                                        start=k == 0 and part == 0, stop=k == TT - 1 and part == 1)
                ins.then_inc(sem("att_pv"), 1)

            def window(r, j):
                values(r, j - 5)
                scores(r, j - 1)
                transpose_probs(r, j - 3, "b")
                transpose_probs(r, j - 4, "a")
                transpose_probs(r, j - 2, "c")
                transpose_probs(r, j - 3, "a")
                transpose_probs(r, j - 2, "b")
                scores(r, j)
                transpose_probs(r, j - 1, "c")
            windows(pe, window)
            enter(pe, "att")
            for t in range(TT + 2):
                if t < TT:
                    b = t % 2
                    pe.wait_ge(sem(f"op_slab{b}"), nth(f"op_slab{b}", 32 * (t // 2 + 1)))
                    if begun(t - 1):
                        pe.wait_ge(sem("op_y"), nth("op_y", t - 1))
                    product(PS[:, b, :], L[b], wo2, KT, 128, TP, CH_D, D,
                            come=made("op_res", 1) if t == 0 else None).then_inc(sem("op_mm"), 1)
                if t >= 2:
                    transposes("op", nb13[t % 2], t - 2)
            enter(pe, "op")
            pe.wait_ge(sem("gate_split"), nth("gate_split", 1))
            product(PS[:, 0, :], L[0], zT, KT, 128, 128, CH_N, N).then_inc(sem("gate_mm"), 1)
            pe.wait_ge(sem("gate_log"), nth("gate_log", 1))
            for t in range(TT):
                ins = TE.transpose(PX[0:TP, 0, 8 * t:8 * t + 8], logT[0:8, t * TP:t * TP + TP], ident[0:8, 0:8])
            ins.then_inc(sem("gate_tr"), 1)

            def comb_columns():
                pe.wait_ge(sem("gate_comb"), nth("gate_comb", TT))
                for t in range(TT):
                    if begun(t - 1):
                        pe.wait_ge(sem("gate_ct"), nth("gate_ct", t - 1))
                    TE.transpose(PX[0:8, t % 2, 0:TP], comb[0:TP, t, :], ident[0:TP, 0:TP])\
                        .then_inc(sem("gate_tc"), 1)
            for r in rounds(pe, EXPERTS):
                for j in range(2):
                    for b in (0, 1):
                        pe.wait_ge(sem("ex_split"), nth("ex_split", 4 * r + 2 * j + b + 1))
                        if begun(3 * (2 * r + j)):
                            pe.wait_ge(sem(("ex_a", "ex_b")[b]), nth(("ex_a", "ex_b")[b], 3 * (2 * r + j)))
                        product(PS[:, b, :], L[b], zT, KT, 128, 128, CH_N, N).then_inc(sem("ex_mm"), 1)
                    if isinstance(r, int) and j == 0:
                        comb_columns()
            enter(pe, "ex")
            pe.wait_ge(sem("b3_in"), nth("b3_in", 16))
            for r in rounds(pe, TT // 2):
                for b in (0, 1):
                    pe.wait_ge(sem(f"w3_slab{b}"), nth(f"w3_slab{b}", 48 * r + 48))
                    if begun(2 * (2 * r + b - 1)):
                        pe.wait_ge(sem("w3_v"), nth("w3_v", 2 * (2 * r + b - 1)))
                    product(PS[:, b, :], LG[b], w3, 2 * KT, 128, TP, CH_D, D, last=False,
                            come=made("w3_res", 1) if isinstance(r, int) and b == 0 else None)
                    for off, n in CH_D:
                        ins = TE.matmul(PS[0:TP, b, off:off + n], ct_tile[b][0:EXPERTS, 0:TP],
                                        b3r[0:EXPERTS, off:off + n], start=False, stop=True)
                    ins.then_inc(sem("w3_mm"), 1)

        @block.scalar
        def _(act):
            def stage_hi(ph, n, chunks, src):
                per = len(chunks)
                for r in rounds(act, n // 2):
                    for b in (0, 1):
                        for c in range(per):
                            q, h = per * b + c, (per * b + c) % 2
                            g = r * (2 * per) + q
                            w = chunks[c][1]
                            rows = TP if chunks is CH_D and ph not in ("m2",) else 128
                            act.wait_ge(sem(ph + "_val"), nth(ph + "_val", g + 1))
                            if begun(32 * (r * per + q // 2)):
                                act.wait_ge(sem(f"{ph}_st{h}"), nth(f"{ph}_st{h}", 32 * (r * per + q // 2)))
                            S.copy(HI[0:rows, 512 * h:512 * h + w], src[0:rows, 512 * h:512 * h + w])\
                                .then_inc(sem(ph + "_hi"), 1)

            def resident_raw_hi(ph, dst, pieces):
                for j in range(pieces):
                    act.wait_ge(sem(f"{ph}_rr{4 * j // pieces}"), nth(f"{ph}_rr{4 * j // pieces}", 16))
                    cols = slice(j * D, (j + 1) * D)
                    S.copy(dst[0][:, cols], dst[2][:, cols]).then_inc(sem(ph + "_rh"), 1)

            for t in range(TT + 1):
                if t < TT:
                    act.wait_ge(sem("ln_var"), nth("ln_var", t + 1))
                    S.activation(rstd[0:TP, :], small[0:TP, 0:1], ACT.Sqrt).then_inc(sem("ln_sd"), 1)
                if t >= 1:
                    u = t - 1
                    act.wait_ge(sem("ln_nb"), nth("ln_nb", u + 1))
                    if begun(32 * (u // 2)):
                        act.wait_ge(sem(f"ln_st{u % 2}"), nth(f"ln_st{u % 2}", 32 * (u // 2)))
                    S.copy(ln_stage[u % 2][0][0:TP, :], nb[u % 2][0:TP, :]).then_inc(sem("ln_hi"), 1)
                    act.wait_ge(sem("ln_tv"), nth("ln_tv", u + 1))
                    S.copy(xnT[0][:, :].rearrange("p (k c) -> p k c", k=KT)[:, :, u * TP:(u + 1) * TP],
                           tv[:, :].rearrange("p (k c) -> p k c", k=KT)).then_inc(sem("ln_nh"), 1)
            enter(act, "ln")

            def stage_elu(ph, n, chunks, rows):
                per = len(chunks)
                for r in rounds(act, n // 2):
                    for b in (0, 1):
                        for c in range(per):
                            q, h = per * b + c, (per * b + c) % 2
                            g = r * (2 * per) + q
                            w = chunks[c][1]
                            cols = slice(512 * h, 512 * h + w)
                            act.wait_ge(sem(ph + "_m"), nth(ph + "_m", g + 1))
                            S.activation(T2[0:rows, cols], T2[0:rows, cols], ACT.Exp).then_inc(sem(ph + "_e"), 1)
                            act.wait_ge(sem(ph + "_val"), nth(ph + "_val", g + 1))
                            if begun(32 * (r * per + q // 2)):
                                act.wait_ge(sem(f"{ph}_st{h}"), nth(f"{ph}_st{h}", 32 * (r * per + q // 2)))
                            S.copy(HI[0:rows, cols], T1[0:rows, cols]).then_inc(sem(ph + "_hi"), 1)
            stage_elu("q", 8, CH_N, 128)
            enter(act, "q")
            stage_elu("k", 10, CH_D, TP)
            enter(act, "k")
            stage_hi("h", 10, CH_D, T1)
            enter(act, "h")

            def resident_hi(ph, dst):
                for r in rounds(act, 4):
                    for b in (0, 1):
                        act.wait_ge(sem(ph + "_mm"), nth(ph + "_mm", 2 * r + b + 1))
                        for c, (off, w) in enumerate(CH_D):
                            S.copy(dst[0][:, bass.ds(r * (2 * D) + (b * D + off), w)], PS[:, b, off:off + w])\
                                .then_inc(sem(ph + "_hi"), 1)
            resident_hi("m1", m1T)
            enter(act, "m1")
            stage_hi("m2", 8, CH_D, T1)
            resident_raw_hi("m3", wo, 8)
            enter(act, "m2")
            resident_hi("m3", m3)
            enter(act, "mix")
            act.wait_ge(sem("neg_src"), nth("neg_src", 1))
            act.wait_ge(sem("iota"), nth("iota", 1))
            for r in rounds(act, GRANULES // 2):
                for b in (0, 1):
                    g = 2 * r + b
                    if begun(GC * g):
                        act.wait_ge(sem("oh_used"), nth("oh_used", GC * g))
                    if begun(g):
                        act.wait_ge(sem("oh_by_act"), nth("oh_by_act", g))
                    apart(act)
                    S.activation(distance[:, :], iota[:, :], ACT.Abs, bias=neg_src[:, bass.ds(GC * g + GC - 1, 1)])\
                        .then_inc(sem("oh_distance"), 1)
                    act.wait_ge(sem("oh_distance"), nth("oh_distance", g + 1))
                    S.activation(oh_src[:, GC - 1, :], distance[:, :], ACT.Relu, bias=ones2[:, 0:1], scale=-1.0)\
                        .then_inc(sem("oh_by_act"), 1)
            act.wait_ge(sem("deg_mm"), nth("deg_mm", 1))
            S.activation(dis[0:TP, :], PX[0:TP, 0, 0:2 * TT].rearrange("p (t e) -> p t e", e=2)[:, :, 0],
                         ACT.Sqrt).then_inc(sem("deg_sd"), 1)
            enter(act, "deg")

            cv = counts[:, :, :]

            def gnn_slab(t):
                b = t % 2
                if begun(t - 1):
                    act.wait_ge(sem("gnn_mm"), nth("gnn_mm", t - 1))
                S.copy(L[b][0][0:TP, 0:TT * TP].rearrange("p (k c) -> p k c", k=TT),
                       cv[0:TP, :, t * TP:t * TP + TP]).then_inc(sem("gnn_sh"), 1)

            gnn_slab(0)
            for t in range(TT + 2):
                if t + 1 < TT:
                    gnn_slab(t + 1)
                if t < TT:
                    act.wait_ge(sem("gnn_var"), nth("gnn_var", t + 1))
                    S.activation(rstd[0:TP, :], small[0:TP, 0:1], ACT.Sqrt).then_inc(sem("gnn_sd"), 1)
                    act.wait_ge(sem("gnn_u"), nth("gnn_u", t + 1))
                    if begun(t - 1):
                        act.wait_ge(sem("gnn_tr"), nth("gnn_tr", t - 1))
                    S.activation(nb9[t % 2][0:TP, :], u9[0:TP, :], ACT.Square, accum_out=small[0:TP, 2:3])\
                        .then_inc(sem("gnn_sq"), 1)
                    act.wait_ge(sem("gnn_ms"), nth("gnn_ms", t + 1))
                    S.activation(small[0:TP, 4:5], small[0:TP, 3:4], ACT.Sqrt).then_inc(sem("gnn_rsd"), 1)
                if t >= 2:
                    if begun(t - 1):
                        act.wait_ge(sem("gnn_tv"), nth("gnn_tv", t - 1))
                    if begun(32 * (t - 2)):
                        act.wait_ge(sem("gnn_st"), nth("gnn_st", 32 * (t - 2)))
                    S.copy(HI[:, 0:KT * TP], tv9[:, :]).then_inc(sem("gnn_nh"), 1)
            enter(act, "gnn")
            act.wait_ge(sem("consts"), nth("consts", 128))
            for r in rounds(act, 8):
                for b in (0, 1):
                    for c, (off, w) in enumerate(CH_N):
                        q, h = 3 * b + c, (3 * b + c) % 2
                        g = r * 6 + q
                        cols = slice(512 * h, 512 * h + w)
                        if c == 0:
                            act.wait_ge(sem("qk_mm"), nth("qk_mm", 2 * r + b + 1))
                        if begun(g - 1):
                            act.wait_ge(sem("qk_lo"), nth("qk_lo", g - 1))
                        apart(act)
                        S.activation(T1[:, cols], PS[:, b, off:off + w], ACT.Identity,
                                     bias=bqk[:, bass.ds(2 * r + b, 1)]).then_inc(sem("qk_psf"), 1)
                        act.wait_ge(sem("qk_psf"), nth("qk_psf", g + 1))
                        for k in range(4):
                            o = k + 1 if k % 2 == 0 else k - 1
                            ins = S.copy(T3[32 * k:32 * k + 32, cols], T1[32 * o:32 * o + 32, cols])
                        ins.then_inc(sem("qk_rot"), 1)
                        act.wait_ge(sem("qk_val"), nth("qk_val", g + 1))
                        if begun(32 * (r * 3 + q // 2)):
                            act.wait_ge(sem(f"qk_st{h}"), nth(f"qk_st{h}", 32 * (r * 3 + q // 2)))
                        S.copy(HI[:, cols], T2[:, cols]).then_inc(sem("qk_hi"), 1)
            enter(act, "qk")
            stage_hi("v", 10, CH_D, T1)
            enter(act, "v")
            def exponentials(r, j):
                if not due(r, j):
                    return
                n, b = r * NT + j, j % 2
                act.wait_ge(sem("att_nm"), nth("att_nm", n + 1))
                for g in GROUPS:
                    if begun(n - 3):
                        act.wait_ge(sem("att_tr" + g), nth("att_tr" + g, n - 3))
                S.activation(prob[j % 4][0:TP, :], PS[0:TP, b, 0:N], ACT.Exp, bias=nmx[0:TP, b:b + 1],
                             scale=HD ** -0.5, accum_out=rs[0:TP, b:b + 1]).then_inc(sem("att_exp"), 1)

            def upper_part(r, j, g):
                if not due(r, j):
                    return
                n = r * NT + j
                act.wait_ge(sem("att_tr" + g), nth("att_tr" + g, n + 1))
                if g == "c" and j % 2 == 0:
                    if begun(r * TT + j // 2 - 1):
                        act.wait_ge(sem("att_pv"), nth("att_pv", r * TT + j // 2 - 1))
                S.copy(pT_part(j // 2 % 2, 0, g, j), group_read(g, j % 2)).then_inc(sem("att_hi" + g), 1)

            def output_copy(r, j):
                if not due(r, j):
                    return
                pair, pb = r * TT + j // 2, j // 2 % 2
                act.wait_ge(sem("att_pv"), nth("att_pv", pair + 1))
                if begun(pair - 1):
                    act.wait_ge(sem("att_osum"), nth("att_osum", pair - 1))
                S.copy(o_tmp[0:64, 250 * pb:250 * pb + 250], PX[64:128, 0, 0:250]).then_inc(sem("att_oc"), 1)

            def output_hi(r, j):
                if not due(r, j):
                    return
                pair, pb = r * TT + j // 2, j // 2 % 2
                oc = slice(250 * pb, 250 * pb + 250)
                act.wait_ge(sem("att_osum"), nth("att_osum", pair + 1))
                if begun(32 * (r * (TT // 2) + j // 4)):
                    act.wait_ge(sem(f"att_st{pb}"), nth(f"att_st{pb}", 32 * (r * (TT // 2) + j // 4)))
                S.copy(o_hi[0:64, oc], o_sum[0:64, oc]).then_inc(sem("att_ohi"), 1)

            def window(r, j):
                upper_part(r, j - 3, "c")
                exponentials(r, j - 2)
                output_copy(r, j - 5)
                upper_part(r, j - 3, "b")
                upper_part(r, j - 4, "a")
                upper_part(r, j - 2, "c")
                exponentials(r, j - 1)
                upper_part(r, j - 3, "a")
                upper_part(r, j - 2, "b")
                output_hi(r, j - 5)
            windows(act, window)
            enter(act, "att")
            resident_raw_hi("op", wo2, 8)
            for t in range(TT + 2):
                if t < TT:
                    act.wait_ge(sem("op_y"), nth("op_y", t + 1))
                    if begun(t - 1):
                        act.wait_ge(sem("op_tr"), nth("op_tr", t - 1))
                    S.activation(nb13[t % 2][0:TP, :], T1[0:TP, :], ACT.Square, accum_out=small[0:TP, 2:3])\
                        .then_inc(sem("op_sq"), 1)
                    act.wait_ge(sem("op_ms"), nth("op_ms", t + 1))
                    S.activation(small[0:TP, 4:5], small[0:TP, 3:4], ACT.Sqrt).then_inc(sem("op_rsd"), 1)
                if t >= 2:
                    if begun(t - 1):
                        act.wait_ge(sem("op_tv"), nth("op_tv", t - 1))
                    S.copy(zT[0][:, :].rearrange("p (k c) -> p k c", k=KT)[:, :, (t - 2) * TP:(t - 1) * TP],
                           tv13[:, :].rearrange("p (k c) -> p k c", k=KT)).then_inc(sem("op_nh"), 1)
            enter(act, "op")
            act.wait_ge(sem("gate_mm"), nth("gate_mm", 1))
            S.copy(logT[0:8, :], PS[0:8, 0, 0:N]).then_inc(sem("gate_log"), 1)
            for t in range(TT):
                act.wait_ge(sem("gate_top"), nth("gate_top", t + 1))
                S.activation(ex8[0:TP, :], lg[0:TP, :], ACT.Exp, bias=nm1[0:TP, 0:1]).then_inc(sem("gate_e8"), 1)
            for t in range(TT):
                act.wait_ge(sem("gate_tc"), nth("gate_tc", t + 1))
                S.copy(combT[0:8, t * TP:t * TP + TP], PX[0:8, t % 2, 0:TP]).then_inc(sem("gate_ct"), 1)
            enter(act, "op")
            for r in rounds(act, EXPERTS):
                for j in range(2):
                    act.wait_ge(sem("ex_mm"), nth("ex_mm", 4 * r + 2 * j + 1))
                    if begun(6 * r + 3 * (j - 1)):
                        act.wait_ge(sem("ex_b"), nth("ex_b", 6 * r + 3 * (j - 1)))
                    apart(act)
                    for off, w in CH_N:
                        S.activation(silu[j][:, off:off + w], PS[:, 0, off:off + w], ACT.Silu,
                                     bias=b1[:, bass.ds(2 * r + j, 1)]).then_inc(sem("ex_a"), 1)
                    for c, (off, w) in enumerate(CH_N):
                        q, h = 3 * j + c, (3 * j + c) % 2
                        g = r * 6 + q
                        cols = slice(512 * h, 512 * h + w)
                        act.wait_ge(sem("ex_val"), nth("ex_val", g + 1))
                        if begun(32 * (r * 3 + q // 2)):
                            act.wait_ge(sem(f"ex_st{h}"), nth(f"ex_st{h}", 32 * (r * 3 + q // 2)))
                        S.copy(HI[:, cols], T2[:, cols]).then_inc(sem("ex_hi"), 1)
            enter(act, "ex")
            resident_raw_hi("w3", w3, 16)

        @block.vector
        def _(dve):
            P_SUB = ALU.subtract

            V.memset(ones2[:, :], 1.0).then_inc(sem("ones2_ready"), 1)

            def stage_lo(ph, r, per, q, g, src, cols, rows):
                dve.wait_ge(sem(ph + "_hi"), nth(ph + "_hi", g + 1))
                if begun(32 * (r * per + q // 2)):
                    dve.wait_ge(sem(f"{ph}_st{q % 2}"), nth(f"{ph}_st{q % 2}", 32 * (r * per + q // 2)))
                V.tensor_tensor(LO[0:rows, cols], src[0:rows, cols], HI[0:rows, cols].bitcast(F32), P_SUB)\
                    .then_inc(sem(ph + "_lo"), 1)

            def resident_raw_lo(ph, dst, pieces):
                for j in range(pieces):
                    dve.wait_ge(sem(ph + "_rh"), nth(ph + "_rh", j + 1))
                    cols = slice(j * D, (j + 1) * D)
                    V.tensor_tensor(dst[1][:, cols], dst[2][:, cols], dst[0][:, cols].bitcast(F32), P_SUB)\
                        .then_inc(sem(ph + "_res"), 1)

            def stats(ph, t, src):
                for k in range(2):
                    V.bn_stats(stat6[0:TP, 6 * k:6 * k + 6], src[0:TP, 512 * k:512 * k + 512]).then_inc(sem(ph + "_bn"), 1)
                dve.wait_ge(sem(ph + "_bn"), nth(ph + "_bn", 2 * t + 2))
                V.bn_aggr(mv[0:TP, :], stat6[0:TP, :]).then_inc(sem(ph + "_ag"), 1)
                dve.wait_ge(sem(ph + "_ag"), nth(ph + "_ag", t + 1))
                V.tensor_scalar(small[0:TP, 0:1], mv[0:TP, 1:2], LN_EPS, None, ALU.add).then_inc(sem(ph + "_var"), 1)
                dve.wait_ge(sem(ph + "_sd"), nth(ph + "_sd", t + 1))
                V.reciprocal(small[0:TP, 1:2], rstd[0:TP, :]).then_inc(sem(ph + "_rc"), 1)
                dve.wait_ge(sem(ph + "_rc"), nth(ph + "_rc", t + 1))

            def ln_tail(t):
                dve.wait_ge(sem("ln_hi"), nth("ln_hi", t + 1))
                hi, lo = ln_stage[t % 2]
                V.tensor_tensor(lo[0:TP, :], nb[t % 2][0:TP, :], hi[0:TP, :].bitcast(F32), P_SUB).then_inc(sem("ln_lo"), 1)
                dve.wait_ge(sem("ln_tr"), nth("ln_tr", t + 1))
                if begun(t):
                    dve.wait_ge(sem("ln_rt"), nth("ln_rt", t))
                px = PX[:, :, 0:4 * TP]
                V.tensor_copy(tv[:, :].rearrange("p (a c) -> p a c", a=2), px).then_inc(sem("ln_tv"), 1)
                dve.wait_ge(sem("ln_nh"), nth("ln_nh", t + 1))
                tile = slice(t * TP, (t + 1) * TP)
                V.tensor_tensor(xnT[1][:, :].rearrange("p (k c) -> p k c", k=KT)[:, :, tile],
                                tv[:, :].rearrange("p (k c) -> p k c", k=KT),
                                xnT[0][:, :].rearrange("p (k c) -> p k c", k=KT)[:, :, tile].bitcast(F32), P_SUB)\
                    .then_inc(sem("ln_rt"), 1)
            for t in range(TT + 1):
                if t < TT:
                    b = t % 2
                    src = [T1, T2][b]
                    dve.wait_ge(sem(f"ln_x{b}"), nth(f"ln_x{b}", 16 * (t // 2 + 1)))
                    stats("ln", t, src)
                    V.tensor_scalar(nb[b][0:TP, :], src[0:TP, :], mv[0:TP, 0:1], small[0:TP, 1:2], ALU.subtract, ALU.mult)\
                        .then_inc(sem("ln_nb"), 1)
                if t >= 1:
                    ln_tail(t - 1)
            enter(dve, "ln")

            def elu(ph, n, chunks, rows, first):
                per = len(chunks)
                for r in rounds(dve, n // 2):
                    for b in (0, 1):
                        for c, (off, w) in enumerate(chunks):
                            q = per * b + c
                            h = q % 2
                            g = r * (2 * per) + q
                            cols = slice(512 * h, 512 * h + w)
                            if c == 0:
                                dve.wait_ge(sem(ph + "_mm"), nth(ph + "_mm", 2 * r + b + 1))
                            first(r, b, off, w, cols)
                            dve.wait_ge(sem(ph + "_psf"), nth(ph + "_psf", g + 1))
                            V.tensor_scalar(T2[0:rows, cols], T1[0:rows, cols], 0.0, None, ALU.min).then_inc(sem(ph + "_m"), 1)
                            dve.wait_ge(sem(ph + "_e"), nth(ph + "_e", g + 1))
                            V.scalar_tensor_tensor(T1[0:rows, cols], T1[0:rows, cols], 0.0, T2[0:rows, cols],
                                                   ALU.max, ALU.add).then_inc(sem(ph + "_val"), 1)
                            dve.wait_ge(sem(ph + "_val"), nth(ph + "_val", g + 1))
                            stage_lo(ph, r, per, q, g, T1, cols, rows)

            dve.wait_ge(sem("consts"), nth("consts", 128))

            def q_first(r, b, off, w, cols):
                V.tensor_scalar(T1[:, cols], PS[:, b, off:off + w], bq[:, bass.ds(2 * r + b, 1)], None, ALU.add)\
                    .then_inc(sem("q_psf"), 1)
            elu("q", 8, CH_N, 128, q_first)
            enter(dve, "q")
            V.memset(ones_r[:, :].bitcast(F32), 1.0).then_inc(sem("ones_ready"), 1)
            V.memset(sorted_e[:, :, :], -1.0)
            dve.wait_ge(sem("edges"), nth("edges", 48))
            V.tensor_copy(edge_pair[0:TP, :, 0], edge_src_i[0:TP, :])
            V.tensor_copy(edge_dst[0:TP, :], edge_dst_i[0:TP, :]).then_inc(sem("sort_step"), 1)
            V.memset(reached[0:TP, 0, :], 1.0)
            V.memset(reached[0:TP, TT, :], 0.0)
            dve.wait_ge(sem("sort_step"), nth("sort_step", 1))
            for b in range(1, TT):
                ins = V.tensor_scalar(reached[0:TP, b, :], edge_dst[0:TP, :], float(b * TP), None, ALU.is_ge)
            ins.then_inc(sem("sort_step"), 1)
            dve.wait_ge(sem("sort_step"), nth("sort_step", 2))
            V.tensor_tensor(member[0:TP, :, :], reached[0:TP, 0:TT, :], reached[0:TP, 1:TT + 1, :], P_SUB)
            V.reduce_sum(edge_tile[0:TP, :], reached[0:TP, 1:TT, :].rearrange("p b c -> p c b"), AX.X)\
                .then_inc(sem("sort_step"), 1)
            dve.wait_ge(sem("sort_step"), nth("sort_step", 3))
            V.scalar_tensor_tensor(edge_pair[0:TP, :, 1], edge_tile[0:TP, :], -float(TP), edge_dst[0:TP, :],
                                   ALU.mult, ALU.add)
            flat = member[0:TP, :, :].rearrange("p b c -> p (b c)")
            V.tensor_tensor_scan(rank[0:TP, :, :].rearrange("p b c -> p (b c)"), flat, flat, 0.0, ALU.add, ALU.max)\
                .then_inc(sem("sort_step"), 1)
            dve.wait_ge(sem("sort_step"), nth("sort_step", 4))
            V.tensor_copy(tile_n[0:TP, 0:1], rank[0:TP, 0, EC - 1:EC])
            V.tensor_tensor(tile_n[0:TP, 1:TT], rank[0:TP, 1:TT, EC - 1], rank[0:TP, 0:TT - 1, EC - 1], P_SUB)\
                .then_inc(sem("sort_tile_n"), 1)
            dve.wait_ge(sem("sort_sums"), nth("sort_sums", 1))
            V.tensor_scalar(gran_i[0:TP, 0, :], PX[0:TP, 1, 0:TT], float(GRANULE - 1), None, ALU.add)\
                .then_inc(sem("sort_step"), 1)
            dve.wait_ge(sem("sort_step"), nth("sort_step", 5))
            V.tensor_scalar(gran_i[0:TP, 1, :], gran_i[0:TP, 0, :], GRANULE.bit_length() - 1, None,
                            ALU.logical_shift_right).then_inc(sem("sort_step"), 1)
            dve.wait_ge(sem("sort_step"), nth("sort_step", 6))
            V.tensor_copy(gran_f[0:TP, :], gran_i[0:TP, 1, :]).then_inc(sem("sort_step"), 1)
            dve.wait_ge(sem("sort_step"), nth("sort_step", 7))
            V.tensor_tensor_scan(gran_sum[0:TP, :], gran_f[0:TP, :], gran_f[0:TP, :], 0.0, ALU.add, ALU.max)\
                .then_inc(sem("sort_step"), 1)
            dve.wait_ge(sem("sort_step"), nth("sort_step", 8))
            V.tensor_tensor(gran_start[0:TP, :], gran_sum[0:TP, :], gran_f[0:TP, :], P_SUB).then_inc(sem("sort_step"), 1)
            dve.wait_ge(sem("sort_step"), nth("sort_step", 9))
            V.scalar_tensor_tensor(tile_off[0:TP, :], gran_start[0:TP, :], float(GRANULE), PX[0:TP, 0, 0:TT],
                                   ALU.mult, ALU.add).then_inc(sem("sort_step"), 1)
            dve.wait_ge(sem("sort_step"), nth("sort_step", 10))
            V.tensor_tensor(tile_off[0:TP, 1:TT], tile_off[0:TP, 1:TT], rank[0:TP, 0:TT - 1, EC - 1], P_SUB)\
                .then_inc(sem("sort_step"), 1)
            dve.wait_ge(sem("sort_step"), nth("sort_step", 11))
            for b in range(TT):
                ins = V.scalar_tensor_tensor(place[0:TP, b, :], rank[0:TP, b, :], tile_off[0:TP, b:b + 1],
                                             member[0:TP, b, :], ALU.add, ALU.mult)
            ins.then_inc(sem("sort_step"), 1)
            dve.wait_ge(sem("sort_step"), nth("sort_step", 12))
            V.reduce_sum(edge_pos[0:TP, :], place[0:TP, :, :].rearrange("p b c -> p c b"), AX.X)\
                .then_inc(sem("sort_step"), 1)
            dve.wait_ge(sem("sort_step"), nth("sort_step", 13))
            V.tensor_scalar(edge_pos_i[0:TP, :], edge_pos[0:TP, :], -1.0, None, ALU.add).then_inc(sem("sort_step"), 1)
            dve.wait_ge(sem("sort_step"), nth("sort_step", 14))
            V.tensor_scalar(edge_col_i[0:TP, :], edge_pos_i[0:TP, :], 7, None, ALU.logical_shift_right)
            V.tensor_scalar(edge_part_i[0:TP, :], edge_pos_i[0:TP, :], 127, None, ALU.bitwise_and)\
                .then_inc(sem("sort_step"), 1)
            dve.wait_ge(sem("sort_step"), nth("sort_step", 15))
            V.tensor_copy(edge_col[0:TP, :], edge_col_i[0:TP, :])
            V.tensor_copy(edge_dst[0:TP, :], edge_part_i[0:TP, :]).then_inc(sem("sort_step"), 1)
            dve.wait_ge(sem("sort_step"), nth("sort_step", 16))
            V.scalar_tensor_tensor(edge_row[0:TP, :], edge_dst[0:TP, :], float(SC), edge_col[0:TP, :], ALU.mult, ALU.add)
            dve.wait_ge(sem("gran_iota"), nth("gran_iota", 1))
            V.tensor_tensor(gran_ge[0:1, :, :], gran_no[0:1, :].unsqueeze(1).broadcast_to([1, TT - 1, GRANULES]),
                            gran_start[0:1, 1:TT].unsqueeze(2).broadcast_to([1, TT - 1, GRANULES]), ALU.is_ge)\
                .then_inc(sem("sort_step"), 1)
            dve.wait_ge(sem("sort_step"), nth("sort_step", 17))
            V.reduce_sum(gran_no[0:1, :], gran_ge[0:1, :, :].rearrange("p b g -> p g b"), AX.X)\
                .then_inc(sem("sort_step"), 1)
            dve.wait_ge(sem("sort_step"), nth("sort_step", 18))
            V.tensor_scalar(gran_at[0:1, :], gran_no[0:1, :], float(N), None, ALU.mult).then_inc(sem("sort_ready"), 1)
            dve.wait_ge(sem("sort_ready"), nth("sort_ready", 1))
            dve.wait_ge(sem("k_bias"), nth("k_bias", 16))

            def k_first(r, b, off, w, cols):
                V.tensor_tensor(T1[0:TP, cols], PS[0:TP, b, off:off + w], bias_b[0:TP, off:off + w], ALU.add)\
                    .then_inc(sem("k_psf"), 1)
            elu("k", 10, CH_D, TP, k_first)
            enter(dve, "k")

            def plain(ph, n, chunks, rows, first):
                per = len(chunks)
                for r in rounds(dve, n // 2):
                    for b in (0, 1):
                        for c, (off, w) in enumerate(chunks):
                            q = per * b + c
                            g = r * (2 * per) + q
                            cols = slice(512 * (q % 2), 512 * (q % 2) + w)
                            if c == 0:
                                dve.wait_ge(sem(ph + "_mm"), nth(ph + "_mm", 2 * r + b + 1))
                            first(r, b, off, w, cols)
                            dve.wait_ge(sem(ph + "_val"), nth(ph + "_val", g + 1))
                            stage_lo(ph, r, per, q, g, T1, cols, rows)

            def add_rows(ph, bias):
                def first(r, b, off, w, cols):
                    V.tensor_tensor(T1[0:TP, cols], PS[0:TP, b, off:off + w], bias[0:TP, off:off + w], ALU.add)\
                        .then_inc(sem(ph + "_val"), 1)
                return first
            dve.wait_ge(sem("g_bias"), nth("g_bias", 16))
            plain("h", 10, CH_D, TP, add_rows("h", bias_a))
            enter(dve, "h")
            dve.wait_ge(sem("ks_mm"), nth("ks_mm", 1))
            V.tensor_copy(ksb[:, :], PS[:, 0, 0:D]).then_inc(sem("ks_v"), 1)

            def resident_lo(ph, dst):
                for r in rounds(dve, 4):
                    for b in (0, 1):
                        for c, (off, w) in enumerate(CH_D):
                            dve.wait_ge(sem(ph + "_hi"), nth(ph + "_hi", 4 * r + 2 * b + c + 1))
                            cols = bass.ds(r * (2 * D) + (b * D + off), w)
                            V.tensor_tensor(dst[1][:, cols], PS[:, b, off:off + w], dst[0][:, cols].bitcast(F32), P_SUB)\
                                .then_inc(sem(ph + "_lo"), 1)
            resident_lo("m1", m1T)
            enter(dve, "m1")

            def m2_first(r, b, off, w, cols):
                V.scalar_tensor_tensor(T1[:, cols], ksb[:, off:off + w], bv[:, bass.ds(2 * r + b, 1)],
                                       PS[:, b, off:off + w], ALU.mult, ALU.add).then_inc(sem("m2_val"), 1)
            plain("m2", 8, CH_D, 128, m2_first)
            resident_raw_lo("m3", wo, 8)
            enter(dve, "m2")
            dve.wait_ge(sem("ks_tr"), nth("ks_tr", 1))
            V.tensor_scalar(T1[:, 0:2 * KT].rearrange("p (k e) -> p k e", e=2),
                            PX[:, :, :].rearrange("p a (k c) -> p (a k) c", c=128)[:, :, 0:2], 1e-6, None, ALU.add)\
                .then_inc(sem("ks_c1"), 1)
            dve.wait_ge(sem("ks_c1"), nth("ks_c1", 1))
            V.tensor_copy(ksT_hi[:, :], T1[:, 0:2 * KT]).then_inc(sem("ks_c2"), 1)
            dve.wait_ge(sem("ks_c2"), nth("ks_c2", 1))
            V.tensor_tensor(ksT_lo[:, :], T1[:, 0:2 * KT], ksT_hi[:, :].bitcast(F32), P_SUB).then_inc(sem("ks_col"), 1)
            resident_lo("m3", m3)
            enter(dve, "m3")
            dve.wait_ge(sem("o_bias"), nth("o_bias", 16))
            for r in rounds(dve, TT // 2):
                for b in (0, 1):
                    dve.wait_ge(sem("mix_mm"), nth("mix_mm", 2 * r + b + 1))
                    V.reciprocal(zr[0:TP, b:b + 1], PS[0:TP, b, 1024:1025]).then_inc(sem("mix_z"), 1)
                    for c in (0, 1):
                        g = 4 * r + 2 * b + c
                        cols = slice(512 * c, 512 * c + 512)
                        dve.wait_ge(sem(f"mix_in{c}"), nth(f"mix_in{c}", 32 * r + 16 * b + 16))
                        if begun(32 * r + 16 * b):
                            dve.wait_ge(sem(f"mix_st{c}"), nth(f"mix_st{c}", 32 * r + 16 * b))
                        V.tensor_tensor(T1[0:TP, cols], T2[0:TP, cols], bias_a[0:TP, cols], ALU.add).then_inc(sem("mix_xb"), 1)
                        dve.wait_ge(sem("mix_xb"), nth("mix_xb", g + 1))
                        dve.wait_ge(sem("mix_z"), nth("mix_z", 2 * r + b + 1))
                        V.scalar_tensor_tensor(T1[0:TP, cols], PS[0:TP, b, cols], zr[0:TP, b:b + 1], T1[0:TP, cols],
                                               ALU.mult, ALU.add).then_inc(sem("mix_v"), 1)
            enter(dve, "mix")
            V.memset(counts[:, 0:TT // 2, :], 0.0).then_inc(sem("counts_zero"), 1)
            dve.wait_ge(sem("sorted_in"), nth("sorted_in", 16))
            V.tensor_scalar(neg_src[:, :], sorted_e[:, :, 0], -1.0, None, ALU.mult).then_inc(sem("neg_src"), 1)
            dve.wait_ge(sem("iota"), nth("iota", 1))

            def onehots(g, k):
                if begun(GC * g + (k + 1 - GC)):
                    dve.wait_ge(sem("oh_used"), nth("oh_used", GC * g + (k + 1 - GC)))
                col = GC * g + k
                src, dst = [sorted_e[:, bass.ds(col, 1) if not isinstance(col, int) else slice(col, col + 1), e]
                            for e in (0, 1)]
                if k < GC - 1:
                    V.tensor_scalar(oh_src[:, k, :], iota[:, :], src, None, ALU.is_equal)
                V.tensor_scalar(oh_dst[:, k, 0:TP], iota[:, 0:TP], dst, None, ALU.is_equal).then_inc(sem("oh_ready"), 1)

            def add_granule(g, b):
                column = dve.value_load(gran_at[0:1, bass.ds(g, 1)], min_val=0, max_val=(TT - 1) * N)
                flat = counts[0:TP, :, :].rearrange("p t c -> p (t c)")[:, bass.ds(column, N)]
                dve.wait_ge(sem("oh_used"), nth("oh_used", GC * g + GC))
                if begun(g):
                    dve.wait_ge(sem("adj_ev"), nth("adj_ev", g))
                V.tensor_tensor(flat, PS[0:TP, b, 0:N], flat, ALU.add).then_inc(sem("adj_ev"), 1)
            dve.wait_ge(sem("counts_zero"), nth("counts_zero", 2))
            for r in rounds(dve, GRANULES // 2):
                for b in (0, 1):
                    for k in range(GC):
                        onehots(2 * r + b, k)
                    if not (isinstance(r, int) and b == 0):
                        add_granule(2 * r + (b - 1), 1 - b)
            add_granule(GRANULES - 1, 1)
            dve.wait_ge(sem("adj_ev"), nth("adj_ev", GRANULES))
            for j in range(TT):
                ins = V.tensor_tensor(counts[0:TP, j, j * TP:(j + 1) * TP], counts[0:TP, j, j * TP:(j + 1) * TP],
                                      ident[0:TP, 0:TP], ALU.add)
            ins.then_inc(sem("loops_in"), 1)
            dve.wait_ge(sem("loops_in"), nth("loops_in", 1))
            for j in range(1, TT):
                if begun(j - 1):
                    dve.wait_ge(sem("count_sum"), nth("count_sum", j - 1))
                V.tensor_tensor(count_sum[0:TP, :], counts[0:TP, 0, :] if j == 1 else count_sum[0:TP, :],
                                counts[0:TP, j, :], ALU.add).then_inc(sem("count_sum"), 1)
            dve.wait_ge(sem("deg_sd"), nth("deg_sd", 1))
            V.reciprocal(dis[0:TP, :], dis[0:TP, :]).then_inc(sem("deg_r"), 1)
            dve.wait_ge(sem("deg_r"), nth("deg_r", 1))
            for j in range(TT):
                ins = V.tensor_scalar(counts[0:TP, j, :], counts[0:TP, j, :], dis[0:TP, j:j + 1], None, ALU.mult)
            ins.then_inc(sem("deg_scaled"), 1)
            enter(dve, "deg")

            def gnn_slab(t):
                b = t % 2
                dve.wait_ge(sem("gnn_sh"), nth("gnn_sh", t + 1))
                V.tensor_tensor(L[b][1][0:TP, 0:TT * TP].rearrange("p (k c) -> p k c", k=TT),
                                counts[0:TP, :, t * TP:t * TP + TP],
                                L[b][0][0:TP, 0:TT * TP].rearrange("p (k c) -> p k c", k=TT).bitcast(F32), P_SUB)\
                    .then_inc(sem("gnn_slab"), 1)

            def rms(ph, t, src, dst):
                dve.wait_ge(sem(ph + "_sq"), nth(ph + "_sq", t + 1))
                V.tensor_scalar(small[0:TP, 3:4], small[0:TP, 2:3], 1.0 / D, RMS_EPS, ALU.mult, ALU.add)\
                    .then_inc(sem(ph + "_ms"), 1)
                dve.wait_ge(sem(ph + "_rsd"), nth(ph + "_rsd", t + 1))
                V.reciprocal(small[0:TP, 5:6], small[0:TP, 4:5]).then_inc(sem(ph + "_rmsr"), 1)
                dve.wait_ge(sem(ph + "_rmsr"), nth(ph + "_rmsr", t + 1))
                V.tensor_scalar(dst[0:TP, :], src[0:TP, :], small[0:TP, 5:6], None, ALU.mult).then_inc(sem(ph + "_nb"), 1)

            def weighted(ph, t, w, dst):
                dve.wait_ge(sem(ph + "_tr"), nth(ph + "_tr", t + 1))
                if begun(t):
                    dve.wait_ge(sem(ph + "_rt"), nth(ph + "_rt", t))
                V.tensor_tensor(dst[:, :].rearrange("p (a k c) -> p a k c", a=2, k=4),
                                PX[:, :, 0:4 * TP].rearrange("p a (k c) -> p a k c", k=4),
                                w[:, :].rearrange("p (a k) -> p a k", a=2).unsqueeze(3).broadcast_to([128, 2, 4, TP]),
                                ALU.mult).then_inc(sem(ph + "_tv"), 1)
            gnn_slab(0)
            for t in range(TT + 2):
                if t + 1 < TT:
                    gnn_slab(t + 1)
                if t < TT:
                    b = t % 2
                    dve.wait_ge(sem("gnn_acc"), nth("gnn_acc", 16 * (t + 1)))
                    dve.wait_ge(sem("gnn_mm"), nth("gnn_mm", t + 1))
                    if begun(16 * t):
                        dve.wait_ge(sem("gnn_sx"), nth("gnn_sx", 16 * t))
                    V.scalar_tensor_tensor(T1[0:TP, :], PS[0:TP, b, 0:D], dis[0:TP, t:t + 1], T2[0:TP, :],
                                           ALU.mult, ALU.add).then_inc(sem("gnn_x1"), 1)
                    dve.wait_ge(sem("gnn_x1"), nth("gnn_x1", t + 1))
                    stats("gnn", t, T1)
                    V.tensor_copy(mean_all[0:TP, t:t + 1], mv[0:TP, 0:1])
                    V.tensor_copy(rstd_all[0:TP, t:t + 1], small[0:TP, 1:2])
                    V.tensor_scalar(u9[0:TP, :], T1[0:TP, :], mv[0:TP, 0:1], small[0:TP, 1:2], ALU.subtract, ALU.mult)\
                        .then_inc(sem("gnn_u"), 1)
                    rms("gnn", t, u9, nb9[b])
                if t >= 2:
                    weighted("gnn", t - 2, n1w, tv9)
                    if begun(t - 1):
                        dve.wait_ge(sem("gnn_nh"), nth("gnn_nh", t - 1))
                    V.tensor_tensor(LO[:, 0:KT * TP], tv9[:, :], HI[:, 0:KT * TP].bitcast(F32), P_SUB)\
                        .then_inc(sem("gnn_rt"), 1)
            enter(dve, "gnn")
            dve.wait_ge(sem("rope_tables"), nth("rope_tables", 32))
            for r in rounds(dve, 8):
                for b in (0, 1):
                    for c, (off, w) in enumerate(CH_N):
                        q = 3 * b + c
                        g = r * 6 + q
                        cols = slice(512 * (q % 2), 512 * (q % 2) + w)
                        dve.wait_ge(sem("qk_psf"), nth("qk_psf", g + 1))
                        V.tensor_tensor(T2[:, cols], T1[:, cols], cosT[:, off:off + w], ALU.mult).then_inc(sem("qk_c"), 1)
                        dve.wait_ge(sem("qk_rot"), nth("qk_rot", g + 1))
                        V.tensor_tensor(T3[:, cols], T3[:, cols], sinT[:, off:off + w], ALU.mult).then_inc(sem("qk_s"), 1)
                        dve.wait_ge(sem("qk_s"), nth("qk_s", g + 1))
                        V.tensor_tensor(T2[:, cols], T2[:, cols], T3[:, cols], ALU.add).then_inc(sem("qk_val"), 1)
                        dve.wait_ge(sem("qk_val"), nth("qk_val", g + 1))
                        stage_lo("qk", r, 3, q, g, T2, cols, 128)
            enter(dve, "qk")
            dve.wait_ge(sem("v2_bias"), nth("v2_bias", 16))
            plain("v", 10, CH_D, TP, add_rows("v", bias_a))
            enter(dve, "v")

            def row_max(r, j):
                if not due(r, j):
                    return
                n, b = r * NT + j, j % 2
                dve.wait_ge(sem("att_sc"), nth("att_sc", n + 1))
                V.reduce_max(mx[0:TP, b:b + 1], PS[0:TP, b, 0:N], AX.X).then_inc(sem("att_mx"), 1)
                dve.wait_ge(sem("att_mx"), nth("att_mx", n + 1))
                V.tensor_scalar(nmx[0:TP, b:b + 1], mx[0:TP, b:b + 1], -(HD ** -0.5), None, ALU.mult)\
                    .then_inc(sem("att_nm"), 1)

            def lower_part(r, j, g):
                if not due(r, j):
                    return
                pb = j // 2 % 2
                dve.wait_ge(sem("att_hi" + g), nth("att_hi" + g, r * NT + j + 1))
                V.tensor_tensor(pT_part(pb, 1, g, j), group_read(g, j % 2), pT_part(pb, 0, g, j).bitcast(F32), P_SUB)\
                    .then_inc(sem("att_lo" + g), 1)

            def output_sum(r, j):
                if not due(r, j):
                    return
                pair, pb = r * TT + j // 2, j // 2 % 2
                oc = slice(250 * pb, 250 * pb + 250)
                dve.wait_ge(sem("att_oc"), nth("att_oc", pair + 1))
                V.tensor_tensor(o_sum[0:64, oc], PX[0:64, 0, 0:250], o_tmp[0:64, oc], ALU.add)\
                    .then_inc(sem("att_osum"), 1)

            def output_lo(r, j):
                if not due(r, j):
                    return
                pair, pb = r * TT + j // 2, j // 2 % 2
                oc = slice(250 * pb, 250 * pb + 250)
                dve.wait_ge(sem("att_ohi"), nth("att_ohi", pair + 1))
                if begun(32 * (r * (TT // 2) + j // 4)):
                    dve.wait_ge(sem(f"att_st{pb}"), nth(f"att_st{pb}", 32 * (r * (TT // 2) + j // 4)))
                V.tensor_tensor(o_lo[0:64, oc], o_sum[0:64, oc], o_hi[0:64, oc].bitcast(F32), P_SUB)\
                    .then_inc(sem("att_olo"), 1)

            def reciprocal_sum(r, j):
                if not due(r, j):
                    return
                b = j % 2
                dve.wait_ge(sem("att_exp"), nth("att_exp", r * NT + j + 1))
                V.reciprocal(rr[0:TP, b:b + 1], rs[0:TP, b:b + 1]).then_inc(sem("att_rr"), 1)

            def window(r, j):
                row_max(r, j - 1)
                lower_part(r, j - 4, "a")
                lower_part(r, j - 3, "b")
                lower_part(r, j - 2, "c")
                reciprocal_sum(r, j - 1)
                output_lo(r, j - 7)
                lower_part(r, j - 3, "a")
                row_max(r, j)
                lower_part(r, j - 1, "c")
                lower_part(r, j - 2, "b")
                reciprocal_sum(r, j)
                output_sum(r, j - 3)
            windows(dve, window)
            enter(dve, "att")
            resident_raw_lo("op", wo2, 8)
            dve.wait_ge(sem("ob_bias"), nth("ob_bias", 16))
            for t in range(TT + 2):
                if t < TT:
                    b = t % 2
                    if begun(t):
                        dve.wait_ge(sem("op_nb"), nth("op_nb", t))
                    dve.wait_ge(sem(f"op_x1{b}"), nth(f"op_x1{b}", 16 * (t // 2 + 1)))
                    V.tensor_scalar(T1[0:TP, :], x_op[b][0:TP, :], mean_all[0:TP, t:t + 1], rstd_all[0:TP, t:t + 1],
                                    ALU.subtract, ALU.mult).then_inc(sem("op_u"), 1)
                    dve.wait_ge(sem("op_u"), nth("op_u", t + 1))
                    V.tensor_tensor(T1[0:TP, :], T1[0:TP, :], bias_a2[0:TP, :], ALU.add).then_inc(sem("op_ub"), 1)
                    dve.wait_ge(sem("op_ub"), nth("op_ub", t + 1))
                    dve.wait_ge(sem("op_mm"), nth("op_mm", t + 1))
                    V.tensor_tensor(T1[0:TP, :], T1[0:TP, :], PS[0:TP, b, 0:D], ALU.add).then_inc(sem("op_y"), 1)
                    dve.wait_ge(sem("op_y"), nth("op_y", t + 1))
                    V.tensor_tensor(x_op[b][0:TP, :], x_op[b][0:TP, :], T1[0:TP, :], ALU.add).then_inc(sem("op_xy"), 1)
                    rms("op", t, T1, nb13[b])
                if t >= 2:
                    weighted("op", t - 2, n2w, tv13)
                    if begun(t - 1):
                        dve.wait_ge(sem("op_nh"), nth("op_nh", t - 1))
                    tile = slice((t - 2) * TP, (t - 1) * TP)
                    V.tensor_tensor(zT[1][:, :].rearrange("p (k c) -> p k c", k=KT)[:, :, tile],
                                    tv13[:, :].rearrange("p (k c) -> p k c", k=KT),
                                    zT[0][:, :].rearrange("p (k c) -> p k c", k=KT)[:, :, tile].bitcast(F32), P_SUB)\
                        .then_inc(sem("op_rt"), 1)
            enter(dve, "op")
            dve.wait_ge(sem("gate_iota"), nth("gate_iota", 1))
            for t in range(TT):
                dve.wait_ge(sem("gate_tr"), nth("gate_tr", 1))
                if begun(t):
                    dve.wait_ge(sem("gate_e8"), nth("gate_e8", t))
                V.tensor_copy(lg[0:TP, :], PX[0:TP, 0, 8 * t:8 * t + 8]).then_inc(sem("gate_lg"), 1)
                dve.wait_ge(sem("gate_lg"), nth("gate_lg", t + 1))
                V.max(m8[0:TP, :], lg[0:TP, :]).then_inc(sem("gate_c"), 1)
                dve.wait_ge(sem("gate_c"), nth("gate_c", 8 * t + 1))
                V.tensor_scalar(nm1[0:TP, 0:1], m8[0:TP, 0:1], -1.0, None, ALU.mult).then_inc(sem("gate_top"), 1)
                V.max_index(top_i[0:TP, :], m8[0:TP, :], lg[0:TP, :]).then_inc(sem("gate_c"), 1)
                dve.wait_ge(sem("gate_c"), nth("gate_c", 8 * t + 2))
                V.tensor_copy(top_f[0:TP, :], top_i[0:TP, :]).then_inc(sem("gate_c"), 1)
                if begun(8 * t + 3):
                    dve.wait_ge(sem("gate_c"), nth("gate_c", 8 * t + 3))
                V.tensor_scalar(mask[0:TP, :], eight[0:TP, :], top_f[0:TP, 0:1], None, ALU.is_equal).then_inc(sem("gate_c"), 1)
                if begun(8 * t + 4):
                    dve.wait_ge(sem("gate_c"), nth("gate_c", 8 * t + 4))
                V.scalar_tensor_tensor(mask[0:TP, :], eight[0:TP, :], top_f[0:TP, 1:2], mask[0:TP, :],
                                       ALU.is_equal, ALU.add).then_inc(sem("gate_c"), 1)
                if begun(8 * t + 5):
                    dve.wait_ge(sem("gate_c"), nth("gate_c", 8 * t + 5))
                dve.wait_ge(sem("gate_e8"), nth("gate_e8", t + 1))
                V.tensor_tensor(comb[0:TP, t, :], ex8[0:TP, :], mask[0:TP, :], ALU.mult).then_inc(sem("gate_c"), 1)
                if begun(8 * t + 6):
                    dve.wait_ge(sem("gate_c"), nth("gate_c", 8 * t + 6))
                V.reduce_sum(small[0:TP, 0:1], comb[0:TP, t, :], AX.X).then_inc(sem("gate_c"), 1)
                if begun(8 * t + 7):
                    dve.wait_ge(sem("gate_c"), nth("gate_c", 8 * t + 7))
                V.reciprocal(small[0:TP, 1:2], small[0:TP, 0:1]).then_inc(sem("gate_c"), 1)
                if begun(8 * t + 8):
                    dve.wait_ge(sem("gate_c"), nth("gate_c", 8 * t + 8))
                V.tensor_scalar(comb[0:TP, t, :], comb[0:TP, t, :], small[0:TP, 1:2], None, ALU.mult).then_inc(sem("gate_comb"), 1)
            for r in rounds(dve, EXPERTS):
                for j in range(2):
                    for c, (off, w) in enumerate(CH_N):
                        q = 3 * j + c
                        g = r * 6 + q
                        cols = slice(512 * (q % 2), 512 * (q % 2) + w)
                        if c == 0:
                            dve.wait_ge(sem("ex_mm"), nth("ex_mm", 4 * r + 2 * j + 2))
                        dve.wait_ge(sem("ex_a"), nth("ex_a", g + 1))
                        V.scalar_tensor_tensor(T2[:, cols], PS[:, 1, off:off + w], b2[:, bass.ds(2 * r + j, 1)],
                                               silu[j][:, off:off + w],
                                               ALU.add, ALU.mult).then_inc(sem("ex_b"), 1)
                        dve.wait_ge(sem("ex_b"), nth("ex_b", g + 1))
                        if q == 0:
                            if isinstance(r, int):
                                dve.wait_ge(sem("comb_first"), nth("comb_first", 16))
                            else:
                                if begun(16 * (EXPERTS - 1)):
                                    dve.wait_ge(sem("comb_in"), nth("comb_in", 16 * (EXPERTS - 1)))
                        V.tensor_tensor(T2[:, cols], T2[:, cols], combB[:, r, off:off + w], ALU.mult)\
                            .then_inc(sem("ex_val"), 1)
                        dve.wait_ge(sem("ex_val"), nth("ex_val", g + 1))
                        stage_lo("ex", r, 3, q, g, T2, cols, 128)
            enter(dve, "ex")
            resident_raw_lo("w3", w3, 16)
            for r in rounds(dve, TT // 2):
                for b in (0, 1):
                    dve.wait_ge(sem("w3_mm"), nth("w3_mm", 2 * r + b + 1))
                    for c in (0, 1):
                        cols = slice(512 * c, 512 * c + 512)
                        dve.wait_ge(sem(f"w3_in{c}"), nth(f"w3_in{c}", 32 * r + 16 * b + 16))
                        if begun(32 * r + 16 * b):
                            dve.wait_ge(sem(f"w3_st{c}"), nth(f"w3_st{c}", 32 * r + 16 * b))
                        V.tensor_tensor(T1[0:TP, cols], T2[0:TP, cols], PS[0:TP, b, cols], ALU.add).then_inc(sem("w3_v"), 1)




def _shape_constants():
    inv = (1.0 / 10000.0 ** (np.arange(0, HD, 2, dtype=np.float32) / HD)).astype(np.float32)
    angle = inv[np.arange(128) % 32][:, None] * np.arange(N, dtype=np.float32)[None, :]
    sign = np.where(np.arange(128) % HD < 32, -1.0, 1.0)[:, None]
    below = np.triu(np.ones((128, 128), np.float32), 1)
    return {"below": below, "cos": np.cos(angle).astype(np.float32), "sin": (sign * np.sin(angle)).astype(np.float32),
            "ident": np.eye(128, dtype=np.float32)}


def kernel(x, src, dst, L0_gnn_W, L0_gnn_b, L0_mix_Wq, L0_mix_bq, L0_mix_Wk, L0_mix_bk, L0_mix_Wv, L0_mix_bv,
           L0_mix_Wo, L0_mix_bo, L0_ffn_norm1_w, L0_ffn_norm2_w, L0_ffn_qkv_w, L0_ffn_qkv_b, L0_ffn_out_w,
           L0_ffn_out_b, L0_ffn_gate_w, L0_ffn_w1, L0_ffn_b1, L0_ffn_w2, L0_ffn_b2, L0_ffn_w3, L0_ffn_b3):
    import concourse.bacc as _bacc
    from concourse.bass_utils import run_bass_kernel_spmd as _run

    def slabs(w):
        w = np.asarray(w)
        return w.reshape(-1, 128, KT, 128).transpose(0, 3, 2, 1)

    def cols(v):
        return np.asarray(v).reshape(-1, 128).T

    w12 = np.stack([np.asarray(L0_ffn_w1), np.asarray(L0_ffn_w2)], axis=1)
    w12 = w12.reshape(EXPERTS, 2, 2, 128, KT, 128).transpose(0, 2, 1, 5, 4, 3).reshape(4 * EXPERTS, 128, KT, 128)
    gate = np.tile(np.asarray(L0_ffn_gate_w).T, (1, 128 // EXPERTS))
    qkv_w, qkv_b = np.asarray(L0_ffn_qkv_w), np.asarray(L0_ffn_qkv_b)
    arrays = {
        "x": x, "src": src, "dst": dst,
        "Wq": slabs(L0_mix_Wq), "Wk": np.asarray(L0_mix_Wk).T, "Wg": np.asarray(L0_gnn_W).T, "Wv": slabs(L0_mix_Wv),
        "Wo": np.asarray(L0_mix_Wo).T, "Wqk": slabs(qkv_w[:2 * D]), "Wv2": qkv_w[2 * D:].T,
        "Wo2": np.asarray(L0_ffn_out_w).T, "gate": gate.reshape(KT, 128, 128).transpose(1, 0, 2), "W12": w12,
        "W3": np.asarray(L0_ffn_w3).transpose(0, 2, 1).reshape(EXPERTS * HID, D),
        "bq": cols(L0_mix_bq), "bv": cols(L0_mix_bv), "bqk": cols(qkv_b[:2 * D]), "b1": cols(np.asarray(L0_ffn_b1).ravel()),
        "b2": cols(np.asarray(L0_ffn_b2).ravel()), "n1": cols(L0_ffn_norm1_w), "n2": cols(L0_ffn_norm2_w),
        "bk": L0_mix_bk, "bg": L0_gnn_b, "bo": L0_mix_bo, "bv2": qkv_b[2 * D:], "ob": L0_ffn_out_b, "b3": L0_ffn_b3,
        **_shape_constants(),
    }
    nc = _bacc.Bacc("TRN2", target_bir_lowering=False, num_devices=1)
    io, feed = {}, {}
    for name, a in arrays.items():
        a = np.ascontiguousarray(a)
        feed["in_" + name] = a
        io[name] = nc.dram_tensor("in_" + name, a.shape, mybir.dt.from_np(a.dtype), kind="ExternalInput").ap()
    io["out"] = nc.dram_tensor("out_rows", (N, D), F32, kind="ExternalOutput").ap()
    build(nc, io)
    return _run(nc, [feed], core_ids=[0]).results[0]["out_rows"]
```
